# Optimizing a Trainium2 kernel written in Bass

```python
import numpy as np
import jax
import jax.numpy as jnp

def _softmax(x, axis=-1):
    return jax.nn.softmax(x, axis=axis)

def _gelu(x):
    return jax.nn.gelu(x, approximate=True)

def _silu(x):
    return jax.nn.silu(x)

def _sigmoid(x):
    return jax.nn.sigmoid(x)

def _layernorm(x, axis=-1, eps=1e-05):
    m = jnp.mean(x, axis=axis, keepdims=True)
    v = jnp.var(x, axis=axis, keepdims=True)
    return (x - m) / jnp.sqrt(v + eps)

def _scatter_add(tgt, idx, src, axis=0):
    return tgt.at[idx].add(src)

def _segment_sum(src, seg, n):
    return jax.ops.segment_sum(src, seg, n)
kernel_name = 'mk_flamingo_gated_d2_seqx_r8_1e4a97'

def setup_inputs(seed: int=0):
    np.random.seed(seed)
    _w = jnp.asarray

    def _rec_inputs():
        import jax
        import jax.numpy as jnp
        _rk = jax.random.key(seed)
        x = 7.22e-05 + 1 * jax.random.normal(jax.random.fold_in(_rk, 1), (16, 256, 128), jnp.float32)
        _lenS = 256 - jax.random.randint(jax.random.fold_in(_rk, 7), (16,), 0, max(1, 256 // 4) + 1, jnp.int32)
        _lenS2 = 64 - jax.random.randint(jax.random.fold_in(_rk, 8), (16,), 0, max(1, 64 // 4) + 1, jnp.int32)
        _ctx_1024P = jax.random.normal(jax.random.fold_in(_rk, 11), (16, 16, 128), jnp.float32)
        _ctx_1024c = jax.random.dirichlet(jax.random.fold_in(_rk, 511), 0.3 * jnp.ones((16,), jnp.float32), (16, 64))
        _ctx_1024t = jnp.einsum('bsk,bkd->bsd', _ctx_1024c, _ctx_1024P)
        _ctx_1024t = _ctx_1024t * jax.lax.rsqrt(jnp.mean(jnp.square(_ctx_1024t)) + 1e-12) * 0.953939
        ctx_1024 = 4.13588e-05 + 0.999923 * (_ctx_1024t + 0.3 * jax.random.normal(jax.random.fold_in(_rk, 611), (16, 64, 128), jnp.float32))
        _validS = jnp.arange(256)[None, :] < _lenS[:, None]
        _validS2 = jnp.arange(64)[None, :] < _lenS2[:, None]
        _causal = jnp.tril(jnp.ones((256, 256), dtype=bool))
        mask_BxS2_if1 = jnp.where(jnp.ones((16, 64), dtype=bool), 1, 0).astype(jnp.int32)
        mask_BxS2_ik0 = jnp.where(jnp.broadcast_to(_validS2[:, :], (16, 64)), 0, 1).astype(jnp.int32)
        _g = jax.random.normal(jax.random.fold_in(_rk, 9001), (2, 2), jnp.float32)
        _g = jnp.sign(_g) * jnp.maximum(jnp.abs(_g), 1.0) + (_g == 0) * 1.0
        g_xattn = _g[0]
        g_ffn = _g[1]
        return (x, ctx_1024, mask_BxS2_if1, mask_BxS2_ik0, g_xattn, g_ffn)
    x, ctx_1024, mask_BxS2_if1, mask_BxS2_ik0, g_xattn, g_ffn = _rec_inputs()

    def _L0_xattn_setup():
        import jax, jax.numpy as jnp
        import numpy as np
        B, S, D, H = (4, 256, 128, 16)
        DK = D // H
        key = jax.random.key(seed)
        ks = jax.random.split(key, 7)
        xq = jax.random.normal(ks[0], (B, S, D), dtype=jnp.float32)
        xk = jax.random.normal(ks[1], (B, S, D), dtype=jnp.float32)
        xv = jax.random.normal(ks[2], (B, S, D), dtype=jnp.float32)
        attention_mask = jnp.ones((B, S), dtype=jnp.int32)
        scale = 0.02
        Wq = jax.random.normal(ks[3], (D, D), dtype=jnp.float32) * scale
        Wk = jax.random.normal(ks[4], (D, D), dtype=jnp.float32) * scale
        Wv = jax.random.normal(ks[5], (D, D), dtype=jnp.float32) * scale
        Wo = jax.random.normal(ks[6], (D, D), dtype=jnp.float32) * scale
        return {'x_query': xq, 'x_key': xk, 'x_value': xv, 'attention_mask': attention_mask, 'Wq': Wq, 'Wk': Wk, 'Wv': Wv, 'Wo': Wo}
    _L0_xattn_all = _L0_xattn_setup()
    _L0_xattn_in = {k: v for k, v in _L0_xattn_all.items() if k in ('Wq', 'Wk', 'Wv', 'Wo')}
    del _L0_xattn_all

    def _L0_ffn_setup():
        import jax, jax.numpy as jnp
        import numpy as np
        DIM = 128
        DEPTH = 2
        HEADS = 8
        DIM_HEAD = 64
        WINDOW = 64
        INNER = HEADS * DIM_HEAD
        HID = int(DIM * 4 * 2 / 3)
        B, N = (2, 1024)
        QK_SCALE = 8.0

        def shift_token(t):
            t1, t2 = jnp.split(t, 2, axis=-1)
            t2 = jnp.pad(t2, ((0, 0), (1, 0), (0, 0)))[:, :-1]
            return jnp.concatenate([t1, t2], axis=-1)

        def l2norm(t):
            return t / jnp.clip(jnp.linalg.norm(t, axis=-1, keepdims=True), 1e-12)

        def rotate_half(x):
            x1, x2 = jnp.split(x, 2, axis=-1)
            return jnp.concatenate([-x2, x1], axis=-1)

        def rotary_xpos(q, k):
            n = q.shape[-2]
            half_idx = jnp.arange(0, DIM_HEAD, 2, dtype=jnp.float32)
            inv_freq = 1.0 / 10000.0 ** (half_idx / DIM_HEAD)
            t = jnp.arange(n, dtype=jnp.float32)
            freqs = t[:, None] * inv_freq[None, :]
            freqs = jnp.concatenate([freqs, freqs], axis=-1)
            base = (half_idx + 0.4 * DIM_HEAD) / (1.4 * DIM_HEAD)
            power = (t - n // 2) / float(WINDOW // 2)
            scale = base[None, :] ** power[:, None]
            scale = jnp.concatenate([scale, scale], axis=-1)
            cos, sin = (jnp.cos(freqs), jnp.sin(freqs))
            q = q * cos * scale + rotate_half(q) * sin * scale
            k = k * cos / scale + rotate_half(k) * sin / scale
            return (q, k)

        def local_attention(q, k, v):
            b, h, n, d = q.shape
            w = n // WINDOW
            bq = q.reshape(b, h, w, WINDOW, d) * QK_SCALE
            bk = k.reshape(b, h, w, WINDOW, d)
            bv = v.reshape(b, h, w, WINDOW, d)

            def look_around(t):
                p = jnp.pad(t, ((0, 0), (0, 0), (1, 0), (0, 0), (0, 0)))
                return jnp.concatenate([p[:, :, :w], p[:, :, 1:]], axis=3)
            bk, bv = (look_around(bk), look_around(bv))
            bt = jnp.arange(n).reshape(w, WINDOW)
            btp = jnp.pad(bt, ((1, 0), (0, 0)), constant_values=-1)
            btk = jnp.concatenate([btp[:w], btp[1:]], axis=1)
            sim = jnp.einsum('bhwid,bhwjd->bhwij', bq, bk)
            i = bt[:, :, None]
            j = btk[:, None, :]
            mask = (i < j) | (i > j + WINDOW) | (j == -1)
            sim = jnp.where(mask, -jnp.finfo(sim.dtype).max, sim)
            attn = jax.nn.softmax(sim, axis=-1)
            out = jnp.einsum('bhwij,bhwjd->bhwid', attn, bv)
            return out.reshape(b, h, n, d)

        def _layer(x, wqkv, qs, ksc, wo, lg, lb, w1, b1, w2, b2):
            b, n, _ = x.shape
            h = shift_token(x)
            qkv = h @ wqkv
            q, k, v = jnp.split(qkv, 3, axis=-1)
            to_heads = lambda t: t.reshape(b, n, HEADS, DIM_HEAD).transpose(0, 2, 1, 3)
            q, k, v = (to_heads(q), to_heads(k), to_heads(v))
            q = l2norm(q) * qs
            k = l2norm(k) * ksc
            q, k = rotary_xpos(q, k)
            o = local_attention(q, k, v)
            o = o.transpose(0, 2, 1, 3).reshape(b, n, INNER)
            x = x + o @ wo
            h = shift_token(x)
            mu = h.mean(-1, keepdims=True)
            var = h.var(-1, keepdims=True)
            h = (h - mu) / jnp.sqrt(var + 1e-05) * lg + lb
            h = h @ w1 + b1
            a, g = jnp.split(h, 2, axis=-1)
            h = a * jax.nn.gelu(g, approximate=False)
            x = x + h @ w2 + b2
            return x
        key = jax.random.key(seed)
        ks = jax.random.split(key, 6)
        return {'x': jax.random.normal(ks[0], (B, N, DIM), jnp.float32), 'wqkv': jax.random.normal(ks[1], (DEPTH, DIM, 3 * INNER), jnp.float32) * 0.02, 'q_scale': jnp.ones((DEPTH, DIM_HEAD), jnp.float32), 'k_scale': jnp.ones((DEPTH, DIM_HEAD), jnp.float32), 'wo': jax.random.normal(ks[2], (DEPTH, INNER, DIM), jnp.float32) * 0.02, 'ln_g': jnp.ones((DEPTH, DIM), jnp.float32), 'ln_b': jnp.zeros((DEPTH, DIM), jnp.float32), 'w1': jax.random.normal(ks[3], (DEPTH, DIM, 2 * HID), jnp.float32) * 0.02, 'b1': jnp.zeros((DEPTH, 2 * HID), jnp.float32), 'w2': jax.random.normal(ks[4], (DEPTH, HID, DIM), jnp.float32) * 0.02, 'b2': jnp.zeros((DEPTH, DIM), jnp.float32)}
    _L0_ffn_all = _L0_ffn_setup()
    _L0_ffn_in = {k: v for k, v in _L0_ffn_all.items() if k in ('wqkv', 'q_scale', 'k_scale', 'wo', 'ln_g', 'ln_b', 'w1', 'b1', 'w2', 'b2')}
    del _L0_ffn_all

    def _L1_xattn_setup():
        import jax, jax.numpy as jnp
        import numpy as np
        HID_DIM = 128
        N_HEADS = 16
        HEAD_DIM = HID_DIM // N_HEADS

        def _split_heads(x, B):
            return x.reshape(B, -1, N_HEADS, HEAD_DIM).transpose(0, 2, 1, 3)
        key = jax.random.key(seed)
        ks = jax.random.split(key, 12)
        B, S, D = (4, 256, HID_DIM)
        sc = 1.0 / np.sqrt(D)
        inp = {'query': jax.random.normal(ks[0], (B, S, D), jnp.float32), 'key': jax.random.normal(ks[1], (B, S, D), jnp.float32), 'value': jax.random.normal(ks[2], (B, S, D), jnp.float32), 'mask': jax.random.randint(ks[3], (B, S), 0, 2, jnp.int32), 'Wq': jax.random.normal(ks[4], (D, D), jnp.float32) * sc, 'bq': jnp.zeros((D,), jnp.float32), 'Wk': jax.random.normal(ks[5], (D, D), jnp.float32) * sc, 'bk': jnp.zeros((D,), jnp.float32), 'Wv': jax.random.normal(ks[6], (D, D), jnp.float32) * sc, 'bv': jnp.zeros((D,), jnp.float32), 'Wfc': jax.random.normal(ks[7], (D, D), jnp.float32) * sc, 'bfc': jnp.zeros((D,), jnp.float32)}
        return inp
    _L1_xattn_all = _L1_xattn_setup()
    _L1_xattn_in = {k: v for k, v in _L1_xattn_all.items() if k in ('Wq', 'bq', 'Wk', 'bk', 'Wv', 'bv', 'Wfc', 'bfc')}
    del _L1_xattn_all

    def _L1_ffn_setup():
        import jax, jax.numpy as jnp
        import numpy as np
        N_EMBD = 128
        EXPERT_SIZES = [(4, 128), (4, 256)]
        TOP_K = 2
        B, S = (1, 256)
        WIDTHS = []
        for count, size in EXPERT_SIZES:
            WIDTHS += [size] * count
        OFFSETS = np.concatenate([[0], np.cumsum(WIDTHS)]).astype(np.int64)
        E = len(WIDTHS)
        TOTAL_W = int(OFFSETS[-1])
        MAX_W = max(WIDTHS)

        def _stack_experts(w1, w2):
            W1e, W2e = ([], [])
            for e in range(E):
                off, wd = (int(OFFSETS[e]), WIDTHS[e])
                pad = MAX_W - wd
                W1e.append(jnp.pad(w1[:, off:off + wd], ((0, 0), (0, pad))))
                W2e.append(jnp.pad(w2[off:off + wd, :], ((0, pad), (0, 0))))
            return (jnp.stack(W1e), jnp.stack(W2e))
        key = jax.random.key(seed)
        k1, k2, k3, k4 = jax.random.split(key, 4)
        x = jax.random.normal(k1, (B, S, N_EMBD), jnp.float32)
        router_w = jax.random.normal(k2, (E, N_EMBD), jnp.float32) * 0.02
        w1 = jax.random.truncated_normal(k3, -3.0, 3.0, (N_EMBD, TOTAL_W), jnp.float32) * 0.02
        w2 = jax.random.truncated_normal(k4, -3.0, 3.0, (TOTAL_W, N_EMBD), jnp.float32) * 0.02
        return {'x': x, 'router_w': router_w, 'w1': w1, 'w2': w2}
    _L1_ffn_all = _L1_ffn_setup()
    _L1_ffn_in = {k: v for k, v in _L1_ffn_all.items() if k in ('router_w', 'w1', 'w2')}
    del _L1_ffn_all
    return {'x': x, 'ctx_1024': ctx_1024, 'mask_BxS2_if1': mask_BxS2_if1, 'mask_BxS2_ik0': mask_BxS2_ik0, 'g_xattn': g_xattn, 'g_ffn': g_ffn, 'L0_xattn_Wq': _L0_xattn_in['Wq'], 'L0_xattn_Wk': _L0_xattn_in['Wk'], 'L0_xattn_Wv': _L0_xattn_in['Wv'], 'L0_xattn_Wo': _L0_xattn_in['Wo'], 'L0_ffn_wqkv': _L0_ffn_in['wqkv'], 'L0_ffn_q_scale': _L0_ffn_in['q_scale'], 'L0_ffn_k_scale': _L0_ffn_in['k_scale'], 'L0_ffn_wo': _L0_ffn_in['wo'], 'L0_ffn_ln_g': _L0_ffn_in['ln_g'], 'L0_ffn_ln_b': _L0_ffn_in['ln_b'], 'L0_ffn_w1': _L0_ffn_in['w1'], 'L0_ffn_b1': _L0_ffn_in['b1'], 'L0_ffn_w2': _L0_ffn_in['w2'], 'L0_ffn_b2': _L0_ffn_in['b2'], 'L1_xattn_Wq': _L1_xattn_in['Wq'], 'L1_xattn_bq': _L1_xattn_in['bq'], 'L1_xattn_Wk': _L1_xattn_in['Wk'], 'L1_xattn_bk': _L1_xattn_in['bk'], 'L1_xattn_Wv': _L1_xattn_in['Wv'], 'L1_xattn_bv': _L1_xattn_in['bv'], 'L1_xattn_Wfc': _L1_xattn_in['Wfc'], 'L1_xattn_bfc': _L1_xattn_in['bfc'], 'L1_ffn_router_w': _L1_ffn_in['router_w'], 'L1_ffn_w1': _L1_ffn_in['w1'], 'L1_ffn_w2': _L1_ffn_in['w2']}

def reference(x, ctx_1024, mask_BxS2_if1, mask_BxS2_ik0, g_xattn, g_ffn, L0_xattn_Wq, L0_xattn_Wk, L0_xattn_Wv, L0_xattn_Wo, L0_ffn_wqkv, L0_ffn_q_scale, L0_ffn_k_scale, L0_ffn_wo, L0_ffn_ln_g, L0_ffn_ln_b, L0_ffn_w1, L0_ffn_b1, L0_ffn_w2, L0_ffn_b2, L1_xattn_Wq, L1_xattn_bq, L1_xattn_Wk, L1_xattn_bk, L1_xattn_Wv, L1_xattn_bv, L1_xattn_Wfc, L1_xattn_bfc, L1_ffn_router_w, L1_ffn_w1, L1_ffn_w2):
    import jax
    import jax.numpy as jnp

    def _L0_xattn_ref(x_query, x_key, x_value, attention_mask, Wq, Wk, Wv, Wo):
        import jax, jax.numpy as jnp
        import numpy as np
        B, S, D, H = (4, 256, 128, 16)
        DK = D // H
        b, sq, d = x_query.shape
        sk = x_key.shape[1]
        Q = x_query @ Wq.T
        K = x_key @ Wk.T
        V = x_value @ Wv.T
        Qh = Q.reshape(b, sq, H, DK).transpose(0, 2, 1, 3)
        Kh = K.reshape(b, sk, H, DK).transpose(0, 2, 1, 3)
        Vh = V.reshape(b, sk, H, DK).transpose(0, 2, 1, 3)
        scores = jnp.einsum('bhqd,bhkd->bhqk', Qh, Kh) / jnp.sqrt(jnp.asarray(DK, dtype=Qh.dtype))
        causal = jnp.tril(jnp.ones((sq, sk), dtype=bool))
        scores = jnp.where(causal[None, None, :, :], scores, -jnp.inf)
        pad = (attention_mask != 0)[:, None, None, :]
        scores = jnp.where(pad, scores, -jnp.inf)
        attn = jax.nn.softmax(scores, axis=-1)
        out = jnp.einsum('bhqk,bhkd->bhqd', attn, Vh)
        out = out.transpose(0, 2, 1, 3).reshape(b, sq, d)
        return out @ Wo.T

    def _L0_ffn_ref(x, wqkv, q_scale, k_scale, wo, ln_g, ln_b, w1, b1, w2, b2):
        import jax, jax.numpy as jnp
        import numpy as np
        DIM = 128
        DEPTH = 2
        HEADS = 8
        DIM_HEAD = 64
        WINDOW = 64
        INNER = HEADS * DIM_HEAD
        HID = int(DIM * 4 * 2 / 3)
        B, N = (2, 1024)
        QK_SCALE = 8.0

        def shift_token(t):
            t1, t2 = jnp.split(t, 2, axis=-1)
            t2 = jnp.pad(t2, ((0, 0), (1, 0), (0, 0)))[:, :-1]
            return jnp.concatenate([t1, t2], axis=-1)

        def l2norm(t):
            return t / jnp.clip(jnp.linalg.norm(t, axis=-1, keepdims=True), 1e-12)

        def rotate_half(x):
            x1, x2 = jnp.split(x, 2, axis=-1)
            return jnp.concatenate([-x2, x1], axis=-1)

        def rotary_xpos(q, k):
            n = q.shape[-2]
            half_idx = jnp.arange(0, DIM_HEAD, 2, dtype=jnp.float32)
            inv_freq = 1.0 / 10000.0 ** (half_idx / DIM_HEAD)
            t = jnp.arange(n, dtype=jnp.float32)
            freqs = t[:, None] * inv_freq[None, :]
            freqs = jnp.concatenate([freqs, freqs], axis=-1)
            base = (half_idx + 0.4 * DIM_HEAD) / (1.4 * DIM_HEAD)
            power = (t - n // 2) / float(WINDOW // 2)
            scale = base[None, :] ** power[:, None]
            scale = jnp.concatenate([scale, scale], axis=-1)
            cos, sin = (jnp.cos(freqs), jnp.sin(freqs))
            q = q * cos * scale + rotate_half(q) * sin * scale
            k = k * cos / scale + rotate_half(k) * sin / scale
            return (q, k)

        def local_attention(q, k, v):
            b, h, n, d = q.shape
            w = n // WINDOW
            bq = q.reshape(b, h, w, WINDOW, d) * QK_SCALE
            bk = k.reshape(b, h, w, WINDOW, d)
            bv = v.reshape(b, h, w, WINDOW, d)

            def look_around(t):
                p = jnp.pad(t, ((0, 0), (0, 0), (1, 0), (0, 0), (0, 0)))
                return jnp.concatenate([p[:, :, :w], p[:, :, 1:]], axis=3)
            bk, bv = (look_around(bk), look_around(bv))
            bt = jnp.arange(n).reshape(w, WINDOW)
            btp = jnp.pad(bt, ((1, 0), (0, 0)), constant_values=-1)
            btk = jnp.concatenate([btp[:w], btp[1:]], axis=1)
            sim = jnp.einsum('bhwid,bhwjd->bhwij', bq, bk)
            i = bt[:, :, None]
            j = btk[:, None, :]
            mask = (i < j) | (i > j + WINDOW) | (j == -1)
            sim = jnp.where(mask, -jnp.finfo(sim.dtype).max, sim)
            attn = jax.nn.softmax(sim, axis=-1)
            out = jnp.einsum('bhwij,bhwjd->bhwid', attn, bv)
            return out.reshape(b, h, n, d)

        def _layer(x, wqkv, qs, ksc, wo, lg, lb, w1, b1, w2, b2):
            b, n, _ = x.shape
            h = shift_token(x)
            qkv = h @ wqkv
            q, k, v = jnp.split(qkv, 3, axis=-1)
            to_heads = lambda t: t.reshape(b, n, HEADS, DIM_HEAD).transpose(0, 2, 1, 3)
            q, k, v = (to_heads(q), to_heads(k), to_heads(v))
            q = l2norm(q) * qs
            k = l2norm(k) * ksc
            q, k = rotary_xpos(q, k)
            o = local_attention(q, k, v)
            o = o.transpose(0, 2, 1, 3).reshape(b, n, INNER)
            x = x + o @ wo
            h = shift_token(x)
            mu = h.mean(-1, keepdims=True)
            var = h.var(-1, keepdims=True)
            h = (h - mu) / jnp.sqrt(var + 1e-05) * lg + lb
            h = h @ w1 + b1
            a, g = jnp.split(h, 2, axis=-1)
            h = a * jax.nn.gelu(g, approximate=False)
            x = x + h @ w2 + b2
            return x
        for l in range(DEPTH):
            x = _layer(x, wqkv[l], q_scale[l], k_scale[l], wo[l], ln_g[l], ln_b[l], w1[l], b1[l], w2[l], b2[l])
        return x

    def _L1_xattn_ref(query, key, value, mask, Wq, bq, Wk, bk, Wv, bv, Wfc, bfc):
        import jax, jax.numpy as jnp
        import numpy as np
        HID_DIM = 128
        N_HEADS = 16
        HEAD_DIM = HID_DIM // N_HEADS

        def _split_heads(x, B):
            return x.reshape(B, -1, N_HEADS, HEAD_DIM).transpose(0, 2, 1, 3)
        B = query.shape[0]
        Q = _split_heads(query @ Wq.T + bq, B)
        K = _split_heads(key @ Wk.T + bk, B)
        V = _split_heads(value @ Wv.T + bv, B)
        scale = jnp.sqrt(jnp.float32(HEAD_DIM))
        energy = jnp.einsum('bhqd,bhkd->bhqk', Q, K) / scale
        energy = jnp.where(mask[:, None, None, :] == 0, jnp.float32(-10000000000.0), energy)
        attention = jax.nn.softmax(energy, axis=-1)
        x = jnp.einsum('bhqk,bhkd->bhqd', attention, V)
        x = x.transpose(0, 2, 1, 3).reshape(B, -1, HID_DIM)
        return x @ Wfc.T + bfc

    def _L1_ffn_ref(x, router_w, w1, w2):
        import jax, jax.numpy as jnp
        import numpy as np
        N_EMBD = 128
        EXPERT_SIZES = [(4, 128), (4, 256)]
        TOP_K = 2
        B, S = (1, 256)
        WIDTHS = []
        for count, size in EXPERT_SIZES:
            WIDTHS += [size] * count
        OFFSETS = np.concatenate([[0], np.cumsum(WIDTHS)]).astype(np.int64)
        E = len(WIDTHS)
        TOTAL_W = int(OFFSETS[-1])
        MAX_W = max(WIDTHS)

        def _stack_experts(w1, w2):
            W1e, W2e = ([], [])
            for e in range(E):
                off, wd = (int(OFFSETS[e]), WIDTHS[e])
                pad = MAX_W - wd
                W1e.append(jnp.pad(w1[:, off:off + wd], ((0, 0), (0, pad))))
                W2e.append(jnp.pad(w2[off:off + wd, :], ((0, pad), (0, 0))))
            return (jnp.stack(W1e), jnp.stack(W2e))
        b, s, d = x.shape
        xf = x.reshape(-1, d)
        logits = xf @ router_w.T
        probs = jax.nn.sigmoid(logits.astype(jnp.float32))
        topw, sel = jax.lax.top_k(probs, TOP_K)
        topw = topw / (topw.sum(-1, keepdims=True) + 1e-20)
        topw = topw.astype(x.dtype)
        onehot = sel[:, :, None] == jnp.arange(E)[None, None, :]
        combine = jnp.sum(topw[:, :, None] * onehot, axis=1)
        W1e, W2e = _stack_experts(w1, w2)
        h = jnp.einsum('td,edw->tew', xf, W1e)
        h = jnp.square(jax.nn.relu(h))
        y = jnp.einsum('tew,ewd->ted', h, W2e)
        out = jnp.einsum('ted,te->td', y, combine)
        return out.reshape(b, s, d)
    x = x + jnp.tanh(g_xattn[0]) * _L0_xattn_ref(_layernorm(x, axis=-1), ctx_1024, ctx_1024, mask_BxS2_if1, L0_xattn_Wq, L0_xattn_Wk, L0_xattn_Wv, L0_xattn_Wo)
    x = x + jnp.tanh(g_ffn[0]) * _L0_ffn_ref(_layernorm(x, axis=-1), L0_ffn_wqkv, L0_ffn_q_scale, L0_ffn_k_scale, L0_ffn_wo, L0_ffn_ln_g, L0_ffn_ln_b, L0_ffn_w1, L0_ffn_b1, L0_ffn_w2, L0_ffn_b2)
    x = x + jnp.tanh(g_xattn[1]) * _L1_xattn_ref(_layernorm(x, axis=-1), ctx_1024, ctx_1024, mask_BxS2_ik0, L1_xattn_Wq, L1_xattn_bq, L1_xattn_Wk, L1_xattn_bk, L1_xattn_Wv, L1_xattn_bv, L1_xattn_Wfc, L1_xattn_bfc)
    x = x + jnp.tanh(g_ffn[1]) * _L1_ffn_ref(_layernorm(x, axis=-1), L1_ffn_router_w, L1_ffn_w1, L1_ffn_w2)
    return x

_drawn_inputs = setup_inputs


def setup_inputs(seed=0):
    import zlib

    import numpy as np

    out = dict(_drawn_inputs(seed))
    spreads = {'g_ffn': (-1.0, 0.6),
     'L0_ffn_q_scale': (1.0, 0.6),
     'L0_ffn_k_scale': (1.0, 0.6),
     'L0_ffn_ln_g': (1.0, 0.6),
     'L0_ffn_ln_b': (0.0, 0.8),
     'L0_ffn_b1': (0.0, 0.47),
     'L0_ffn_b2': (0.0, 0.1),
     'L1_xattn_bq': (0.0, 0.1),
     'L1_xattn_bk': (0.0, 0.8),
     'L1_xattn_bv': (0.0, 0.1),
     'L1_xattn_bfc': (0.0, 0.1)}
    factors = {'L0_xattn_Wq': 8.0,
     'L0_xattn_Wk': 8.0,
     'L0_xattn_Wv': 4.723,
     'L0_xattn_Wo': 4.83,
     'L1_ffn_router_w': 4.691,
     'L1_ffn_w1': 4.252,
     'L1_ffn_w2': 3.959}
    for name, (base, spread) in spreads.items():
        noise = np.random.default_rng([zlib.crc32(name.encode()), seed]).standard_normal(out[name].shape)
        drawn = base * np.exp(spread * noise) if base else spread * noise
        out[name] = jnp.asarray(drawn.astype(out[name].dtype))
    for name, factor in factors.items():
        out[name] = (out[name] * factor).astype(out[name].dtype)
    return out
```

```python
from contextlib import ExitStack

import numpy as np

import concourse.bass as bass
from concourse import mybir

F32 = mybir.dt.float32
BF16 = mybir.dt.bfloat16
I32 = mybir.dt.int32
U32 = mybir.dt.uint32
ALU = mybir.AluOpType
ACT = mybir.ActivationFunctionType
AX_X = mybir.AxisListType.X

P = 128
D = 128
B, S, SC = 16, 256, 64
T = B * S // P
UPS = S // P
XH, XD = 16, 8
XP = XH // 2
LH, LD, WIN = 8, 64, 64
LP = LH // 2
INNER = LH * LD
QK_SCALE = 8
HID = 341
HCH = [128, 128, 85]
EW = [128] * 4 + [256] * 4
E = len(EW)
CH = sum(EW) // P
UNROLL = 4
AWAY = -2.0e38
PADDED = -1.0e38


def position_tables():
    f = np.float32
    half = np.arange(0, LD, 2, dtype=f)
    inv = f(1.0) / np.power(f(10000.0), half / f(LD))
    t = np.arange(S, dtype=f)
    fr = t[:, None] * inv[None, :]
    fr = np.concatenate([fr, fr], -1)
    base = (half + f(0.4 * LD)) / f(1.4 * LD)
    power = (t - f(S // 2)) / f(WIN // 2)
    sc = np.power(base[None, :], power[:, None])
    sc = np.concatenate([sc, sc], -1).astype(f)
    cos, sin = np.cos(fr).astype(f), np.sin(fr).astype(f)
    sgn = np.concatenate([-np.ones(LD // 2, f), np.ones(LD // 2, f)])
    c = np.stack([cos * sc * f(QK_SCALE), cos / sc], 1)
    s = np.stack([sin * sc * sgn * f(QK_SCALE), sin / sc * sgn], 1)
    lay = lambda a: a.reshape(UPS, P, 2, LD).transpose(1, 0, 2, 3).reshape(P, -1).astype(f)
    return lay(c), lay(s)


def constants():
    f = np.float32
    p = np.arange(P)
    cos, sin = position_tables()
    own = (p[:, None] // XD == np.arange(XH)[None, :]).astype(f)
    half = (p[:, None] // SC == np.arange(2)[None, :]).astype(f)
    iota = np.broadcast_to(np.arange(E, dtype=f), (P, E))
    c32 = np.concatenate([np.eye(P, dtype=f), own, half, iota, cos, sin], 1)
    q = p % WIN
    m = np.zeros((P, UPS, 2, 2, WIN), f)
    k = np.arange(WIN)
    for u in range(UPS):
        for x in range(2):
            w = 2 * u + x
            for slot, kw in enumerate(local_keys(w)):
                off = (kw - w) * WIN if kw is not None else None
                rel = None if off is None else k[None, :] + off - q[:, None]
                bad = np.ones((P, WIN), bool) if rel is None else (rel > 0) | (rel < -WIN)
                m[:, u, x, slot] = np.where(bad, AWAY, 0)
    causal = np.where(k[None, :] > p[:, None], AWAY, 0).astype(f)
    c16 = np.concatenate([np.eye(P, dtype=f), np.ones((P, P), f), causal, m.reshape(P, -1)], 1)
    return np.ascontiguousarray(c32), np.ascontiguousarray(c16.astype(f))


def local_keys(w):
    return (w, w - 1 if w else None) if w % 2 == 0 else (w - 1, w)


class Unit:

    def __init__(self, j, c):
        self.j, self.c = j, c

    def at(self, per, add=0):
        return self.j * (UNROLL * per) + (self.c * per + add)

    def half(self, per, add=0):
        return self.j * (UNROLL // 2 * per) + (self.c // 2 * per + add)

    def back(self, k):
        return Unit(self.j, self.c - k)

    @property
    def u(self):
        return self.c % 2

    @property
    def bp(self):
        return self.c // 2 % 2

    @property
    def ring(self):
        return self.c % UNROLL


class Sig:

    def __init__(self, sem, base, per, units, halved=False, total=None):
        self.sem, self.base, self.per, self.units, self.halved = sem, base, per, units, halved
        self.total = per * (units // 2 if halved else units) if total is None else total

    def wait(self, eng, unit, count=None):
        if isinstance(unit.j, int):
            n = unit.at(1)
            if n < 0:
                return
            unit = Unit(0, min(n, self.units - 1))
        n = self.per if count is None else count
        eng.wait_ge(self.sem, (unit.half if self.halved else unit.at)(self.per, self.base + n))

    def wait_count(self, eng, n):
        eng.wait_ge(self.sem, self.base + n)

    def wait_all(self, eng):
        self.wait_count(eng, self.total)


def run_stages(eng, stages, units=T):
    lags = [lag for lag, _ in stages]
    first = -(-(max(lags) + 4) // UNROLL) * UNROLL

    def step(s):
        for lag, stage in stages:
            if 0 <= s - lag < units:
                stage(Unit(0, s - lag))

    for s in range(first):
        step(s)
    with eng.Fori(first // UNROLL, units // UNROLL, 1) as j:
        for c in range(UNROLL):
            for lag, stage in stages:
                stage(Unit(j, c - lag))
    for s in range(units, units + max(lags)):
        step(s)


def build(nc, a, out):
    with ExitStack() as ctx:
        def sb(name, cols, dt=F32, rows=P):
            return ctx.enter_context(nc.sbuf_tensor(name, [rows, cols], dt))

        def bank(name, n=1):
            return ctx.enter_context(nc.psum_tensor(name, [P, 512 * n], F32))

        def sem(name):
            return ctx.enter_context(nc.semaphore(name))

        x = sb("x", T * D)
        y = sb("y", T * D)
        y2 = sb("y2", T * D)
        c32 = sb("c32", a["c32"].shape[1])
        c16 = sb("c16", a["c16"].shape[1], BF16)
        o = 0
        ident = c32[:, 0:P]
        own = c32[:, P:P + XH]
        halves = c32[:, P + XH:P + XH + 2]
        iota = c32[:, P + XH + 2:P + XH + 2 + E]
        o = P + XH + 2 + E
        nt = UPS * 2 * LD
        cos_t, sin_t = c32[:, o:o + nt], c32[:, o + nt:o + 2 * nt]
        ident16 = c16[:, 0:P]
        ones16 = c16[0:1, P:2 * P]
        causal = c16[0:WIN, 2 * P:2 * P + SC]
        lmask = c16[:, 2 * P + SC:].rearrange("p (u n) -> p u n", u=UPS)
        small = sb("small", 64)
        neg_half, one = small[:, 0:1], small[:, 1:2]
        tg = small[:, 2:6]
        graw = small[:, 6:10]
        bq, bk = small[:, 10:11], small[:, 11:12]
        wq = [sb(f"wq{l}", D) for l in range(2)]
        wk = [sb(f"wk{l}", D) for l in range(2)]
        wv = [sb(f"wv{l}", D) for l in range(2)]
        wo = [sb(f"wo{l}", D) for l in range(2)]
        bv = sb("bv", D)
        bfc = sb("bfc", D, F32, 1)
        ones_row = sb("ones_row", P, F32, 1)

        progs = {e: [] for e in ("sync", "scalar", "vector", "gpsimd", "tensor")}
        phase = {}
        idle = []

        def sig(name, per, units=T, halved=False, total=None):
            number, base = idle.pop(0) if idle else (sem(f"sem_{phase['name']}{name}"), 0)
            s = Sig(number, base, per, units, halved, total)
            phase["sigs"].append(s)
            return s

        def prog(engine):
            return lambda f: progs[engine].append(f)

        def phase_begin(name):
            mem = ExitStack()
            phase.update(name=name + "_", sigs=[], mem=mem)

            def psb(label, cols, dt=F32, rows=P):
                return mem.enter_context(nc.sbuf_tensor(f"{name}_{label}", [rows, cols], dt))

            def many(label, n, cols, dt=F32):
                return [psb(f"{label}{i}", cols, dt) for i in range(n)]

            def pbank(label, n=1):
                return mem.enter_context(nc.psum_tensor(f"{name}_{label}", [P, 512 * n], F32))
            return psb, many, pbank

        def phase_end():
            done = list(phase["sigs"])
            idle.extend((s.sem, s.base + s.total) for s in done)
            phase["mem"].close()
            for e in progs:
                progs[e].append(lambda eng: [s.wait_all(eng) for s in done])

        tok = lambda t, n: t[:, bass.ds(n.at(D), D)]

        boot, _, _ = phase_begin("boot")
        c16f = boot("c16f", a["c16"].shape[1])
        graws = [a["g_xattn"], a["g_ffn"]]
        col = lambda v: v.rearrange("(p o) -> p o", o=1)
        loads = [
            (c32[:, :], a["c32"]), (c16f[:, :], a["c16"]),
            (x[:, :].rearrange("p (t d) -> p t d", d=D), a["x"].rearrange("b (u p) d -> p (b u) d", p=P)),
            (graw[:, 0:2], graws[0].partition_broadcast(P)), (graw[:, 2:4], graws[1].partition_broadcast(P)),
            (bq, col(a["L1_xattn_bq"])), (bk, col(a["L1_xattn_bk"])), (bv[:, :], a["L1_xattn_bv"].partition_broadcast(P)),
        ]
        loads.append((bfc[:, :], a["L1_xattn_bfc"].rearrange("(o d) -> o d", o=1)))
        for l, names in enumerate((("Wq", "Wk", "Wv", "Wo"), ("Wq", "Wk", "Wv", "Wfc"))):
            loads += [(w[l][:, :], a[f"L{l}_xattn_{name}T"]) for w, name in zip((wq, wk, wv, wo), names)]
        s_load = sig("load", 0, total=16 * len(loads))
        s_clear = sig("clear", 0, total=3)
        s_tanh = sig("tanh", 0, total=1)
        s_c16 = sig("c16", 0, total=1)

        @prog("vector")
        def _(v):
            s_load.wait_all(v)
            v.tensor_copy(c16[:, :], c16f[:, :]).then_inc(s_c16.sem, 1)

        @prog("gpsimd")
        def _(g):
            for t, v_ in ((ones_row[:, :], 1.0), (neg_half, -0.5), (one, 1.0)):
                g.memset(t, v_).then_inc(s_clear.sem, 1)

        @prog("sync")
        def _(sp):
            for dst, src in loads:
                sp.dma_start(dst, src).then_inc(s_load.sem, 16)

        @prog("scalar")
        def _(act):
            s_load.wait_all(act)
            act.activation(tg, graw, ACT.Tanh).then_inc(s_tanh.sem, 1)
        phase_end()

        s_spare = {e: sem(f"spare_{e}") for e in ("vector", "gpsimd")}

        def alone(eng, name):
            eng.sem_inc(s_spare[name], 1)

        def layernorm(name, src, st, s_ready):
            s_st = sig(name + "_stats", 2)
            s_nm = sig(name + "_norm", 1)
            s_rs = sig(name + "_rstd", 2)

            def stats(v, n):
                t = st[n.u]
                if s_ready:
                    s_ready.wait(v, n)
                s_nm.wait(v, n.back(2))
                alone(v, "vector")
                v.bn_stats(t[:, 0:6], src(n)).then_inc(s_st.sem, 1)
                s_st.wait(v, n, 1)
                alone(v, "vector")
                v.bn_aggr(t[:, 6:8], t[:, 0:6]).then_inc(s_st.sem, 1)

            def rstd(g, n):
                t = st[n.u]
                s_st.wait(g, n)
                s_nm.wait(g, n.back(2))
                alone(g, "gpsimd")
                g.tensor_scalar(t[:, 8:9], t[:, 7:8], 1e-5, None, ALU.add).then_inc(s_rs.sem, 1)
                s_rs.wait(g, n, 1)
                g.tensor_tensor(t[:, 9:10], t[:, 8:9], neg_half, ALU.pow).then_inc(s_rs.sem, 1)

            def norm(v, n, dst, free=None):
                t = st[n.u]
                s_rs.wait(v, n)
                if free:
                    free.wait(v, n.back(2))
                v.tensor_scalar(dst, src(n), t[:, 6:7], t[:, 9:10], ALU.subtract, ALU.mult).then_inc(s_nm.sem, 1)
            return s_nm, stats, rstd, norm

        def cross_attention(l):
            res = ExitStack()
            rsb = lambda name, cols, dt=F32, rows=P: res.enter_context(nc.sbuf_tensor(f"x{l}_{name}", [rows, cols], dt))
            kT = rsb("kT", B * SC)
            vall = rsb("vall", B * D)
            padrow = rsb("padrow", B * SC, BF16, 1)
            if not l:
                maskc = rsb("maskc", B)
                maskci = rsb("maskci", B, I32)

            psb, many, pbank = phase_begin(f"xc{l}")
            ctxT = psb("ctxT", B * SC)
            maski, maskf = psb("maski", B * SC, I32), psb("maskf", B * SC)
            ctx2 = many("ctx2", 2, P)
            ps_k, ps_v = pbank("ps_k", 2), [pbank(f"ps_v{i}") for i in range(2)]
            s_c = sig("c", 0, total=32 if l else 64)
            s_mc = sig("mc", 0, total=0 if l else 2)
            s_k = sig("k", 0, total=1)
            s_ks = sig("ks", 0, total=1)
            s_md = sig("md", 0, total=4 if l else 2)
            s_cd = sig("cd", 2, B)
            s_vp = sig("vp", 1, B)
            s_ve = sig("ve", 1, B)
            mask = a[("mask_BxS2_if1", "mask_BxS2_ik0")[l]].rearrange("b s -> (b s)")

            @prog("sync")
            def _(sp):
                sp.dma_start(ctxT[:, :], a["ctxT"]).then_inc(s_c.sem, 16)
                sp.dma_start(maski[:, :], mask.partition_broadcast(P)).then_inc(s_c.sem, 16)
                if not l:
                    for i in range(2):
                        sp.dma_start(maskci[SC * i:SC * i + SC, :], a["mask0T"]).then_inc(s_c.sem, 16)

            @prog("tensor")
            def _(pe):
                s_c.wait_all(pe)
                for i in range(2):
                    m = pe.matmul(ps_k[:, 512 * i:512 * i + 512], wk[l][:, :], ctxT[:, 512 * i:512 * i + 512],
                                  start=True, stop=True)
                m.then_inc(s_k.sem, 1)

                def values(n):
                    s_cd.wait(pe, n)
                    s_ve.wait(pe, n.back(2))
                    pe.matmul(ps_v[n.u][:, 0:D], ctx2[n.u][:, :], wv[l][:, :], start=True, stop=True)\
                        .then_inc(s_vp.sem, 1)
                run_stages(pe, [(0, values)], B)

            @prog("scalar")
            def _(act):
                s_k.wait_all(act)
                act.activation(kT[:, :], ps_k[:, :], ACT.Identity, bias=bk if l else 0.0).then_inc(s_ks.sem, 1)

            @prog("vector")
            def _(v):
                s_c.wait_all(v)
                v.tensor_copy(maskf[:, :], maski[:, :]).then_inc(s_md.sem, 1)
                s_md.wait_count(v, 1)
                v.tensor_scalar(padrow[:, :], maskf[0:1, :], 0.0, -1e10 * XD ** 0.5 if l else PADDED,
                                ALU.is_equal, ALU.mult).then_inc(s_md.sem, 1)
                if l:
                    s_md.wait_count(v, 2)
                    v.tensor_scalar(maskf[:, :], maskf[:, :], 0.0, None, ALU.not_equal).then_inc(s_md.sem, 1)
                    s_md.wait_count(v, 3)
                    s_ks.wait_all(v)
                    v.tensor_tensor(kT[:, :], kT[:, :], maskf[:, :], ALU.mult).then_inc(s_md.sem, 1)

                if not l:
                    v.tensor_copy(maskc[:, :], maskci[:, :]).then_inc(s_mc.sem, 1)
                    s_mc.wait_count(v, 1)
                    v.tensor_scalar(maskc[:, :], maskc[:, :], 0.0, None, ALU.not_equal).then_inc(s_mc.sem, 1)
                    s_mc.wait_all(v)

                def values(n):
                    s_vp.wait(v, n)
                    if l:
                        i = v.tensor_tensor(tok(vall, n), ps_v[n.u][:, 0:D], bv[:, :], ALU.add)
                    else:
                        i = v.tensor_tensor(tok(vall, n), ps_v[n.u][:, 0:D],
                                            maskc[:, bass.ds(n.at(1), 1)].broadcast_to([P, D]), ALU.mult)
                    i.then_inc(s_ve.sem, 1)
                run_stages(v, [(0, values)], B)

            @prog("gpsimd")
            def _(g):
                s_c.wait_all(g)

                def twice(n):
                    s_vp.wait(g, n.back(2))
                    for i in range(2):
                        g.tensor_copy(ctx2[n.u][:, SC * i:SC * i + SC], ctxT[:, bass.ds(n.at(SC), SC)])\
                            .then_inc(s_cd.sem, 1)
                run_stages(g, [(0, twice)], B)
            phase_end()

            psb, many, pbank = phase_begin(f"x{l}")
            st, st2, stat = many("st", 2, 16), many("st2", 2, 16), many("stat", 2, 2 * XH)
            h, hT, qT = many("h", 2, D), many("hT", 2, D), many("qT", 2, D)
            e_ = many("e", 2, XH * SC)
            eT = many("eT", 2, XH * SC)
            od = many("od", 2, 2 * P)
            on, onT = many("on", 2, D), many("onT", 2, D)
            kblk, vpair = many("kblk", 2, XH * SC), many("vpair", 2, XP * 32)
            ps_s, ps_t = pbank("ps_s", 2), pbank("ps_t", 2)
            ps_x, ps_q, ps_o, ps_w = (pbank(f"ps{i}") for i in range(4))
            s_z = sig("z", 0, total=4 if l else 2)
            s_h, s_hc, s_q, s_qc = (sig(i, 1) for i in ("h", "hc", "q", "qc"))
            s_blk = sig("blk", 3 if l else 4, T, True)
            s_s, s_e, s_t, s_tc, s_o, s_oc, s_w, s_up = (sig(i, 1) for i in ("s", "e", "t", "tc", "o", "oc", "w", "up"))
            s_sm = sig("sm", 2)
            s_ot = sig("ot", 1)
            s_on = sig("on", 2)
            s_nt, s_nc = sig("nt", 1), sig("nc", 1)
            s_ln, ln_stats, ln_rstd, ln_norm = layernorm("ln", lambda n: tok(x, n), st, None)
            if not l:
                _, y_stats, y_rstd, y_norm = layernorm("ly", lambda n: tok(x, n), st2, s_up)

            @prog("tensor")
            def _(pe):
                def transpose_h(n):
                    s_ln.wait(pe, n)
                    s_hc.wait(pe, n.back(1))
                    pe.transpose(ps_x[:, 0:P], h[n.u][:, :], ident).then_inc(s_h.sem, 1)

                def project_q(n):
                    s_hc.wait(pe, n)
                    s_qc.wait(pe, n.back(1))
                    pe.matmul(ps_q[:, 0:P], wq[l][:, :], hT[n.u][:, :], start=True, stop=True).then_inc(s_q.sem, 1)

                def scores(n):
                    s_qc.wait(pe, n)
                    s_blk.wait(pe, n)
                    s_sm.wait(pe, n.back(1))
                    for i in range(2):
                        dst = ps_s[:, 512 * i:512 * i + 512]
                        pad = padrow[0:1, bass.ds(n.half(SC), SC)].unsqueeze(1).broadcast_to([1, XH // 2, SC])
                        pe.matmul(dst, qT[n.u][:, :], kblk[n.bp][:, 512 * i:512 * i + 512], start=True, stop=False)
                        if not l and n.u == 0:
                            pe.matmul(dst, ident16[0:SC, :], causal.unsqueeze(1).broadcast_to([SC, XH // 2, SC]),
                                      start=False, stop=False)
                        m = pe.matmul(dst, ones16, pad, start=False, stop=True)
                    m.then_inc(s_s.sem, 1)

                def transpose_e(n):
                    s_e.wait(pe, n)
                    s_tc.wait(pe, n.back(1))
                    for i in range(XP):
                        m = pe.transpose(ps_t[:, P * i:P * i + P], e_[n.u][:, P * i:P * i + P], ident)
                    m.then_inc(s_t.sem, 1)

                def outputs(n):
                    s_tc.wait(pe, n)
                    s_on.wait(pe, n.back(1))
                    for pair in range(XP):
                        r, j = divmod(pair, 4)
                        m = pe.matmul(ps_o[32 * j:32 * j + 32, P * r:P * r + P],
                                      vpair[n.bp][:, 32 * pair:32 * pair + 32],
                                      eT[n.u][:, P * pair:P * pair + P], start=True, stop=True)
                    m.then_inc(s_o.sem, 1)

                def transpose_o(n):
                    s_oc.wait(pe, n)
                    for r in range(2):
                        m = pe.transpose(ps_o[:, 256 + P * r:256 + P * r + P], od[n.u][:, P * r:P * r + P], ident)
                    m.then_inc(s_ot.sem, 1)

                def transpose_on(n):
                    s_on.wait(pe, n)
                    s_up.wait(pe, n.back(1))
                    pe.transpose(ps_w[:, P:2 * P], on[n.u][:, :], ident).then_inc(s_nt.sem, 1)

                def project_o(n):
                    s_nc.wait(pe, n)
                    m = pe.matmul(ps_w[:, 0:D], onT[n.u][:, :], wo[l][:, :], start=True, stop=not l)
                    if l:
                        m = pe.matmul(ps_w[:, 0:D], ones_row[:, :], bfc[:, :], start=False, stop=True)
                    m.then_inc(s_w.sem, 1)
                run_stages(pe, [(5, transpose_e), (6, transpose_o), (3, project_q), (7, transpose_on), (2, transpose_h),
                                (4, scores), (7, project_o), (5, outputs)])

            @prog("scalar")
            def _(act):
                def copy_h(n):
                    s_h.wait(act, n)
                    s_q.wait(act, n.back(2))
                    act.activation(hT[n.u][:, :], ps_x[:, 0:P], ACT.Copy).then_inc(s_hc.sem, 1)

                def copy_q(n):
                    s_q.wait(act, n)
                    s_s.wait(act, n.back(2))
                    act.activation(qT[n.u][:, :], ps_q[:, 0:P], ACT.Identity, bias=bq if l else 0.0)\
                        .then_inc(s_qc.sem, 1)

                def exps(n):
                    s_sm.wait(act, n)
                    act.activation(e_[n.u][:, :], e_[n.u][:, :], ACT.Exp, scale=XD ** -0.5).then_inc(s_e.sem, 1)

                def copy_e(n):
                    s_t.wait(act, n)
                    s_o.wait(act, n.back(2))
                    act.activation(eT[n.u][:, :], ps_t[:, :], ACT.Copy).then_inc(s_tc.sem, 1)

                def copy_o(n):
                    s_o.wait(act, n)
                    s_ot.wait(act, n.back(2))
                    act.activation(od[n.u][:, :], ps_o[:, 0:2 * P], ACT.Copy).then_inc(s_oc.sem, 1)

                def copy_on(n):
                    s_nt.wait(act, n)
                    s_w.wait(act, n.back(2))
                    act.activation(onT[n.u][:, :], ps_w[:, P:2 * P], ACT.Copy).then_inc(s_nc.sem, 1)
                run_stages(act, [(5, copy_e), (3, copy_q), (7, copy_on), (2, copy_h), (4, exps), (5, copy_o)])

            @prog("vector")
            def _(v):
                def softmax(n):
                    s_s.wait(v, n)
                    sc = ps_s[:, :].rearrange("p (h k) -> p h k", k=SC)
                    v.tensor_reduce(stat[n.u][:, 0:XH], sc, AX_X, ALU.max, negate=True).then_inc(s_sm.sem, 1)
                    s_sm.wait(v, n, 1)
                    s_t.wait(v, n.back(2))
                    v.tensor_tensor(e_[n.u][:, :].rearrange("p (h k) -> p h k", k=SC), sc,
                                    stat[n.u][:, 0:XH].unsqueeze(2).broadcast_to([P, XH, SC]), ALU.add)\
                        .then_inc(s_sm.sem, 1)

                def update(n):
                    s_w.wait(v, n)
                    v.scalar_tensor_tensor(out=tok(x, n), in0=ps_w[:, 0:D], scalar=tg[:, l:l + 1], in1=tok(x, n),
                                           op0=ALU.mult, op1=ALU.add).then_inc(s_up.sem, 1)

                def divide(n):
                    s_ot.wait(v, n)
                    s_nt.wait(v, n.back(2))
                    o4 = ps_o[:, 256:512].rearrange("p (r c) -> p r c", c=32)
                    inv = stat[n.u][:, XH:2 * XH].rearrange("p (r e) -> p r e", e=2)
                    v.reciprocal(inv, o4[:, :, 16:18]).then_inc(s_on.sem, 1)
                    s_on.wait(v, n, 1)
                    v.tensor_tensor(on[n.u][:, :].rearrange("p (r e d) -> p r e d", e=2, d=XD),
                                    o4[:, :, 0:16].rearrange("p r (e d) -> p r e d", e=2),
                                    inv.unsqueeze(3).broadcast_to([P, XP, 2, XD]), ALU.mult).then_inc(s_on.sem, 1)
                stages = [(0, lambda n: ln_stats(v, n)), (6, divide), (1, lambda n: ln_norm(v, n, h[n.u][:, :], s_h)),
                          (7, update), (4, softmax)]
                if not l:
                    stages = [(9, lambda n: y_norm(v, n, tok(y, n))), (8, lambda n: y_stats(v, n))] + stages
                run_stages(v, stages)

            @prog("gpsimd")
            def _(g):
                for t in vpair:
                    g.memset(t[:, :], 0.0).then_inc(s_z.sem, 1)
                s_z.wait_count(g, 2)
                sum_cols = lambda t: t[:, :].rearrange("p (r c) -> p r c", c=32)[:, :, 16:18]
                if l:
                    for t in vpair:
                        g.tensor_copy(sum_cols(t), halves.unsqueeze(1).broadcast_to([P, XP, 2])).then_inc(s_z.sem, 1)
                    s_z.wait_all(g)

                def blocks(n):
                    if n.u:
                        return
                    s_o.wait(g, n.back(3))
                    g.tensor_tensor(kblk[n.bp][:, :].rearrange("p (h k) -> p h k", k=SC),
                                    kT[:, bass.ds(n.half(SC), SC)].unsqueeze(1).broadcast_to([P, XH, SC]),
                                    own.unsqueeze(2).broadcast_to([P, XH, SC]), ALU.mult).then_inc(s_blk.sem, 1)
                    for i in range(2):
                        s_blk.wait(g, n, 1 + i)
                        src = vall[SC * i:SC * i + SC, bass.ds(n.half(D), D)]\
                            .rearrange("p (r e d) -> p r e d", e=2, d=XD)[:, :, i, :]
                        dst = vpair[n.bp][SC * i:SC * i + SC, :].rearrange("p (r c) -> p r c", c=32)
                        g.tensor_copy(dst[:, :, XD * i:XD * i + XD], src).then_inc(s_blk.sem, 1)
                    s_blk.wait(g, n, 3)
                    if not l:
                        mc = maskc[:, bass.ds(n.half(1), 1)].unsqueeze(2).broadcast_to([P, XP, 2])
                        g.tensor_tensor(sum_cols(vpair[n.bp]), halves.unsqueeze(1).broadcast_to([P, XP, 2]), mc,
                                        ALU.mult).then_inc(s_blk.sem, 1)

                stages = [(0, lambda n: ln_rstd(g, n)), (2, blocks)]
                if not l:
                    stages = [(8, lambda n: y_rstd(g, n))] + stages
                run_stages(g, stages)
            phase_end()
            res.close()

        def shift(sp, h, s_d, s_free, src):
            def stage(n):
                s_free.wait(sp, n.back(2))
                t, s = h[n.u], s_d[n.u].sem
                sp.dma_start(t[:, 0:64], src[:, bass.ds(n.at(D), 64)]).then_inc(s, 16)
                sp.dma_start(t[1:P, 64:D], src[0:P - 1, bass.ds(n.at(D, 64), 64)]).then_inc(s, 16)
                if n.u:
                    sp.dma_start(t[0:1, 64:D], src[P - 1:P, bass.ds(n.at(D, 64 - D), 64)]).then_inc(s, 16)
            return stage

        def local_attention(l):
            psb, many, pbank = phase_begin(f"a{l}")
            wqkv, lwo = psb("wqkv", 3 * INNER), psb("wo", LP * D)
            scl = psb("scl", 4 * LD)
            rtab = psb("rtab", 2 * nt)
            h, hT = many("h", 2, D), many("hT", 2, D)
            sq = many("sq", 1, 2 * INNER)
            rot, rot2 = many("rot", 2, 2 * INNER), many("rot2", 1, 2 * INNER)
            stat = many("stat", 2, 64)
            qbd = many("qbd", 2, LP * 2 * P)
            kTr = many("kTr", 2, LP * S)
            vt, vx = many("vt", UNROLL, INNER), many("vx", 2, INNER)
            e_, eT = many("e", 2, LP * 2 * P), many("eT", 2, LP * 2 * P)
            oT = many("oT", 2, INNER)
            ps_qk, ps_s, ps_t = pbank("ps_qk", 2), pbank("ps_s", 2), pbank("ps_t", 2)
            ps_a, ps_b = pbank("ps_a"), pbank("ps_b")
            wl = [(wqkv[:, :], a["L0_ffn_wqkv"][l]),
                  (lwo[:, :].rearrange("p (c d) -> p c d", d=D), a["L0_ffn_wo"][l].rearrange("(c p) d -> p c d", p=P))]
            for i, name in enumerate(("L0_ffn_q_scale", "L0_ffn_k_scale")):
                v_ = a[name][l]
                for lo, src in ((LD * i, v_), (2 * LD + LD * i, v_[LD // 2:LD]), (2 * LD + LD * i + LD // 2, v_[0:LD // 2])):
                    wl.append((scl[:, lo:lo + src.shape[0]], src.partition_broadcast(P)))
            s_wl = sig("wl", 0, total=16 * len(wl))
            s_tab = sig("tab", 0, total=2 * UPS)
            s_z = sig("z", 0, total=3)
            s_d = [sig("d0", 32, T, True), sig("d1", 48, T, True)]
            s_h, s_hc, s_vc, s_t, s_kc, s_s, s_en, s_et, s_o, s_oc, s_y, s_yc = (
                sig(i, 1) for i in ("h", "hc", "vc", "t", "kc", "s", "en", "et", "o", "oc", "y", "yc"))
            s_qkv = sig("qkv", 2)
            s_vx = [sig(f"vx{u}", 1, T, True) for u in range(2)]
            s_sq = sig("sq", 2)
            s_r = sig("r", 7)
            s_n = sig("n", 4)
            s_qc = sig("qc", 2)
            s_mx = sig("mx", 2)
            s_e = sig("e", 2 * LP)
            s_ecv, s_eca = sig("ecv", 1), sig("eca", 1)

            @prog("sync")
            def _(sp):
                for dst, src in wl:
                    sp.dma_start(dst, src).then_inc(s_wl.sem, 16)
                s_z.wait_all(sp)
                run_stages(sp, [(0, shift(sp, h, s_d, s_h, y))])

            @prog("tensor")
            def _(pe):
                s_wl.wait_all(pe)

                def transpose_h(n):
                    s_d[n.u].wait(pe, n)
                    s_yc.wait(pe, n.back(5))
                    pe.transpose(ps_a[:, 0:P], h[n.u][:, :], ident).then_inc(s_h.sem, 1)

                def qkv(n):
                    s_hc.wait(pe, n)
                    s_r.wait(pe, n.back(1))
                    s_sq.wait(pe, n.back(1))
                    for i in range(2):
                        m = pe.matmul(ps_qk[:, 512 * i:512 * i + 512], hT[n.u][:, :], wqkv[:, 512 * i:512 * i + 512],
                                      start=True, stop=True)
                    m.then_inc(s_qkv.sem, 1)
                    s_oc.wait(pe, n.back(4))
                    pe.matmul(ps_b[:, :], hT[n.u][:, :], wqkv[:, 1024:1536], start=True, stop=True)\
                        .then_inc(s_qkv.sem, 1)

                def transpose_qk(n):
                    s_n.wait(pe, n)
                    s_ecv.wait(pe, n.back(2))
                    s_eca.wait(pe, n.back(2))
                    for i in range(2 * LP):
                        m = pe.transpose(ps_t[:, P * i:P * i + P], rot[n.u][:, P * i:P * i + P], ident)
                    m.then_inc(s_t.sem, 1)

                def scores(n):
                    s_qc.wait(pe, n)
                    s_kc.wait(pe, n)
                    s_e.wait(pe, n.back(1))
                    for i in range(2):
                        dst = ps_s[:, 512 * i:512 * i + 512]
                        pe.matmul(dst, ident16, lmask[:, n.u, :].unsqueeze(1).broadcast_to([P, 2, 2 * P]),
                                  start=True, stop=False)
                        for k in range(4):
                            pair, x_ = 2 * i + k // 2, k % 2
                            at = P * (2 * pair + x_)
                            ky = kTr[n.bp][:, S * pair:S * pair + S].rearrange("p (w k) -> p w k", k=WIN)
                            w = 2 * n.u + x_
                            own_, other = local_keys(w)
                            if other is None:
                                ky = ky[:, own_:own_ + 1, :].broadcast_to([P, 2, WIN])
                            elif other < own_:
                                ky = ky[:, other:own_ + 1, :][:, ::-1, :]
                            else:
                                ky = ky[:, own_:other + 1, :]
                            m = pe.matmul(ps_s[:, at:at + P].rearrange("p (w k) -> p w k", k=WIN),
                                          qbd[n.u][:, at:at + P], ky, start=False, stop=(k == 3))
                    m.then_inc(s_s.sem, 1)

                def transpose_e(n):
                    s_en.wait(pe, n)
                    s_qc.wait(pe, n.back(-1))
                    s_kc.wait(pe, n.back(-1))
                    for i in range(2 * LP):
                        m = pe.transpose(ps_t[:, P * i:P * i + P], e_[n.u][:, P * i:P * i + P], ident)
                    m.then_inc(s_et.sem, 1)

                def outputs(n):
                    s_ecv.wait(pe, n)
                    s_eca.wait(pe, n)
                    if n.u:
                        s_vx[0].wait(pe, n)
                        s_vx[1].wait(pe, n)
                    s_vc.wait(pe, n.back(-3))
                    for pair in range(LP):
                        for x_ in range(2):
                            w = 2 * n.u + x_
                            vv = vx[n.bp] if w == 2 else vt[n.ring]
                            at = P * (2 * pair + x_)
                            for e in range(2):
                                m = pe.matmul(ps_b[LD * e:LD * e + LD, P * pair + WIN * x_:P * pair + WIN * x_ + WIN],
                                              vv[:, P * pair + LD * e:P * pair + LD * e + LD],
                                              eT[n.u][:, at + WIN * e:at + WIN * e + WIN], start=True, stop=True)
                    m.then_inc(s_o.sem, 1)

                def project(n):
                    s_oc.wait(pe, n)
                    s_hc.wait(pe, n.back(-4))
                    for pair in range(LP):
                        m = pe.matmul(ps_a[:, 0:D], oT[n.u][:, P * pair:P * pair + P], lwo[:, D * pair:D * pair + D],
                                      start=(pair == 0), stop=(pair == LP - 1))
                    m.then_inc(s_y.sem, 1)
                run_stages(pe, [(4, scores), (5, transpose_e), (6, project), (2, qkv), (5, outputs), (1, transpose_h),
                                (3, transpose_qk)])

            @prog("scalar")
            def _(act):
                def copy_k(n):
                    s_t.wait(act, n)
                    s_s.wait(act, n.back(2))
                    act.activation(kTr[n.bp][:, :].rearrange("p (r t) -> p r t", t=S)[:, :, P * n.u:P * n.u + P],
                                   ps_t[:, 512:1024].rearrange("p (r t) -> p r t", t=P), ACT.Copy).then_inc(s_kc.sem, 1)

                def copy_e(n):
                    s_et.wait(act, n)
                    s_o.wait(act, n.back(2))
                    act.activation(eT[n.u][:, 512:1024], ps_t[:, 512:1024], ACT.Copy).then_inc(s_eca.sem, 1)

                def exps(n):
                    s_mx.wait(act, n, 1)
                    s_et.wait(act, n.back(2))
                    for i in range(2 * LP):
                        act.activation(e_[n.u][:, P * i:P * i + P], ps_s[:, P * i:P * i + P], ACT.Exp,
                                       bias=stat[n.u][:, i:i + 1], accum_out=stat[n.u][:, 8 + i:9 + i])\
                            .then_inc(s_e.sem, 1)

                def square(n):
                    s_qkv.wait(act, n, 1)
                    s_r.wait(act, n.back(1))
                    for i in range(2):
                        at = slice(INNER * i, INNER * i + INNER)
                        act.activation(sq[0][:, at], ps_qk[:, at], ACT.Square).then_inc(s_sq.sem, 1)

                def copy_v(n):
                    s_qkv.wait(act, n)
                    s_o.wait(act, n.back(4))
                    if n.u:
                        act.activation(vx[n.bp][0:WIN, :], ps_b[0:WIN, :], ACT.Copy).then_inc(s_vx[1].sem, 1)
                    else:
                        s_vx[0].wait(act, n.back(4))
                    act.activation(vt[n.ring][:, :], ps_b[:, :], ACT.Copy).then_inc(s_vc.sem, 1)

                def copy_vx(n):
                    if not n.u:
                        s_vc.wait(act, n)
                        s_o.wait(act, n.back(3))
                        act.activation(vx[n.bp][WIN:P, :], vt[n.ring][WIN:P, :], ACT.Copy).then_inc(s_vx[0].sem, 1)

                def copy_h(n):
                    s_h.wait(act, n)
                    s_qkv.wait(act, n.back(2))
                    act.activation(hT[n.u][:, :], ps_a[:, 0:P], ACT.Copy).then_inc(s_hc.sem, 1)
                run_stages(act, [(4, copy_k), (5, copy_e), (4, exps), (2, square), (2, copy_v), (4, copy_vx), (1, copy_h)])

            @prog("vector")
            def _(v):
                s_wl.wait_all(v)
                for u in range(UPS):
                    for i, src in enumerate((cos_t, sin_t)):
                        w = 2 * LD
                        v.tensor_tensor(rtab[:, nt * i + w * u:nt * i + w * u + w], src[:, w * u:w * u + w],
                                        scl[:, w * i:w * i + w], ALU.mult).then_inc(s_tab.sem, 1)
                s_tab.wait_all(v)
                s_z.wait_all(v)

                def copy_q(n):
                    s_t.wait(v, n)
                    s_s.wait(v, n.back(2))
                    for e in range(2):
                        dst = qbd[n.u][LD * e:LD * e + LD, :].rearrange("p (r e q) -> p r e q", e=2, q=WIN)[:, :, e, :]
                        v.tensor_copy(dst, ps_t[LD * e:LD * e + LD, 0:512].rearrange("p (r q) -> p r q", q=WIN))\
                            .then_inc(s_qc.sem, 1)

                def maxima(n):
                    s_s.wait(v, n)
                    s_mx.wait(v, n.back(2))
                    s_en.wait(v, n.back(2))
                    v.tensor_reduce(stat[n.u][:, 0:8], ps_s[:, :].rearrange("p (r k) -> p r k", k=P), AX_X, ALU.max,
                                    negate=True).then_inc(s_mx.sem, 1)

                def sums(n):
                    s_e.wait(v, n)
                    v.reciprocal(stat[n.u][:, 16:24], stat[n.u][:, 8:16]).then_inc(s_mx.sem, 1)

                def copy_e(n):
                    s_et.wait(v, n)
                    s_o.wait(v, n.back(2))
                    v.tensor_copy(eT[n.u][:, 0:512], ps_t[:, 0:512]).then_inc(s_ecv.sem, 1)

                def update(n):
                    s_y.wait(v, n)
                    v.tensor_tensor(tok(y2, n), ps_a[:, 0:D], tok(y, n), ALU.add).then_inc(s_yc.sem, 1)

                def rotate(n):
                    s_qkv.wait(v, n, 1)
                    s_n.wait(v, n.back(1), 2)
                    s_t.wait(v, n.back(2))
                    for i in range(2):
                        s_sq.wait(v, n, i + 1)
                        at = slice(INNER * i, INNER * i + INNER)
                        qk, out1, out2 = (t[:, at].rearrange("p (h d) -> p h d", d=LD)
                                          for t in (ps_qk, rot[n.u], rot2[0]))
                        lo = 2 * LD * n.u + LD * i
                        cos_, sin_ = rtab[:, lo:lo + LD], rtab[:, nt + lo:nt + lo + LD]
                        v.tensor_tensor(out1, qk, cos_.unsqueeze(1).broadcast_to([P, LH, LD]), ALU.mult)\
                            .then_inc(s_r.sem, 1)
                        for lo in (0, LD // 2):
                            hi = LD // 2 - lo
                            v.tensor_tensor(out2[:, :, lo:lo + LD // 2], qk[:, :, hi:hi + LD // 2],
                                            sin_[:, lo:lo + LD // 2].unsqueeze(1).broadcast_to([P, LH, LD // 2]),
                                            ALU.mult).then_inc(s_r.sem, 1)
                    v.reduce_sum(stat[n.u][:, 32:48], sq[0][:, :].rearrange("p (h d) -> p h d", d=LD), axis=AX_X)\
                        .then_inc(s_r.sem, 1)

                def copy_o(n):
                    s_o.wait(v, n)
                    s_y.wait(v, n.back(2))
                    v.tensor_copy(oT[n.u][:, :], ps_b[:, :]).then_inc(s_oc.sem, 1)
                run_stages(v, [(4, copy_q), (4, maxima), (5, copy_e), (6, update), (4, sums), (2, rotate), (5, copy_o)])

            @prog("gpsimd")
            def _(g):
                for t in qbd:
                    g.memset(t[:, :], 0.0).then_inc(s_z.sem, 1)
                g.memset(h[0][0:1, 64:D], 0.0).then_inc(s_z.sem, 1)

                def normalise(n):
                    s_r.wait(g, n)
                    t = stat[n.u]
                    alone(g, "gpsimd")
                    g.tensor_scalar(t[:, 32:48], t[:, 32:48], 1e-24, None, ALU.max).then_inc(s_n.sem, 1)
                    r = rot[n.u][:, :]
                    g.tensor_tensor(r, r, rot2[0][:, :], ALU.add).then_inc(s_n.sem, 1)
                    s_n.wait(g, n, 2)
                    g.tensor_tensor(t[:, 48:64], t[:, 32:48], neg_half.broadcast_to([P, 16]), ALU.pow)\
                        .then_inc(s_n.sem, 1)
                    s_n.wait(g, n, 3)
                    r = r.rearrange("p (h d) -> p h d", d=LD)
                    g.tensor_tensor(r, r, t[:, 48:64].unsqueeze(2).broadcast_to([P, 16, LD]), ALU.mult)\
                        .then_inc(s_n.sem, 1)

                def attention(n):
                    s_mx.wait(g, n)
                    e3 = e_[n.u][:, :].rearrange("p (r k) -> p r k", k=P)
                    g.tensor_tensor(e3, e3, stat[n.u][:, 16:24].unsqueeze(2).broadcast_to([P, 8, P]), ALU.mult)\
                        .then_inc(s_en.sem, 1)
                run_stages(g, [(4, attention), (2, normalise)])
            phase_end()

        def mlp(l):
            psb, many, pbank = phase_begin(f"f{l}")
            w1, w2 = psb("w1", 2 * HID), psb("w2", 3 * D)
            vec = psb("vec", 8)
            h, hn, hT, st = many("h", 2, D), many("hn", 2, D), many("hT", 2, D), many("st", 2, 16)
            gl, act_ = many("gl", 2, 3 * P), many("act", 2, 3 * P)
            yo = many("yo", 2, D)
            ps_x, ps_y = [pbank(f"ps_x{i}") for i in range(2)], [pbank(f"ps_y{i}") for i in range(2)]
            ps_a, ps_g = [pbank(f"ps_a{i}") for i in range(2)], [pbank(f"ps_g{i}") for i in range(2)]
            bias = a["L0_ffn_b1"][l]
            wl = [(w1[:, :], a["L0_ffn_w1"][l]), (vec[:, 0:1], col(a["L0_ffn_ln_g"][l])),
                  (vec[:, 1:2], col(a["L0_ffn_ln_b"][l]))]
            for c, k in enumerate(HCH):
                wl += [(w2[0:k, D * c:D * c + D], a["L0_ffn_w2"][l][P * c:P * c + k, :]),
                       (vec[0:k, 2 + c:3 + c], col(bias[P * c:P * c + k])),
                       (vec[0:k, 5 + c:6 + c], col(bias[HID + P * c:HID + P * c + k]))]
            wl.append((w2[HCH[2]:HCH[2] + 1, 2 * D:3 * D], a["L0_ffn_b2"][l].rearrange("(o d) -> o d", o=1)))
            s_wl = sig("wl", 0, total=16 * len(wl))
            s_z = sig("z", 0, total=3)
            s_d = [sig("d0", 32, T, True), sig("d1", 48, T, True)]
            s_ln, ln_stats, ln_rstd, ln_norm = layernorm("ln", lambda n: h[n.u][:, :], st, None)
            s_t, s_hc, s_g, s_a, s_y, s_yc = (sig(i, 1) for i in ("t", "hc", "g", "a", "y", "yc"))
            s_gl, s_ac = sig("gl", 3), sig("ac", 3)
            s_up = sig("up", l)

            @prog("sync")
            def _(sp):
                for dst, src in wl:
                    sp.dma_start(dst, src).then_inc(s_wl.sem, 16)
                s_z.wait_all(sp)
                run_stages(sp, [(0, shift(sp, h, s_d, s_ln, y2))])

            @prog("tensor")
            def _(pe):
                s_wl.wait_all(pe)

                def transpose_h(n):
                    s_ln.wait(pe, n)
                    s_hc.wait(pe, n.back(2))
                    pe.transpose(ps_x[n.u][:, 0:P], hn[n.u][:, :], ident).then_inc(s_t.sem, 1)

                def up(n):
                    s_hc.wait(pe, n)
                    for dst, lo, s_, free in ((ps_g, HID, s_g, s_gl), (ps_a, 0, s_a, s_ac)):
                        free.wait(pe, n.back(2))
                        for c, k in enumerate(HCH):
                            m = pe.matmul(dst[n.u][0:k, P * c:P * c + P], w1[:, lo + P * c:lo + P * c + k],
                                          hT[n.u][:, :], start=True, stop=True)
                        m.then_inc(s_.sem, 1)

                def down(n):
                    s_ac.wait(pe, n)
                    s_yc.wait(pe, n.back(2))
                    for c, k in enumerate(HCH):
                        k += c == 2
                        m = pe.matmul(ps_y[n.u][:, 0:D], act_[n.u][0:k, P * c:P * c + P], w2[0:k, D * c:D * c + D],
                                      start=(c == 0), stop=(c == 2))
                    m.then_inc(s_y.sem, 1)
                run_stages(pe, [(3, transpose_h), (6, down), (4, up)])

            @prog("scalar")
            def _(act):
                s_wl.wait_all(act)

                def copy_h(n):
                    s_t.wait(act, n)
                    s_g.wait(act, n.back(2))
                    s_a.wait(act, n.back(2))
                    act.activation(hT[n.u][:, :], ps_x[n.u][:, 0:P], ACT.Identity, bias=vec[:, 1:2], scale=vec[:, 0:1])\
                        .then_inc(s_hc.sem, 1)

                def gelu(n):
                    s_g.wait(act, n)
                    s_ac.wait(act, n.back(2))
                    for c, k in enumerate(HCH):
                        act.activation(gl[n.u][0:k, P * c:P * c + P], ps_g[n.u][0:k, P * c:P * c + P], ACT.Gelu,
                                       bias=vec[0:k, 5 + c:6 + c]).then_inc(s_gl.sem, 1)
                run_stages(act, [(3, copy_h), (4, gelu)])

            @prog("vector")
            def _(v):
                s_wl.wait_all(v)
                s_z.wait_all(v)

                def stats(n):
                    s_d[n.u].wait(v, n)
                    ln_stats(v, n)

                def gate(n):
                    s_gl.wait(v, n)
                    s_a.wait(v, n)
                    s_y.wait(v, n.back(2))
                    for c, k in enumerate(HCH):
                        at = slice(P * c, P * c + P)
                        v.scalar_tensor_tensor(out=act_[n.u][0:k, at], in0=ps_a[n.u][0:k, at], scalar=vec[0:k, 2 + c:3 + c],
                                               in1=gl[n.u][0:k, at], op0=ALU.add, op1=ALU.mult).then_inc(s_ac.sem, 1)

                def update(n):
                    s_y.wait(v, n)
                    dst = tok(y, n) if not l else yo[n.u][:, :]
                    v.tensor_tensor(dst, ps_y[n.u][:, 0:D], tok(y2, n), ALU.add).then_inc(s_yc.sem, 1)
                    if l:
                        s_yc.wait(v, n)
                        v.scalar_tensor_tensor(out=tok(x, n), in0=yo[n.u][:, :], scalar=tg[:, 2:3], in1=tok(x, n),
                                               op0=ALU.mult, op1=ALU.add).then_inc(s_up.sem, 1)
                run_stages(v, [(1, stats), (6, update), (5, gate), (2, lambda n: ln_norm(v, n, hn[n.u][:, :], s_t))])

            @prog("gpsimd")
            def _(g):
                g.memset(h[0][0:1, 64:D], 0.0).then_inc(s_z.sem, 1)
                for t in act_:
                    g.memset(t[64:P, 2 * P:3 * P], 1.0).then_inc(s_z.sem, 1)
                run_stages(g, [(1, lambda n: ln_rstd(g, n))])
            phase_end()

        def experts():
            psb, many, pbank = phase_begin("m")
            w1, w2, rw = psb("w1", CH * P), psb("w2", CH * D), psb("rw", E)
            h, hT, st = many("h", 2, D), many("hT", 2, D), many("st", 2, 16)
            rt = many("rt", 2, 64)
            ri = many("ri", 2, E, U32)
            up_ = many("up", 2, CH * P)
            yw = many("yw", 2, E * D)
            ys = many("ys", 2, D)
            ps_h = [pbank(f"ps_h{i}") for i in range(CH // 4)]
            ps_y = pbank("ps_y", 2)
            ps_x, ps_r = pbank("ps_x"), pbank("ps_r")
            wl = [(w1[:, :], a["L1_ffn_w1"]), (w2[:, :].rearrange("p (c d) -> p c d", d=D),
                                               a["L1_ffn_w2"].rearrange("(c p) d -> p c d", p=P)), (rw[:, :], a["router_wT"])]
            s_wl = sig("wl", 0, total=16 * len(wl))
            s_ln, ln_stats, ln_rstd, ln_norm = layernorm("ln", lambda n: tok(x, n), st, None)
            s_t, s_hc, s_r, s_p, s_y, s_up = (sig(i, 1) for i in ("t", "hc", "r", "p", "y", "up"))
            s_h, s_re, s_sq = (sig(i, CH // 4) for i in ("h", "re", "sq"))
            s_top = sig("top", 9)
            s_comb = sig("comb", 1)
            s_yw = sig("yw", 2)
            s_out = sig("out", 16)

            @prog("sync")
            def _(sp):
                for dst, src in wl:
                    sp.dma_start(dst, src).then_inc(s_wl.sem, 16)

                def store(n):
                    s_up.wait(sp, n)
                    dst = out.rearrange("b s d -> (b s) d")[bass.ds(n.at(P), P), :]
                    sp.dma_start(dst, tok(x, n)).then_inc(s_out.sem, 16)
                run_stages(sp, [(6, store)])

            @prog("tensor")
            def _(pe):
                s_wl.wait_all(pe)

                def transpose_h(n):
                    s_ln.wait(pe, n)
                    s_hc.wait(pe, n.back(1))
                    pe.transpose(ps_x[:, 0:P], h[n.u][:, :], ident).then_inc(s_t.sem, 1)

                def route(n):
                    s_hc.wait(pe, n)
                    s_p.wait(pe, n.back(1))
                    pe.matmul(ps_r[:, 0:E], hT[n.u][:, :], rw[:, :], start=True, stop=True).then_inc(s_r.sem, 1)

                def up(n):
                    for b in range(CH // 4):
                        s_re.wait(pe, n.back(1), b + 1)
                        for i in range(4):
                            c = 4 * b + i
                            m = pe.matmul(ps_h[b][:, P * i:P * i + P], w1[:, P * c:P * c + P], hT[n.u][:, :],
                                          start=True, stop=True)
                        m.then_inc(s_h.sem, 1)

                def down(n):
                    s_sq.wait(pe, n)
                    s_yw.wait(pe, n.back(1), 1)
                    c = 0
                    for e, w in enumerate(EW):
                        for i in range(w // P):
                            m = pe.matmul(ps_y[:, D * e:D * e + D], up_[n.u][:, P * c:P * c + P], w2[:, D * c:D * c + D],
                                          start=(i == 0), stop=(i == w // P - 1))
                            c += 1
                    m.then_inc(s_y.sem, 1)
                run_stages(pe, [(2, transpose_h), (4, down), (3, route), (3, up)])

            @prog("scalar")
            def _(act):
                def copy_h(n):
                    s_t.wait(act, n)
                    s_r.wait(act, n.back(2))
                    s_h.wait(act, n.back(2))
                    act.activation(hT[n.u][:, :], ps_x[:, 0:P], ACT.Copy).then_inc(s_hc.sem, 1)

                def probabilities(n):
                    s_r.wait(act, n)
                    s_top.wait(act, n.back(2))
                    act.activation(rt[n.u][:, 0:E], ps_r[:, 0:E], ACT.Sigmoid).then_inc(s_p.sem, 1)

                def relu(n):
                    for b in range(CH // 4):
                        s_h.wait(act, n, b + 1)
                        s_y.wait(act, n.back(2))
                        act.activation(up_[n.u][:, 512 * b:512 * b + 512], ps_h[b][:, :], ACT.Relu).then_inc(s_re.sem, 1)
                run_stages(act, [(2, copy_h), (3, probabilities), (3, relu)])

            @prog("vector")
            def _(v):
                def top2(n):
                    t, ti = rt[n.u], ri[n.u]
                    step = [0]

                    def do(i):
                        i.then_inc(s_top.sem, 1)
                        step[0] += 1
                        s_top.wait(v, n, step[0])
                        alone(v, "vector")
                    s_p.wait(v, n)
                    s_yw.wait(v, n.back(2), 1)
                    alone(v, "vector")
                    do(v.max(t[:, 8:16], t[:, 0:E]))
                    do(v.max_index(ti[:, :], t[:, 8:16], t[:, 0:E]))
                    do(v.tensor_copy(t[:, 16:18], ti[:, 0:2]))
                    do(v.tensor_tensor(t[:, 18:19], t[:, 8:9], t[:, 9:10], ALU.add))
                    do(v.tensor_scalar(t[:, 18:19], t[:, 18:19], 1e-20, None, ALU.add))
                    do(v.reciprocal(t[:, 19:20], t[:, 18:19]))
                    do(v.tensor_scalar(t[:, 20:22], t[:, 8:10], t[:, 19:20], None, ALU.mult))
                    do(v.tensor_scalar(t[:, 24:32], iota, t[:, 16:17], t[:, 20:21], ALU.is_equal, ALU.mult))
                    v.tensor_scalar(t[:, 32:40], iota, t[:, 17:18], t[:, 21:22], ALU.is_equal, ALU.mult)\
                        .then_inc(s_top.sem, 1)

                def square(n):
                    for b in range(CH // 4):
                        s_re.wait(v, n, b + 1)
                        r = up_[n.u][:, 512 * b:512 * b + 512]
                        v.tensor_tensor(r, r, r, ALU.mult).then_inc(s_sq.sem, 1)

                def combine(n):
                    t = rt[n.u]
                    s_top.wait(v, n)
                    v.tensor_tensor(t[:, 40:48], t[:, 24:32], t[:, 32:40], ALU.add).then_inc(s_comb.sem, 1)
                    s_comb.wait(v, n)
                    s_y.wait(v, n)
                    v.tensor_tensor(yw[n.u][:, :].rearrange("p (e d) -> p e d", d=D),
                                    ps_y[:, :].rearrange("p (e d) -> p e d", d=D),
                                    t[:, 40:48].unsqueeze(2).broadcast_to([P, E, D]), ALU.mult).then_inc(s_yw.sem, 1)
                    s_yw.wait(v, n, 1)
                    v.reduce_sum(ys[n.u][:, :], yw[n.u][:, :].rearrange("p (e d) -> p d e", d=D), axis=AX_X)\
                        .then_inc(s_yw.sem, 1)
                    s_yw.wait(v, n)
                    v.scalar_tensor_tensor(out=tok(x, n), in0=ys[n.u][:, :], scalar=tg[:, 3:4], in1=tok(x, n),
                                           op0=ALU.mult, op1=ALU.add).then_inc(s_up.sem, 1)
                run_stages(v, [(0, lambda n: ln_stats(v, n)), (1, lambda n: ln_norm(v, n, h[n.u][:, :], s_t)), (3, top2),
                               (3, square), (4, combine)])

            @prog("gpsimd")
            def _(g):
                run_stages(g, [(0, lambda n: ln_rstd(g, n))])
            phase_end()

        cross_attention(0)
        for l in range(2):
            local_attention(l)
            mlp(l)
        cross_attention(1)
        experts()

        block = ctx.enter_context(nc.Block())
        starts = {"sync": block.sync, "scalar": block.scalar, "vector": block.vector, "gpsimd": block.gpsimd,
                  "tensor": block.tensor}
        for name, steps in progs.items():
            @starts[name]
            def _(eng, steps=steps):
                for f in steps:
                    f(eng)


_AS_IS = ["x", "mask_BxS2_if1", "mask_BxS2_ik0", "g_xattn", "g_ffn", "L0_ffn_wqkv", "L0_ffn_q_scale", "L0_ffn_k_scale",
          "L0_ffn_wo", "L0_ffn_ln_g", "L0_ffn_ln_b", "L0_ffn_w1", "L0_ffn_b1", "L0_ffn_w2", "L0_ffn_b2", "L1_xattn_bq",
          "L1_xattn_bk", "L1_xattn_bv", "L1_xattn_bfc", "L1_ffn_w1", "L1_ffn_w2"]
_TRANSPOSED = {"L0_xattn_WqT": "L0_xattn_Wq", "L0_xattn_WkT": "L0_xattn_Wk", "L0_xattn_WvT": "L0_xattn_Wv",
               "L0_xattn_WoT": "L0_xattn_Wo", "L1_xattn_WqT": "L1_xattn_Wq", "L1_xattn_WkT": "L1_xattn_Wk",
               "L1_xattn_WvT": "L1_xattn_Wv", "L1_xattn_WfcT": "L1_xattn_Wfc", "router_wT": "L1_ffn_router_w"}


def kernel(**inputs):
    import concourse.bacc as _bacc
    from concourse.bass_utils import run_bass_kernel_spmd as _run

    nc = _bacc.Bacc("TRN2", target_bir_lowering=False, num_devices=1)
    arrays = {n: np.ascontiguousarray(inputs[n]) for n in _AS_IS}
    arrays.update({n: np.ascontiguousarray(np.asarray(inputs[m]).T) for n, m in _TRANSPOSED.items()})
    arrays["ctxT"] = np.ascontiguousarray(np.asarray(inputs["ctx_1024"]).reshape(B * SC, D).T)
    arrays["mask0T"] = np.ascontiguousarray(np.asarray(inputs["mask_BxS2_if1"]).T)
    arrays["c32"], arrays["c16"] = constants()
    sent, args = {}, {}
    for name, v in arrays.items():
        key = f"in_{name}_dram"
        sent[key] = v
        args[name] = nc.dram_tensor(key, v.shape, mybir.dt.from_np(v.dtype), kind="ExternalInput").ap()
    out = nc.dram_tensor("out_0_dram", (B, S, D), F32, kind="ExternalOutput").ap()
    build(nc, args, out)
    r = _run(nc, [sent], core_ids=[0])
    return r.results[0]["out_0_dram"]
```

```python
from contextlib import ExitStack

import numpy as np

import concourse.bass as bass
from concourse import mybir

F32 = mybir.dt.float32
BF16 = mybir.dt.bfloat16
I32 = mybir.dt.int32
U32 = mybir.dt.uint32
ALU = mybir.AluOpType
ACT = mybir.ActivationFunctionType
AX_X = mybir.AxisListType.X

P = 128
D = 128
B, S, SC = 16, 256, 64
T = B * S // P
UPS = S // P
XH, XD = 16, 8
XP = XH // 2
LH, LD, WIN = 8, 64, 64
LP = LH // 2
INNER = LH * LD
QK_SCALE = 8
HID = 341
HCH = [128, 128, 85]
EW = [128] * 4 + [256] * 4
E = len(EW)
CH = sum(EW) // P
UNROLL = 4
AWAY = -2.0e38
PADDED = -1.0e38


def position_tables():
    f = np.float32
    half = np.arange(0, LD, 2, dtype=f)
    inv = f(1.0) / np.power(f(10000.0), half / f(LD))
    t = np.arange(S, dtype=f)
    fr = t[:, None] * inv[None, :]
    fr = np.concatenate([fr, fr], -1)
    base = (half + f(0.4 * LD)) / f(1.4 * LD)
    power = (t - f(S // 2)) / f(WIN // 2)
    sc = np.power(base[None, :], power[:, None])
    sc = np.concatenate([sc, sc], -1).astype(f)
    cos, sin = np.cos(fr).astype(f), np.sin(fr).astype(f)
    sgn = np.concatenate([-np.ones(LD // 2, f), np.ones(LD // 2, f)])
    c = np.stack([cos * sc * f(QK_SCALE), cos / sc], 1)
    s = np.stack([sin * sc * sgn * f(QK_SCALE), sin / sc * sgn], 1)
    lay = lambda a: a.reshape(UPS, P, 2, LD).transpose(1, 0, 2, 3).reshape(P, -1).astype(f)
    return lay(c), lay(s)


def constants():
    f = np.float32
    p = np.arange(P)
    cos, sin = position_tables()
    own = (p[:, None] // XD == np.arange(XH)[None, :]).astype(f)
    half = (p[:, None] // SC == np.arange(2)[None, :]).astype(f)
    iota = np.broadcast_to(np.arange(E, dtype=f), (P, E))
    c32 = np.concatenate([np.eye(P, dtype=f), own, half, iota, cos, sin], 1)
    q = p % WIN
    m = np.zeros((P, UPS, 2, 2, WIN), f)
    k = np.arange(WIN)
    for u in range(UPS):
        for x in range(2):
            w = 2 * u + x
            for slot, kw in enumerate(local_keys(w)):
                off = (kw - w) * WIN if kw is not None else None
                rel = None if off is None else k[None, :] + off - q[:, None]
                bad = np.ones((P, WIN), bool) if rel is None else (rel > 0) | (rel < -WIN)
                m[:, u, x, slot] = np.where(bad, AWAY, 0)
    causal = np.where(k[None, :] > p[:, None], AWAY, 0).astype(f)
    c16 = np.concatenate([np.eye(P, dtype=f), np.ones((P, P), f), causal, m.reshape(P, -1)], 1)
    return np.ascontiguousarray(c32), np.ascontiguousarray(c16.astype(f))


def local_keys(w):
    return (w, w - 1 if w else None) if w % 2 == 0 else (w - 1, w)


class Unit:

    def __init__(self, j, c):
        self.j, self.c = j, c

    def at(self, per, add=0):
        return self.j * (UNROLL * per) + (self.c * per + add)

    def group(self, every, per, add=0):
        return self.j * (UNROLL // every * per) + (self.c // every * per + add)

    def half(self, per, add=0):
        return self.group(2, per, add)

    def back(self, k):
        return Unit(self.j, self.c - k)

    @property
    def u(self):
        return self.c % 2

    @property
    def bp(self):
        return self.c // 2 % 2

    @property
    def ring(self):
        return self.c % UNROLL


class Sig:

    def __init__(self, sem, base, per, units, every=1, total=None):
        self.sem, self.base, self.per, self.units, self.every = sem, base, per, units, every
        self.total = per * (units // every) if total is None else total

    def wait(self, eng, unit, count=None):
        if isinstance(unit.j, int):
            n = unit.at(1)
            if n < 0:
                return
            unit = Unit(0, min(n, self.units - 1))
        n = self.per if count is None else count
        eng.wait_ge(self.sem, unit.group(self.every, self.per, self.base + n))

    def wait_count(self, eng, n):
        eng.wait_ge(self.sem, self.base + n)

    def wait_all(self, eng):
        self.wait_count(eng, self.total)


def run_stages(eng, stages, units=T):
    lags = [lag for lag, _ in stages]
    first = -(-(max(lags) + 4) // UNROLL) * UNROLL

    def step(s):
        for lag, stage in stages:
            if 0 <= s - lag < units:
                stage(Unit(0, s - lag))

    for s in range(first):
        step(s)
    with eng.Fori(first // UNROLL, units // UNROLL, 1) as j:
        for c in range(UNROLL):
            for lag, stage in stages:
                stage(Unit(j, c - lag))
    for s in range(units, units + max(lags)):
        step(s)


def build(nc, a, out):
    with ExitStack() as ctx:
        def sb(name, cols, dt=F32, rows=P):
            return ctx.enter_context(nc.sbuf_tensor(name, [rows, cols], dt))

        def bank(name, n=1):
            return ctx.enter_context(nc.psum_tensor(name, [P, 512 * n], F32))

        def sem(name):
            return ctx.enter_context(nc.semaphore(name))

        x = sb("x", T * D)
        y = sb("y", T * D)
        y2 = sb("y2", T * D)
        c32 = sb("c32", a["c32"].shape[1])
        c16 = sb("c16", a["c16"].shape[1], BF16)
        o = 0
        ident = c32[:, 0:P]
        own = c32[:, P:P + XH]
        halves = c32[:, P + XH:P + XH + 2]
        iota = c32[:, P + XH + 2:P + XH + 2 + E]
        o = P + XH + 2 + E
        nt = UPS * 2 * LD
        cos_t, sin_t = c32[:, o:o + nt], c32[:, o + nt:o + 2 * nt]
        ident16 = c16[:, 0:P]
        ones16 = c16[0:1, P:2 * P]
        causal = c16[0:WIN, 2 * P:2 * P + SC]
        lmask = c16[:, 2 * P + SC:].rearrange("p (u n) -> p u n", u=UPS)
        small = sb("small", 64)
        neg_half, one = small[:, 0:1], small[:, 1:2]
        tg = small[:, 2:6]
        graw = small[:, 6:10]
        bq, bk = small[:, 10:11], small[:, 11:12]
        wq = [sb(f"wq{l}", D) for l in range(2)]
        wk = [sb(f"wk{l}", D) for l in range(2)]
        wv = [sb(f"wv{l}", D) for l in range(2)]
        wo = [sb(f"wo{l}", D) for l in range(2)]
        bv = sb("bv", D)
        bfc = sb("bfc", D, F32, 1)
        ones_row = sb("ones_row", P, F32, 1)

        progs = {e: [] for e in ("sync", "scalar", "vector", "gpsimd", "tensor")}
        phase = {}
        idle = []

        def sig(name, per, units=T, every=1, total=None):
            number, base = idle.pop(0) if idle else (sem(f"sem_{phase['name']}{name}"), 0)
            s = Sig(number, base, per, units, every, total)
            phase["sigs"].append(s)
            return s

        def prog(engine):
            return lambda f: progs[engine].append(f)

        def phase_begin(name):
            mem = ExitStack()
            phase.update(name=name + "_", sigs=[], mem=mem)

            def psb(label, cols, dt=F32, rows=P):
                return mem.enter_context(nc.sbuf_tensor(f"{name}_{label}", [rows, cols], dt))

            def many(label, n, cols, dt=F32):
                return [psb(f"{label}{i}", cols, dt) for i in range(n)]

            def pbank(label, n=1):
                return mem.enter_context(nc.psum_tensor(f"{name}_{label}", [P, 512 * n], F32))
            return psb, many, pbank

        def phase_end():
            done = list(phase["sigs"])
            idle.extend((s.sem, s.base + s.total) for s in done)
            phase["mem"].close()
            for e in progs:
                progs[e].append(lambda eng: [s.wait_all(eng) for s in done])

        tok = lambda t, n: t[:, bass.ds(n.at(D), D)]

        boot, _, _ = phase_begin("boot")
        c16f = boot("c16f", a["c16"].shape[1])
        graws = [a["g_xattn"], a["g_ffn"]]
        col = lambda v: v.rearrange("(p o) -> p o", o=1)
        loads = [
            (c32[:, :], a["c32"]), (c16f[:, :], a["c16"]),
            (x[:, :].rearrange("p (t d) -> p t d", d=D), a["x"].rearrange("b (u p) d -> p (b u) d", p=P)),
            (graw[:, 0:2], graws[0].partition_broadcast(P)), (graw[:, 2:4], graws[1].partition_broadcast(P)),
            (bq, col(a["L1_xattn_bq"])), (bk, col(a["L1_xattn_bk"])), (bv[:, :], a["L1_xattn_bv"].partition_broadcast(P)),
        ]
        loads.append((bfc[:, :], a["L1_xattn_bfc"].rearrange("(o d) -> o d", o=1)))
        for l, names in enumerate((("Wq", "Wk", "Wv", "Wo"), ("Wq", "Wk", "Wv", "Wfc"))):
            loads += [(w[l][:, :], a[f"L{l}_xattn_{name}T"]) for w, name in zip((wq, wk, wv, wo), names)]
        s_load = sig("load", 0, total=16 * len(loads))
        s_clear = sig("clear", 0, total=3)
        s_tanh = sig("tanh", 0, total=1)
        s_c16 = sig("c16", 0, total=1)

        @prog("vector")
        def _(v):
            s_load.wait_all(v)
            v.tensor_copy(c16[:, :], c16f[:, :]).then_inc(s_c16.sem, 1)

        @prog("gpsimd")
        def _(g):
            for t, v_ in ((ones_row[:, :], 1.0), (neg_half, -0.5), (one, 1.0)):
                g.memset(t, v_).then_inc(s_clear.sem, 1)

        @prog("sync")
        def _(sp):
            for dst, src in loads:
                sp.dma_start(dst, src).then_inc(s_load.sem, 16)

        @prog("scalar")
        def _(act):
            s_load.wait_all(act)
            act.activation(tg, graw, ACT.Tanh).then_inc(s_tanh.sem, 1)
        phase_end()

        s_spare = {e: sem(f"spare_{e}") for e in ("vector", "gpsimd")}

        def alone(eng, name):
            eng.sem_inc(s_spare[name], 1)

        def layernorm(name, src, st, s_ready):
            s_st = sig(name + "_stats", 2)
            s_nm = sig(name + "_norm", 1)
            s_rs = sig(name + "_rstd", 2)

            def stats(v, n):
                t = st[n.u]
                if s_ready:
                    s_ready.wait(v, n)
                s_nm.wait(v, n.back(2))
                alone(v, "vector")
                v.bn_stats(t[:, 0:6], src(n)).then_inc(s_st.sem, 1)
                s_st.wait(v, n, 1)
                alone(v, "vector")
                v.bn_aggr(t[:, 6:8], t[:, 0:6]).then_inc(s_st.sem, 1)

            def rstd(g, n):
                t = st[n.u]
                s_st.wait(g, n)
                s_nm.wait(g, n.back(2))
                alone(g, "gpsimd")
                g.tensor_scalar(t[:, 8:9], t[:, 7:8], 1e-5, None, ALU.add).then_inc(s_rs.sem, 1)
                s_rs.wait(g, n, 1)
                g.tensor_tensor(t[:, 9:10], t[:, 8:9], neg_half, ALU.pow).then_inc(s_rs.sem, 1)

            def norm(v, n, dst, free=None):
                t = st[n.u]
                s_rs.wait(v, n)
                if free:
                    free.wait(v, n.back(2))
                v.tensor_scalar(dst, src(n), t[:, 6:7], t[:, 9:10], ALU.subtract, ALU.mult).then_inc(s_nm.sem, 1)
            return s_nm, stats, rstd, norm

        def cross_attention(l):
            res = ExitStack()
            rsb = lambda name, cols, dt=F32, rows=P: res.enter_context(nc.sbuf_tensor(f"x{l}_{name}", [rows, cols], dt))
            kT = rsb("kT", B * SC)
            vall = rsb("vall", B * D)
            padrow = rsb("padrow", B * SC, BF16, 1)
            if not l:
                maskc = rsb("maskc", B)
                maskci = rsb("maskci", B, I32)

            psb, many, pbank = phase_begin(f"xc{l}")
            ctxT = psb("ctxT", B * SC)
            maski, maskf = psb("maski", B * SC, I32), psb("maskf", B * SC)
            ctx2 = many("ctx2", 2, P)
            ps_k, ps_v = pbank("ps_k", 2), [pbank(f"ps_v{i}") for i in range(2)]
            s_c = sig("c", 0, total=32 if l else 64)
            s_mc = sig("mc", 0, total=0 if l else 2)
            s_k = sig("k", 0, total=1)
            s_ks = sig("ks", 0, total=1)
            s_md = sig("md", 0, total=4 if l else 2)
            s_cd = sig("cd", 2, B)
            s_vp = sig("vp", 1, B)
            s_ve = sig("ve", 1, B)
            mask = a[("mask_BxS2_if1", "mask_BxS2_ik0")[l]].rearrange("b s -> (b s)")

            @prog("sync")
            def _(sp):
                sp.dma_start(ctxT[:, :], a["ctxT"]).then_inc(s_c.sem, 16)
                sp.dma_start(maski[:, :], mask.partition_broadcast(P)).then_inc(s_c.sem, 16)
                if not l:
                    for i in range(2):
                        sp.dma_start(maskci[SC * i:SC * i + SC, :], a["mask0T"]).then_inc(s_c.sem, 16)

            @prog("tensor")
            def _(pe):
                s_c.wait_all(pe)
                for i in range(2):
                    m = pe.matmul(ps_k[:, 512 * i:512 * i + 512], wk[l][:, :], ctxT[:, 512 * i:512 * i + 512],
                                  start=True, stop=True)
                m.then_inc(s_k.sem, 1)

                def values(n):
                    s_cd.wait(pe, n)
                    s_ve.wait(pe, n.back(2))
                    pe.matmul(ps_v[n.u][:, 0:D], ctx2[n.u][:, :], wv[l][:, :], start=True, stop=True)\
                        .then_inc(s_vp.sem, 1)
                run_stages(pe, [(0, values)], B)

            @prog("scalar")
            def _(act):
                s_k.wait_all(act)
                act.activation(kT[:, :], ps_k[:, :], ACT.Identity, bias=bk if l else 0.0).then_inc(s_ks.sem, 1)

            @prog("vector")
            def _(v):
                s_c.wait_all(v)
                v.tensor_copy(maskf[:, :], maski[:, :]).then_inc(s_md.sem, 1)
                s_md.wait_count(v, 1)
                v.tensor_scalar(padrow[:, :], maskf[0:1, :], 0.0, -1e10 * XD ** 0.5 if l else PADDED,
                                ALU.is_equal, ALU.mult).then_inc(s_md.sem, 1)
                if l:
                    s_md.wait_count(v, 2)
                    v.tensor_scalar(maskf[:, :], maskf[:, :], 0.0, None, ALU.not_equal).then_inc(s_md.sem, 1)
                    s_md.wait_count(v, 3)
                    s_ks.wait_all(v)
                    v.tensor_tensor(kT[:, :], kT[:, :], maskf[:, :], ALU.mult).then_inc(s_md.sem, 1)

                if not l:
                    v.tensor_copy(maskc[:, :], maskci[:, :]).then_inc(s_mc.sem, 1)
                    s_mc.wait_count(v, 1)
                    v.tensor_scalar(maskc[:, :], maskc[:, :], 0.0, None, ALU.not_equal).then_inc(s_mc.sem, 1)
                    s_mc.wait_all(v)

                def values(n):
                    s_vp.wait(v, n)
                    if l:
                        i = v.tensor_tensor(tok(vall, n), ps_v[n.u][:, 0:D], bv[:, :], ALU.add)
                    else:
                        i = v.tensor_tensor(tok(vall, n), ps_v[n.u][:, 0:D],
                                            maskc[:, bass.ds(n.at(1), 1)].broadcast_to([P, D]), ALU.mult)
                    i.then_inc(s_ve.sem, 1)
                run_stages(v, [(0, values)], B)

            @prog("gpsimd")
            def _(g):
                s_c.wait_all(g)

                def twice(n):
                    s_vp.wait(g, n.back(2))
                    for i in range(2):
                        g.tensor_copy(ctx2[n.u][:, SC * i:SC * i + SC], ctxT[:, bass.ds(n.at(SC), SC)])\
                            .then_inc(s_cd.sem, 1)
                run_stages(g, [(0, twice)], B)
            phase_end()

            psb, many, pbank = phase_begin(f"x{l}")
            st, st2, stat = many("st", 2, 16), many("st2", 2, 16), many("stat", 2, 2 * XH)
            h, hT, qT = many("h", 2, D), many("hT", 2, D), many("qT", 2, D)
            e_ = many("e", 2, XH * SC)
            eT = many("eT", 2, XH * SC)
            od = many("od", 2, 2 * P)
            on, onT = many("on", 2, D), many("onT", 2, D)
            kblk, vpair = many("kblk", 2, XH * SC), many("vpair", 2, XP * 32)
            ps_s, ps_t = pbank("ps_s", 2), pbank("ps_t", 2)
            ps_x, ps_q, ps_o, ps_w = (pbank(f"ps{i}") for i in range(4))
            s_z = sig("z", 0, total=4 if l else 2)
            s_h, s_hc, s_q, s_qc = (sig(i, 1) for i in ("h", "hc", "q", "qc"))
            s_kb = sig("kb", 1, T, 2)
            s_vb = sig("vb", 2 if l else 3, T, 2)
            s_s, s_e, s_t, s_tc, s_o, s_oc, s_w, s_up = (sig(i, 1) for i in ("s", "e", "t", "tc", "o", "oc", "w", "up"))
            s_sm = sig("sm", 2)
            s_ot = sig("ot", 1)
            s_on = sig("on", 2)
            s_nt, s_nc = sig("nt", 1), sig("nc", 1)
            s_ln, ln_stats, ln_rstd, ln_norm = layernorm("ln", lambda n: tok(x, n), st, None)
            if not l:
                _, y_stats, y_rstd, y_norm = layernorm("ly", lambda n: tok(x, n), st2, s_up)

            @prog("tensor")
            def _(pe):
                def transpose_h(n):
                    s_ln.wait(pe, n)
                    s_hc.wait(pe, n.back(1))
                    pe.transpose(ps_x[:, 0:P], h[n.u][:, :], ident).then_inc(s_h.sem, 1)

                def project_q(n):
                    s_hc.wait(pe, n)
                    s_qc.wait(pe, n.back(1))
                    pe.matmul(ps_q[:, 0:P], wq[l][:, :], hT[n.u][:, :], start=True, stop=True).then_inc(s_q.sem, 1)

                def scores(n):
                    s_qc.wait(pe, n)
                    s_kb.wait(pe, n)
                    s_sm.wait(pe, n.back(1))
                    for i in range(2):
                        dst = ps_s[:, 512 * i:512 * i + 512]
                        pad = padrow[0:1, bass.ds(n.half(SC), SC)].unsqueeze(1).broadcast_to([1, XH // 2, SC])
                        pe.matmul(dst, qT[n.u][:, :], kblk[n.bp][:, 512 * i:512 * i + 512], start=True, stop=False)
                        if not l and n.u == 0:
                            pe.matmul(dst, ident16[0:SC, :], causal.unsqueeze(1).broadcast_to([SC, XH // 2, SC]),
                                      start=False, stop=False)
                        m = pe.matmul(dst, ones16, pad, start=False, stop=True)
                    m.then_inc(s_s.sem, 1)

                def transpose_e(n):
                    s_e.wait(pe, n)
                    s_tc.wait(pe, n.back(1))
                    for i in range(XP):
                        m = pe.transpose(ps_t[:, P * i:P * i + P], e_[n.u][:, P * i:P * i + P], ident)
                    m.then_inc(s_t.sem, 1)

                def outputs(n):
                    s_tc.wait(pe, n)
                    s_vb.wait(pe, n)
                    s_on.wait(pe, n.back(1))
                    for pair in range(XP):
                        r, j = divmod(pair, 4)
                        m = pe.matmul(ps_o[32 * j:32 * j + 32, P * r:P * r + P],
                                      vpair[n.bp][:, 32 * pair:32 * pair + 32],
                                      eT[n.u][:, P * pair:P * pair + P], start=True, stop=True)
                    m.then_inc(s_o.sem, 1)

                def transpose_o(n):
                    s_oc.wait(pe, n)
                    for r in range(2):
                        m = pe.transpose(ps_o[:, 256 + P * r:256 + P * r + P], od[n.u][:, P * r:P * r + P], ident)
                    m.then_inc(s_ot.sem, 1)

                def transpose_on(n):
                    s_on.wait(pe, n)
                    s_up.wait(pe, n.back(1))
                    pe.transpose(ps_w[:, P:2 * P], on[n.u][:, :], ident).then_inc(s_nt.sem, 1)

                def project_o(n):
                    s_nc.wait(pe, n)
                    m = pe.matmul(ps_w[:, 0:D], onT[n.u][:, :], wo[l][:, :], start=True, stop=not l)
                    if l:
                        m = pe.matmul(ps_w[:, 0:D], ones_row[:, :], bfc[:, :], start=False, stop=True)
                    m.then_inc(s_w.sem, 1)
                run_stages(pe, [(9, project_o), (2, transpose_h), (3, project_q), (7, transpose_o), (4, scores),
                                (8, transpose_on), (5, transpose_e), (6, outputs)])

            @prog("scalar")
            def _(act):
                def copy_h(n):
                    s_h.wait(act, n)
                    s_q.wait(act, n.back(2))
                    act.activation(hT[n.u][:, :], ps_x[:, 0:P], ACT.Copy).then_inc(s_hc.sem, 1)

                def copy_q(n):
                    s_q.wait(act, n)
                    s_s.wait(act, n.back(2))
                    act.activation(qT[n.u][:, :], ps_q[:, 0:P], ACT.Identity, bias=bq if l else 0.0)\
                        .then_inc(s_qc.sem, 1)

                def exps(n):
                    s_sm.wait(act, n)
                    act.activation(e_[n.u][:, :], e_[n.u][:, :], ACT.Exp, scale=XD ** -0.5).then_inc(s_e.sem, 1)

                def copy_e(n):
                    s_t.wait(act, n)
                    s_o.wait(act, n.back(2))
                    act.activation(eT[n.u][:, :], ps_t[:, :], ACT.Copy).then_inc(s_tc.sem, 1)

                def copy_o(n):
                    s_o.wait(act, n)
                    s_ot.wait(act, n.back(2))
                    act.activation(od[n.u][:, :], ps_o[:, 0:2 * P], ACT.Copy).then_inc(s_oc.sem, 1)

                def copy_on(n):
                    s_nt.wait(act, n)
                    s_w.wait(act, n.back(2))
                    act.activation(onT[n.u][:, :], ps_w[:, P:2 * P], ACT.Copy).then_inc(s_nc.sem, 1)
                run_stages(act, [(5, exps), (2, copy_h), (3, copy_q), (8, copy_on), (5, copy_e), (6, copy_o)])

            @prog("vector")
            def _(v):
                def softmax(n):
                    s_s.wait(v, n)
                    sc = ps_s[:, :].rearrange("p (h k) -> p h k", k=SC)
                    v.tensor_reduce(stat[n.u][:, 0:XH], sc, AX_X, ALU.max, negate=True).then_inc(s_sm.sem, 1)
                    s_sm.wait(v, n, 1)
                    s_t.wait(v, n.back(2))
                    v.tensor_tensor(e_[n.u][:, :].rearrange("p (h k) -> p h k", k=SC), sc,
                                    stat[n.u][:, 0:XH].unsqueeze(2).broadcast_to([P, XH, SC]), ALU.add)\
                        .then_inc(s_sm.sem, 1)

                def update(n):
                    s_w.wait(v, n)
                    v.scalar_tensor_tensor(out=tok(x, n), in0=ps_w[:, 0:D], scalar=tg[:, l:l + 1], in1=tok(x, n),
                                           op0=ALU.mult, op1=ALU.add).then_inc(s_up.sem, 1)

                def divide(n):
                    s_ot.wait(v, n)
                    s_nt.wait(v, n.back(2))
                    o4 = ps_o[:, 256:512].rearrange("p (r c) -> p r c", c=32)
                    inv = stat[n.u][:, XH:2 * XH].rearrange("p (r e) -> p r e", e=2)
                    v.reciprocal(inv, o4[:, :, 16:18]).then_inc(s_on.sem, 1)
                    s_on.wait(v, n, 1)
                    v.tensor_tensor(on[n.u][:, :].rearrange("p (r e d) -> p r e d", e=2, d=XD),
                                    o4[:, :, 0:16].rearrange("p r (e d) -> p r e d", e=2),
                                    inv.unsqueeze(3).broadcast_to([P, XP, 2, XD]), ALU.mult).then_inc(s_on.sem, 1)
                stages = [(9, update), (7, divide), (0, lambda n: ln_stats(v, n)),
                          (1, lambda n: ln_norm(v, n, h[n.u][:, :], s_h)), (4, softmax)]
                if not l:
                    stages = stages[:-1] + [(11, lambda n: y_norm(v, n, tok(y, n))), (10, lambda n: y_stats(v, n)), stages[-1]]
                run_stages(v, stages)

            @prog("gpsimd")
            def _(g):
                for t in vpair:
                    g.memset(t[:, :], 0.0).then_inc(s_z.sem, 1)
                s_z.wait_count(g, 2)
                sum_cols = lambda t: t[:, :].rearrange("p (r c) -> p r c", c=32)[:, :, 16:18]
                if l:
                    for t in vpair:
                        g.tensor_copy(sum_cols(t), halves.unsqueeze(1).broadcast_to([P, XP, 2])).then_inc(s_z.sem, 1)
                    s_z.wait_all(g)

                def key_blocks(n):
                    if n.u:
                        return
                    s_s.wait(g, n.back(3))
                    g.tensor_tensor(kblk[n.bp][:, :].rearrange("p (h k) -> p h k", k=SC),
                                    kT[:, bass.ds(n.half(SC), SC)].unsqueeze(1).broadcast_to([P, XH, SC]),
                                    own.unsqueeze(2).broadcast_to([P, XH, SC]), ALU.mult).then_inc(s_kb.sem, 1)

                def value_blocks(n):
                    if n.u:
                        return
                    s_o.wait(g, n.back(3))
                    s_kb.wait(g, n)
                    for i in range(2):
                        if i:
                            s_vb.wait(g, n, i)
                        src = vall[SC * i:SC * i + SC, bass.ds(n.half(D), D)]\
                            .rearrange("p (r e d) -> p r e d", e=2, d=XD)[:, :, i, :]
                        dst = vpair[n.bp][SC * i:SC * i + SC, :].rearrange("p (r c) -> p r c", c=32)
                        g.tensor_copy(dst[:, :, XD * i:XD * i + XD], src).then_inc(s_vb.sem, 1)
                    s_vb.wait(g, n, 2)
                    if not l:
                        mc = maskc[:, bass.ds(n.half(1), 1)].unsqueeze(2).broadcast_to([P, XP, 2])
                        g.tensor_tensor(sum_cols(vpair[n.bp]), halves.unsqueeze(1).broadcast_to([P, XP, 2]), mc,
                                        ALU.mult).then_inc(s_vb.sem, 1)

                stages = [(0, lambda n: ln_rstd(g, n)), (2, key_blocks), (4, value_blocks)]
                if not l:
                    stages = [(10, lambda n: y_rstd(g, n))] + stages
                run_stages(g, stages)
            phase_end()
            res.close()

        def shift(sp, h, s_d, s_free, src):
            def stage(n):
                s_free.wait(sp, n.back(UNROLL))
                t, s = h[n.ring], s_d[n.ring].sem
                sp.dma_start(t[:, 0:64], src[:, bass.ds(n.at(D), 64)]).then_inc(s, 16)
                sp.dma_start(t[1:P, 64:D], src[0:P - 1, bass.ds(n.at(D, 64), 64)]).then_inc(s, 16)
                if n.u:
                    sp.dma_start(t[0:1, 64:D], src[P - 1:P, bass.ds(n.at(D, 64 - D), 64)]).then_inc(s, 16)
            return stage

        def local_attention(l):
            psb, many, pbank = phase_begin(f"a{l}")
            wqkv, lwo = psb("wqkv", 3 * INNER), psb("wo", LP * D)
            scl = psb("scl", 4 * LD)
            rtab = psb("rtab", 2 * nt)
            h, hT = many("h", UNROLL, D), many("hT", UNROLL, D)
            sq = many("sq", 1, 2 * INNER)
            rot, rot2 = many("rot", 2, 2 * INNER), many("rot2", 1, 2 * INNER)
            stat = many("stat", 2, 64)
            qbd = many("qbd", 2, LP * 2 * P)
            kTr = many("kTr", 2, LP * S)
            vt, vx = many("vt", UNROLL, INNER), many("vx", 2, INNER)
            e_, eT = many("e", 2, LP * 2 * P), many("eT", 2, LP * 2 * P)
            oT = many("oT", 2, INNER)
            ps_qk, ps_s, ps_t = pbank("ps_qk", 2), pbank("ps_s", 2), pbank("ps_t", 2)
            ps_a, ps_b = pbank("ps_a"), pbank("ps_b")
            wl = [(wqkv[:, :], a["L0_ffn_wqkv"][l]),
                  (lwo[:, :].rearrange("p (c d) -> p c d", d=D), a["L0_ffn_wo"][l].rearrange("(c p) d -> p c d", p=P))]
            for i, name in enumerate(("L0_ffn_q_scale", "L0_ffn_k_scale")):
                v_ = a[name][l]
                for lo, src in ((LD * i, v_), (2 * LD + LD * i, v_[LD // 2:LD]), (2 * LD + LD * i + LD // 2, v_[0:LD // 2])):
                    wl.append((scl[:, lo:lo + src.shape[0]], src.partition_broadcast(P)))
            s_wl = sig("wl", 0, total=16 * len(wl))
            s_tab = sig("tab", 0, total=2 * UPS)
            s_z = sig("z", 0, total=4)
            s_d = [sig(f"d{i}", 48 if i % 2 else 32, T, UNROLL) for i in range(UNROLL)]
            s_h, s_hc, s_vc, s_t, s_kc, s_s, s_en, s_et, s_o, s_oc, s_y, s_yc = (
                sig(i, 1) for i in ("h", "hc", "vc", "t", "kc", "s", "en", "et", "o", "oc", "y", "yc"))
            s_qk, s_v = sig("qk", 1), sig("v", 1)
            s_vx = [sig(f"vx{u}", 1, T, 2) for u in range(2)]
            s_sq = sig("sq", 2)
            s_r = sig("r", 7)
            s_n = sig("n", 4)
            s_nq = sig("nq", 1)
            s_qc = sig("qc", 2)
            s_mx = sig("mx", 2)
            s_e = sig("e", 2 * LP)
            s_ecv, s_eca = sig("ecv", 1), sig("eca", 1)

            @prog("sync")
            def _(sp):
                for dst, src in wl:
                    sp.dma_start(dst, src).then_inc(s_wl.sem, 16)
                s_z.wait_all(sp)
                run_stages(sp, [(0, shift(sp, h, s_d, s_h, y))])

            @prog("tensor")
            def _(pe):
                s_wl.wait_all(pe)

                def transpose_h(n):
                    s_d[n.ring].wait(pe, n)
                    s_hc.wait(pe, n.back(1))
                    s_yc.wait(pe, n.back(7))
                    pe.transpose(ps_a[:, 0:P], h[n.ring][:, :], ident).then_inc(s_h.sem, 1)

                def qk(n):
                    s_hc.wait(pe, n)
                    s_r.wait(pe, n.back(1))
                    s_sq.wait(pe, n.back(1))
                    for i in range(2):
                        m = pe.matmul(ps_qk[:, 512 * i:512 * i + 512], hT[n.ring][:, :], wqkv[:, 512 * i:512 * i + 512],
                                      start=True, stop=True)
                    m.then_inc(s_qk.sem, 1)

                def values(n):
                    s_vc.wait(pe, n.back(1))
                    s_oc.wait(pe, n.back(3))
                    pe.matmul(ps_b[:, :], hT[n.ring][:, :], wqkv[:, 1024:1536], start=True, stop=True)\
                        .then_inc(s_v.sem, 1)

                def transpose_qk(n):
                    s_n.wait(pe, n)
                    s_ecv.wait(pe, n.back(2))
                    s_eca.wait(pe, n.back(2))
                    for i in range(2 * LP):
                        m = pe.transpose(ps_t[:, P * i:P * i + P], rot[n.u][:, P * i:P * i + P], ident)
                    m.then_inc(s_t.sem, 1)

                def scores(n):
                    s_qc.wait(pe, n)
                    s_kc.wait(pe, n)
                    s_e.wait(pe, n.back(1))
                    for i in range(2):
                        dst = ps_s[:, 512 * i:512 * i + 512]
                        pe.matmul(dst, ident16, lmask[:, n.u, :].unsqueeze(1).broadcast_to([P, 2, 2 * P]),
                                  start=True, stop=False)
                        for k in range(4):
                            pair, x_ = 2 * i + k // 2, k % 2
                            at = P * (2 * pair + x_)
                            ky = kTr[n.bp][:, S * pair:S * pair + S].rearrange("p (w k) -> p w k", k=WIN)
                            w = 2 * n.u + x_
                            own_, other = local_keys(w)
                            if other is None:
                                ky = ky[:, own_:own_ + 1, :].broadcast_to([P, 2, WIN])
                            elif other < own_:
                                ky = ky[:, other:own_ + 1, :][:, ::-1, :]
                            else:
                                ky = ky[:, own_:other + 1, :]
                            m = pe.matmul(ps_s[:, at:at + P].rearrange("p (w k) -> p w k", k=WIN),
                                          qbd[n.u][:, at:at + P], ky, start=False, stop=(k == 3))
                    m.then_inc(s_s.sem, 1)

                def transpose_e(n):
                    s_en.wait(pe, n)
                    s_qc.wait(pe, n.back(-1))
                    s_kc.wait(pe, n.back(-1))
                    for i in range(2 * LP):
                        m = pe.transpose(ps_t[:, P * i:P * i + P], e_[n.u][:, P * i:P * i + P], ident)
                    m.then_inc(s_et.sem, 1)

                def outputs(n):
                    s_ecv.wait(pe, n)
                    s_eca.wait(pe, n)
                    if n.u:
                        s_vx[0].wait(pe, n)
                        s_vx[1].wait(pe, n)
                    s_oc.wait(pe, n.back(1))
                    s_vc.wait(pe, n.back(-2))
                    for pair in range(LP):
                        for x_ in range(2):
                            w = 2 * n.u + x_
                            vv = vx[n.bp] if w == 2 else vt[n.ring]
                            at = P * (2 * pair + x_)
                            for e in range(2):
                                m = pe.matmul(ps_b[LD * e:LD * e + LD, P * pair + WIN * x_:P * pair + WIN * x_ + WIN],
                                              vv[:, P * pair + LD * e:P * pair + LD * e + LD],
                                              eT[n.u][:, at + WIN * e:at + WIN * e + WIN], start=True, stop=True)
                    m.then_inc(s_o.sem, 1)

                def project(n):
                    s_oc.wait(pe, n)
                    s_yc.wait(pe, n.back(1))
                    s_hc.wait(pe, n.back(-6))
                    for pair in range(LP):
                        m = pe.matmul(ps_a[:, 0:D], oT[n.u][:, P * pair:P * pair + P], lwo[:, D * pair:D * pair + D],
                                      start=(pair == 0), stop=(pair == LP - 1))
                    m.then_inc(s_y.sem, 1)
                run_stages(pe, [(5, scores), (6, transpose_e), (7, outputs), (1, transpose_h), (4, transpose_qk),
                                (2, qk), (4, values), (7, project)])

            @prog("scalar")
            def _(act):
                def copy_k(n):
                    s_t.wait(act, n)
                    s_s.wait(act, n.back(2))
                    act.activation(kTr[n.bp][:, :].rearrange("p (r t) -> p r t", t=S)[:, :, P * n.u:P * n.u + P],
                                   ps_t[:, 512:1024].rearrange("p (r t) -> p r t", t=P), ACT.Copy).then_inc(s_kc.sem, 1)

                def copy_e(n):
                    s_et.wait(act, n)
                    s_o.wait(act, n.back(2))
                    act.activation(eT[n.u][:, 512:1024], ps_t[:, 512:1024], ACT.Copy).then_inc(s_eca.sem, 1)

                def copy_o(n):
                    s_o.wait(act, n)
                    s_y.wait(act, n.back(2))
                    act.activation(oT[n.u][:, :], ps_b[:, :], ACT.Copy).then_inc(s_oc.sem, 1)

                def exps(n):
                    s_mx.wait(act, n, 1)
                    s_et.wait(act, n.back(2))
                    for i in range(2 * LP):
                        act.activation(e_[n.u][:, P * i:P * i + P], ps_s[:, P * i:P * i + P], ACT.Exp,
                                       bias=stat[n.u][:, i:i + 1], accum_out=stat[n.u][:, 8 + i:9 + i])\
                            .then_inc(s_e.sem, 1)

                def square(n):
                    s_qk.wait(act, n)
                    s_r.wait(act, n.back(1))
                    for i in range(2):
                        at = slice(INNER * i, INNER * i + INNER)
                        act.activation(sq[0][:, at], ps_qk[:, at], ACT.Square).then_inc(s_sq.sem, 1)

                def copy_v(n):
                    s_v.wait(act, n)
                    s_o.wait(act, n.back(4))
                    if n.u:
                        act.activation(vx[n.bp][0:WIN, :], ps_b[0:WIN, :], ACT.Copy).then_inc(s_vx[1].sem, 1)
                    else:
                        s_vx[0].wait(act, n.back(4))
                    act.activation(vt[n.ring][:, :], ps_b[:, :], ACT.Copy).then_inc(s_vc.sem, 1)

                def copy_vx(n):
                    if not n.u:
                        s_vc.wait(act, n)
                        s_o.wait(act, n.back(3))
                        act.activation(vx[n.bp][WIN:P, :], vt[n.ring][WIN:P, :], ACT.Copy).then_inc(s_vx[0].sem, 1)

                def copy_h(n):
                    s_h.wait(act, n)
                    s_v.wait(act, n.back(UNROLL))
                    act.activation(hT[n.ring][:, :], ps_a[:, 0:P], ACT.Copy).then_inc(s_hc.sem, 1)
                run_stages(act, [(6, copy_e), (5, exps), (7, copy_o), (1, copy_h), (4, copy_k), (2, square), (4, copy_v), (5, copy_vx)])

            @prog("vector")
            def _(v):
                s_wl.wait_all(v)
                for u in range(UPS):
                    for i, src in enumerate((cos_t, sin_t)):
                        w = 2 * LD
                        v.tensor_tensor(rtab[:, nt * i + w * u:nt * i + w * u + w], src[:, w * u:w * u + w],
                                        scl[:, w * i:w * i + w], ALU.mult).then_inc(s_tab.sem, 1)
                s_tab.wait_all(v)
                s_z.wait_all(v)

                def copy_q(n):
                    s_t.wait(v, n)
                    s_s.wait(v, n.back(2))
                    for e in range(2):
                        dst = qbd[n.u][LD * e:LD * e + LD, :].rearrange("p (r e q) -> p r e q", e=2, q=WIN)[:, :, e, :]
                        v.tensor_copy(dst, ps_t[LD * e:LD * e + LD, 0:512].rearrange("p (r q) -> p r q", q=WIN))\
                            .then_inc(s_qc.sem, 1)

                def maxima(n):
                    s_s.wait(v, n)
                    s_mx.wait(v, n.back(2))
                    s_en.wait(v, n.back(2))
                    v.tensor_reduce(stat[n.u][:, 0:8], ps_s[:, :].rearrange("p (r k) -> p r k", k=P), AX_X, ALU.max,
                                    negate=True).then_inc(s_mx.sem, 1)

                def sums(n):
                    s_e.wait(v, n)
                    v.reciprocal(stat[n.u][:, 16:24], stat[n.u][:, 8:16]).then_inc(s_mx.sem, 1)

                def copy_e(n):
                    s_et.wait(v, n)
                    s_o.wait(v, n.back(2))
                    v.tensor_copy(eT[n.u][:, 0:512], ps_t[:, 0:512]).then_inc(s_ecv.sem, 1)

                def add_q(n):
                    s_r.wait(v, n)
                    r = rot[n.u][:, 0:INNER]
                    v.tensor_tensor(r, r, rot2[0][:, 0:INNER], ALU.add).then_inc(s_nq.sem, 1)

                def update(n):
                    s_y.wait(v, n)
                    v.tensor_tensor(tok(y2, n), ps_a[:, 0:D], tok(y, n), ALU.add).then_inc(s_yc.sem, 1)

                def rotate(n):
                    s_qk.wait(v, n)
                    s_n.wait(v, n.back(1), 2)
                    s_nq.wait(v, n.back(1))
                    s_t.wait(v, n.back(2))
                    for i in range(2):
                        s_sq.wait(v, n, i + 1)
                        at = slice(INNER * i, INNER * i + INNER)
                        qk, out1, out2 = (t[:, at].rearrange("p (h d) -> p h d", d=LD)
                                          for t in (ps_qk, rot[n.u], rot2[0]))
                        lo = 2 * LD * n.u + LD * i
                        cos_, sin_ = rtab[:, lo:lo + LD], rtab[:, nt + lo:nt + lo + LD]
                        v.tensor_tensor(out1, qk, cos_.unsqueeze(1).broadcast_to([P, LH, LD]), ALU.mult)\
                            .then_inc(s_r.sem, 1)
                        for lo in (0, LD // 2):
                            hi = LD // 2 - lo
                            v.tensor_tensor(out2[:, :, lo:lo + LD // 2], qk[:, :, hi:hi + LD // 2],
                                            sin_[:, lo:lo + LD // 2].unsqueeze(1).broadcast_to([P, LH, LD // 2]),
                                            ALU.mult).then_inc(s_r.sem, 1)
                    v.reduce_sum(stat[n.u][:, 32:48], sq[0][:, :].rearrange("p (h d) -> p h d", d=LD), axis=AX_X)\
                        .then_inc(s_r.sem, 1)

                run_stages(v, [(8, update), (5, maxima), (6, copy_e), (3, add_q), (4, copy_q), (5, sums), (2, rotate)])

            @prog("gpsimd")
            def _(g):
                for t in qbd:
                    g.memset(t[:, :], 0.0).then_inc(s_z.sem, 1)
                for t in h[::UPS]:
                    g.memset(t[0:1, 64:D], 0.0).then_inc(s_z.sem, 1)

                def normalise(n):
                    s_r.wait(g, n)
                    t = stat[n.u]
                    alone(g, "gpsimd")
                    g.tensor_scalar(t[:, 32:48], t[:, 32:48], 1e-24, None, ALU.max).then_inc(s_n.sem, 1)
                    r = rot[n.u][:, INNER:]
                    g.tensor_tensor(r, r, rot2[0][:, INNER:], ALU.add).then_inc(s_n.sem, 1)
                    s_n.wait(g, n, 2)
                    g.tensor_tensor(t[:, 48:64], t[:, 32:48], neg_half.broadcast_to([P, 16]), ALU.pow)\
                        .then_inc(s_n.sem, 1)
                    s_n.wait(g, n, 3)
                    s_nq.wait(g, n)
                    r = rot[n.u][:, :].rearrange("p (h d) -> p h d", d=LD)
                    g.tensor_tensor(r, r, t[:, 48:64].unsqueeze(2).broadcast_to([P, 16, LD]), ALU.mult)\
                        .then_inc(s_n.sem, 1)

                def attention(n):
                    s_mx.wait(g, n)
                    e3 = e_[n.u][:, :].rearrange("p (r k) -> p r k", k=P)
                    g.tensor_tensor(e3, e3, stat[n.u][:, 16:24].unsqueeze(2).broadcast_to([P, 8, P]), ALU.mult)\
                        .then_inc(s_en.sem, 1)
                run_stages(g, [(3, normalise), (5, attention)])
            phase_end()

        def mlp(l):
            psb, many, pbank = phase_begin(f"f{l}")
            w1, w2 = psb("w1", 2 * HID), psb("w2", 3 * D)
            vec = psb("vec", 8)
            h, hn, hT, st = many("h", UNROLL, D), many("hn", 2, D), many("hT", 2, D), many("st", 2, 16)
            gl, act_ = many("gl", 2, 3 * P), many("act", 2, 3 * P)
            yo = many("yo", 2, D)
            ps_x, ps_y = [pbank(f"ps_x{i}") for i in range(2)], [pbank(f"ps_y{i}") for i in range(2)]
            ps_a, ps_g = [pbank(f"ps_a{i}") for i in range(2)], [pbank(f"ps_g{i}") for i in range(2)]
            bias = a["L0_ffn_b1"][l]
            wl = [(w1[:, :], a["L0_ffn_w1"][l]), (vec[:, 0:1], col(a["L0_ffn_ln_g"][l])),
                  (vec[:, 1:2], col(a["L0_ffn_ln_b"][l]))]
            for c, k in enumerate(HCH):
                wl += [(w2[0:k, D * c:D * c + D], a["L0_ffn_w2"][l][P * c:P * c + k, :]),
                       (vec[0:k, 2 + c:3 + c], col(bias[P * c:P * c + k])),
                       (vec[0:k, 5 + c:6 + c], col(bias[HID + P * c:HID + P * c + k]))]
            wl.append((w2[HCH[2]:HCH[2] + 1, 2 * D:3 * D], a["L0_ffn_b2"][l].rearrange("(o d) -> o d", o=1)))
            s_wl = sig("wl", 0, total=16 * len(wl))
            s_z = sig("z", 0, total=4)
            s_d = [sig(f"d{i}", 48 if i % 2 else 32, T, UNROLL) for i in range(UNROLL)]
            s_ln, ln_stats, ln_rstd, ln_norm = layernorm("ln", lambda n: h[n.ring][:, :], st, None)
            s_t, s_hc, s_g, s_a, s_y, s_yc = (sig(i, 1) for i in ("t", "hc", "g", "a", "y", "yc"))
            s_gl, s_ac = sig("gl", 3), sig("ac", 3)
            s_up = sig("up", l)

            @prog("sync")
            def _(sp):
                for dst, src in wl:
                    sp.dma_start(dst, src).then_inc(s_wl.sem, 16)
                s_z.wait_all(sp)
                run_stages(sp, [(0, shift(sp, h, s_d, s_ln, y2))])

            @prog("tensor")
            def _(pe):
                s_wl.wait_all(pe)

                def transpose_h(n):
                    s_ln.wait(pe, n)
                    s_hc.wait(pe, n.back(2))
                    pe.transpose(ps_x[n.u][:, 0:P], hn[n.u][:, :], ident).then_inc(s_t.sem, 1)

                def up(n):
                    s_hc.wait(pe, n)
                    for dst, lo, s_, free in ((ps_g, HID, s_g, s_gl), (ps_a, 0, s_a, s_ac)):
                        free.wait(pe, n.back(2))
                        for c, k in enumerate(HCH):
                            m = pe.matmul(dst[n.u][0:k, P * c:P * c + P], w1[:, lo + P * c:lo + P * c + k],
                                          hT[n.u][:, :], start=True, stop=True)
                        m.then_inc(s_.sem, 1)

                def down(n):
                    s_ac.wait(pe, n)
                    s_yc.wait(pe, n.back(2))
                    for c, k in enumerate(HCH):
                        k += c == 2
                        m = pe.matmul(ps_y[n.u][:, 0:D], act_[n.u][0:k, P * c:P * c + P], w2[0:k, D * c:D * c + D],
                                      start=(c == 0), stop=(c == 2))
                    m.then_inc(s_y.sem, 1)
                run_stages(pe, [(4, transpose_h), (7, down), (5, up)])

            @prog("scalar")
            def _(act):
                s_wl.wait_all(act)

                def copy_h(n):
                    s_t.wait(act, n)
                    s_g.wait(act, n.back(2))
                    s_a.wait(act, n.back(2))
                    act.activation(hT[n.u][:, :], ps_x[n.u][:, 0:P], ACT.Identity, bias=vec[:, 1:2], scale=vec[:, 0:1])\
                        .then_inc(s_hc.sem, 1)

                def gelu(n):
                    s_g.wait(act, n)
                    s_ac.wait(act, n.back(2))
                    for c, k in enumerate(HCH):
                        act.activation(gl[n.u][0:k, P * c:P * c + P], ps_g[n.u][0:k, P * c:P * c + P], ACT.Gelu,
                                       bias=vec[0:k, 5 + c:6 + c]).then_inc(s_gl.sem, 1)
                run_stages(act, [(4, copy_h), (5, gelu)])

            @prog("vector")
            def _(v):
                s_wl.wait_all(v)
                s_z.wait_all(v)

                def stats(n):
                    s_d[n.ring].wait(v, n)
                    ln_stats(v, n)

                def gate(n):
                    s_gl.wait(v, n)
                    s_a.wait(v, n)
                    s_y.wait(v, n.back(2))
                    for c, k in enumerate(HCH):
                        at = slice(P * c, P * c + P)
                        v.scalar_tensor_tensor(out=act_[n.u][0:k, at], in0=ps_a[n.u][0:k, at], scalar=vec[0:k, 2 + c:3 + c],
                                               in1=gl[n.u][0:k, at], op0=ALU.add, op1=ALU.mult).then_inc(s_ac.sem, 1)

                def update(n):
                    s_y.wait(v, n)
                    dst = tok(y, n) if not l else yo[n.u][:, :]
                    v.tensor_tensor(dst, ps_y[n.u][:, 0:D], tok(y2, n), ALU.add).then_inc(s_yc.sem, 1)
                    if l:
                        s_yc.wait(v, n)
                        v.scalar_tensor_tensor(out=tok(x, n), in0=yo[n.u][:, :], scalar=tg[:, 2:3], in1=tok(x, n),
                                               op0=ALU.mult, op1=ALU.add).then_inc(s_up.sem, 1)
                run_stages(v, [(6, gate), (8, update), (2, stats), (3, lambda n: ln_norm(v, n, hn[n.u][:, :], s_t))])

            @prog("gpsimd")
            def _(g):
                for t in h[::UPS]:
                    g.memset(t[0:1, 64:D], 0.0).then_inc(s_z.sem, 1)
                for t in act_:
                    g.memset(t[64:P, 2 * P:3 * P], 1.0).then_inc(s_z.sem, 1)
                run_stages(g, [(2, lambda n: ln_rstd(g, n))])
            phase_end()

        def experts():
            psb, many, pbank = phase_begin("m")
            w1, w2, rw = psb("w1", CH * P), psb("w2", CH * D), psb("rw", E)
            h, hT, st = many("h", 2, D), many("hT", 2, D), many("st", 2, 16)
            rt = many("rt", 2, 64)
            ri = many("ri", 2, E, U32)
            up_ = many("up", 2, CH * P)
            yw = many("yw", 2, E * D)
            ys = many("ys", 2, D)
            ps_h = [pbank(f"ps_h{i}") for i in range(CH // 4)]
            ps_y = pbank("ps_y", 2)
            ps_x, ps_r = pbank("ps_x"), pbank("ps_r")
            wl = [(w1[:, :], a["L1_ffn_w1"]), (w2[:, :].rearrange("p (c d) -> p c d", d=D),
                                               a["L1_ffn_w2"].rearrange("(c p) d -> p c d", p=P)), (rw[:, :], a["router_wT"])]
            s_wl = sig("wl", 0, total=16 * len(wl))
            s_ln, ln_stats, ln_rstd, ln_norm = layernorm("ln", lambda n: tok(x, n), st, None)
            s_t, s_hc, s_r, s_p, s_y, s_up = (sig(i, 1) for i in ("t", "hc", "r", "p", "y", "up"))
            s_h, s_re, s_sq = (sig(i, CH // 4) for i in ("h", "re", "sq"))
            s_top = sig("top", 9)
            s_comb = sig("comb", 1)
            s_yw = sig("yw", 2)
            s_out = sig("out", 16)

            @prog("sync")
            def _(sp):
                for dst, src in wl:
                    sp.dma_start(dst, src).then_inc(s_wl.sem, 16)

                def store(n):
                    s_up.wait(sp, n)
                    dst = out.rearrange("b s d -> (b s) d")[bass.ds(n.at(P), P), :]
                    sp.dma_start(dst, tok(x, n)).then_inc(s_out.sem, 16)
                run_stages(sp, [(7, store)])

            @prog("tensor")
            def _(pe):
                s_wl.wait_all(pe)

                def transpose_h(n):
                    s_ln.wait(pe, n)
                    s_hc.wait(pe, n.back(1))
                    pe.transpose(ps_x[:, 0:P], h[n.u][:, :], ident).then_inc(s_t.sem, 1)

                def route(n):
                    s_hc.wait(pe, n)
                    s_p.wait(pe, n.back(1))
                    pe.matmul(ps_r[:, 0:E], hT[n.u][:, :], rw[:, :], start=True, stop=True).then_inc(s_r.sem, 1)

                def up(n):
                    for b in range(CH // 4):
                        s_re.wait(pe, n.back(1), b + 1)
                        for i in range(4):
                            c = 4 * b + i
                            m = pe.matmul(ps_h[b][:, P * i:P * i + P], w1[:, P * c:P * c + P], hT[n.u][:, :],
                                          start=True, stop=True)
                        m.then_inc(s_h.sem, 1)

                def down(n):
                    s_sq.wait(pe, n)
                    s_yw.wait(pe, n.back(1), 1)
                    c = 0
                    for e, w in enumerate(EW):
                        for i in range(w // P):
                            m = pe.matmul(ps_y[:, D * e:D * e + D], up_[n.u][:, P * c:P * c + P], w2[:, D * c:D * c + D],
                                          start=(i == 0), stop=(i == w // P - 1))
                            c += 1
                    m.then_inc(s_y.sem, 1)
                run_stages(pe, [(2, transpose_h), (3, route), (3, up), (4, down)])

            @prog("scalar")
            def _(act):
                def copy_h(n):
                    s_t.wait(act, n)
                    s_r.wait(act, n.back(2))
                    s_h.wait(act, n.back(2))
                    act.activation(hT[n.u][:, :], ps_x[:, 0:P], ACT.Copy).then_inc(s_hc.sem, 1)

                def probabilities(n):
                    s_r.wait(act, n)
                    s_top.wait(act, n.back(2))
                    act.activation(rt[n.u][:, 0:E], ps_r[:, 0:E], ACT.Sigmoid).then_inc(s_p.sem, 1)

                def relu(n):
                    for b in range(CH // 4):
                        s_h.wait(act, n, b + 1)
                        s_y.wait(act, n.back(2))
                        act.activation(up_[n.u][:, 512 * b:512 * b + 512], ps_h[b][:, :], ACT.Relu).then_inc(s_re.sem, 1)

                def square(n):
                    for b in range(CH // 4):
                        s_re.wait(act, n, b + 1)
                        r = up_[n.u][:, 512 * b:512 * b + 512]
                        act.activation(r, r, ACT.Square).then_inc(s_sq.sem, 1)
                run_stages(act, [(2, copy_h), (3, probabilities), (3, relu), (3, square)])

            @prog("vector")
            def _(v):
                def top2(first, last):
                    def stage(n):
                        t, ti = rt[n.u], ri[n.u]
                        steps = [
                            lambda: v.max(t[:, 8:16], t[:, 0:E]),
                            lambda: v.max_index(ti[:, :], t[:, 8:16], t[:, 0:E]),
                            lambda: v.tensor_copy(t[:, 16:18], ti[:, 0:2]),
                            lambda: v.tensor_tensor(t[:, 18:19], t[:, 8:9], t[:, 9:10], ALU.add),
                            lambda: v.tensor_scalar(t[:, 18:19], t[:, 18:19], 1e-20, None, ALU.add),
                            lambda: v.reciprocal(t[:, 19:20], t[:, 18:19]),
                            lambda: v.tensor_scalar(t[:, 20:22], t[:, 8:10], t[:, 19:20], None, ALU.mult),
                            lambda: v.tensor_scalar(t[:, 24:32], iota, t[:, 16:17], t[:, 20:21], ALU.is_equal, ALU.mult),
                            lambda: v.tensor_scalar(t[:, 32:40], iota, t[:, 17:18], t[:, 21:22], ALU.is_equal, ALU.mult),
                        ]
                        for i in range(first, last):
                            if i:
                                s_top.wait(v, n, i)
                            else:
                                s_p.wait(v, n)
                                s_yw.wait(v, n.back(2), 1)
                            alone(v, "vector")
                            steps[i]().then_inc(s_top.sem, 1)
                    return stage

                def weights(n):
                    t = rt[n.u]
                    s_top.wait(v, n)
                    v.tensor_tensor(t[:, 40:48], t[:, 24:32], t[:, 32:40], ALU.add).then_inc(s_comb.sem, 1)

                def weigh(n):
                    s_comb.wait(v, n)
                    s_y.wait(v, n)
                    v.tensor_tensor(yw[n.u][:, :].rearrange("p (e d) -> p e d", d=D),
                                    ps_y[:, :].rearrange("p (e d) -> p e d", d=D),
                                    rt[n.u][:, 40:48].unsqueeze(2).broadcast_to([P, E, D]), ALU.mult)\
                        .then_inc(s_yw.sem, 1)

                def add_up(n):
                    s_yw.wait(v, n, 1)
                    v.reduce_sum(ys[n.u][:, :], yw[n.u][:, :].rearrange("p (e d) -> p d e", d=D), axis=AX_X)\
                        .then_inc(s_yw.sem, 1)

                def update(n):
                    s_yw.wait(v, n)
                    v.scalar_tensor_tensor(out=tok(x, n), in0=ys[n.u][:, :], scalar=tg[:, 3:4], in1=tok(x, n),
                                           op0=ALU.mult, op1=ALU.add).then_inc(s_up.sem, 1)
                run_stages(v, [(5, weigh), (3, top2(0, 1)), (0, lambda n: ln_stats(v, n)), (3, top2(1, 2)), (5, add_up),
                               (3, top2(2, 3)), (1, lambda n: ln_norm(v, n, h[n.u][:, :], s_t)), (3, top2(3, 5)),
                               (5, update), (3, top2(5, 9)), (3, weights)])

            @prog("gpsimd")
            def _(g):
                run_stages(g, [(0, lambda n: ln_rstd(g, n))])
            phase_end()

        cross_attention(0)
        for l in range(2):
            local_attention(l)
            mlp(l)
        cross_attention(1)
        experts()

        block = ctx.enter_context(nc.Block())
        starts = {"sync": block.sync, "scalar": block.scalar, "vector": block.vector, "gpsimd": block.gpsimd,
                  "tensor": block.tensor}
        for name, steps in progs.items():
            @starts[name]
            def _(eng, steps=steps):
                for f in steps:
                    f(eng)


_AS_IS = ["x", "mask_BxS2_if1", "mask_BxS2_ik0", "g_xattn", "g_ffn", "L0_ffn_wqkv", "L0_ffn_q_scale", "L0_ffn_k_scale",
          "L0_ffn_wo", "L0_ffn_ln_g", "L0_ffn_ln_b", "L0_ffn_w1", "L0_ffn_b1", "L0_ffn_w2", "L0_ffn_b2", "L1_xattn_bq",
          "L1_xattn_bk", "L1_xattn_bv", "L1_xattn_bfc", "L1_ffn_w1", "L1_ffn_w2"]
_TRANSPOSED = {"L0_xattn_WqT": "L0_xattn_Wq", "L0_xattn_WkT": "L0_xattn_Wk", "L0_xattn_WvT": "L0_xattn_Wv",
               "L0_xattn_WoT": "L0_xattn_Wo", "L1_xattn_WqT": "L1_xattn_Wq", "L1_xattn_WkT": "L1_xattn_Wk",
               "L1_xattn_WvT": "L1_xattn_Wv", "L1_xattn_WfcT": "L1_xattn_Wfc", "router_wT": "L1_ffn_router_w"}


def kernel(**inputs):
    import concourse.bacc as _bacc
    from concourse.bass_utils import run_bass_kernel_spmd as _run

    nc = _bacc.Bacc("TRN2", target_bir_lowering=False, num_devices=1)
    arrays = {n: np.ascontiguousarray(inputs[n]) for n in _AS_IS}
    arrays.update({n: np.ascontiguousarray(np.asarray(inputs[m]).T) for n, m in _TRANSPOSED.items()})
    arrays["ctxT"] = np.ascontiguousarray(np.asarray(inputs["ctx_1024"]).reshape(B * SC, D).T)
    arrays["mask0T"] = np.ascontiguousarray(np.asarray(inputs["mask_BxS2_if1"]).T)
    arrays["c32"], arrays["c16"] = constants()
    sent, args = {}, {}
    for name, v in arrays.items():
        key = f"in_{name}_dram"
        sent[key] = v
        args[name] = nc.dram_tensor(key, v.shape, mybir.dt.from_np(v.dtype), kind="ExternalInput").ap()
    out = nc.dram_tensor("out_0_dram", (B, S, D), F32, kind="ExternalOutput").ap()
    build(nc, args, out)
    r = _run(nc, [sent], core_ids=[0])
    return r.results[0]["out_0_dram"]
```

```python
from contextlib import ExitStack

import numpy as np

import concourse.bass as bass
from concourse import mybir

F32 = mybir.dt.float32
F32R = mybir.dt.float32r
BF16 = mybir.dt.bfloat16
I32 = mybir.dt.int32
U32 = mybir.dt.uint32
ALU = mybir.AluOpType
ACT = mybir.ActivationFunctionType
AX_X = mybir.AxisListType.X

P = 128
D = 128
B, S, SC = 16, 256, 64
T = B * S // P
UPS = S // P
XH, XD = 16, 8
XP = XH // 2
LH, LD, WIN = 8, 64, 64
LP = LH // 2
INNER = LH * LD
QK_SCALE = 8
HID = 341
HCH = [128, 128, 85]
EW = [128] * 4 + [256] * 4
E = len(EW)
CH = sum(EW) // P
UNROLL = 4
AWAY = -2.0e38
PADDED = -1.0e38


def position_tables():
    f = np.float32
    half = np.arange(0, LD, 2, dtype=f)
    inv = f(1.0) / np.power(f(10000.0), half / f(LD))
    t = np.arange(S, dtype=f)
    fr = t[:, None] * inv[None, :]
    fr = np.concatenate([fr, fr], -1)
    base = (half + f(0.4 * LD)) / f(1.4 * LD)
    power = (t - f(S // 2)) / f(WIN // 2)
    sc = np.power(base[None, :], power[:, None])
    sc = np.concatenate([sc, sc], -1).astype(f)
    cos, sin = np.cos(fr).astype(f), np.sin(fr).astype(f)
    sgn = np.concatenate([-np.ones(LD // 2, f), np.ones(LD // 2, f)])
    c = np.stack([cos * sc * f(QK_SCALE), cos / sc], 1)
    s = np.stack([sin * sc * sgn * f(QK_SCALE), sin / sc * sgn], 1)
    lay = lambda a: a.reshape(UPS, P, 2, LD).transpose(1, 0, 2, 3).reshape(P, -1).astype(f)
    return lay(c), lay(s)


def constants():
    f = np.float32
    p = np.arange(P)
    cos, sin = position_tables()
    own = (p[:, None] // XD == np.arange(XH)[None, :]).astype(f)
    half = (p[:, None] // SC == np.arange(2)[None, :]).astype(f)
    iota = np.broadcast_to(np.arange(E, dtype=f), (P, E))
    c32 = np.concatenate([np.eye(P, dtype=f), own, half, iota, cos, sin], 1)
    q = p % WIN
    m = np.zeros((P, UPS, 2, 2, WIN), f)
    k = np.arange(WIN)
    for u in range(UPS):
        for x in range(2):
            w = 2 * u + x
            for slot, kw in enumerate(local_keys(w)):
                off = (kw - w) * WIN if kw is not None else None
                rel = None if off is None else k[None, :] + off - q[:, None]
                bad = np.ones((P, WIN), bool) if rel is None else (rel > 0) | (rel < -WIN)
                m[:, u, x, slot] = np.where(bad, AWAY, 0)
    causal = np.where(k[None, :] > p[:, None], AWAY, 0).astype(f)
    c16 = np.concatenate([np.eye(P, dtype=f), np.ones((P, P), f), causal, m.reshape(P, -1)], 1)
    return np.ascontiguousarray(c32), np.ascontiguousarray(c16.astype(f))


def local_keys(w):
    return (w, w - 1 if w else None) if w % 2 == 0 else (w - 1, w)


class Unit:

    def __init__(self, j, c):
        self.j, self.c = j, c

    def at(self, per, add=0):
        return self.j * (UNROLL * per) + (self.c * per + add)

    def group(self, every, per, add=0):
        return self.j * (UNROLL // every * per) + (self.c // every * per + add)

    def half(self, per, add=0):
        return self.group(2, per, add)

    def back(self, k):
        return Unit(self.j, self.c - k)

    @property
    def u(self):
        return self.c % 2

    @property
    def bp(self):
        return self.c // 2 % 2

    @property
    def ring(self):
        return self.c % UNROLL


class Sig:

    def __init__(self, sem, base, per, units, every=1, total=None):
        self.sem, self.base, self.per, self.units, self.every = sem, base, per, units, every
        self.total = per * (units // every) if total is None else total

    def wait(self, eng, unit, count=None):
        if isinstance(unit.j, int):
            n = unit.at(1)
            if n < 0:
                return
            unit = Unit(0, min(n, self.units - 1))
        n = self.per if count is None else count
        eng.wait_ge(self.sem, unit.group(self.every, self.per, self.base + n))

    def wait_count(self, eng, n):
        eng.wait_ge(self.sem, self.base + n)

    def wait_all(self, eng):
        self.wait_count(eng, self.total)


def run_stages(eng, stages, units=T):
    lags = [lag for lag, _ in stages]
    first = -(-(max(lags) + 4) // UNROLL) * UNROLL

    def step(s):
        for lag, stage in stages:
            if 0 <= s - lag < units:
                stage(Unit(0, s - lag))

    for s in range(first):
        step(s)
    with eng.Fori(first // UNROLL, units // UNROLL, 1) as j:
        for c in range(UNROLL):
            for lag, stage in stages:
                stage(Unit(j, c - lag))
    for s in range(units, units + max(lags)):
        step(s)


def build(nc, a, out):
    with ExitStack() as ctx:
        def sb(name, cols, dt=F32, rows=P):
            return ctx.enter_context(nc.sbuf_tensor(name, [rows, cols], dt))

        def bank(name, n=1):
            return ctx.enter_context(nc.psum_tensor(name, [P, 512 * n], F32))

        def sem(name):
            return ctx.enter_context(nc.semaphore(name))

        x = sb("x", T * D)
        y = sb("y", T * D)
        y2 = sb("y2", T * D)
        c32 = sb("c32", a["c32"].shape[1])
        c16 = sb("c16", a["c16"].shape[1], BF16)
        o = 0
        ident = c32[:, 0:P]
        own = c32[:, P:P + XH]
        halves = c32[:, P + XH:P + XH + 2]
        iota = c32[:, P + XH + 2:P + XH + 2 + E]
        o = P + XH + 2 + E
        nt = UPS * 2 * LD
        cos_t, sin_t = c32[:, o:o + nt], c32[:, o + nt:o + 2 * nt]
        ident16 = c16[:, 0:P]
        ones16 = c16[0:1, P:2 * P]
        causal = c16[0:WIN, 2 * P:2 * P + SC]
        lmask = c16[:, 2 * P + SC:].rearrange("p (u n) -> p u n", u=UPS)
        small = sb("small", 64)
        neg_half, one = small[:, 0:1], small[:, 1:2]
        tg = small[:, 2:6]
        graw = small[:, 6:10]
        bq, bk = small[:, 10:11], small[:, 11:12]
        wq = [sb(f"wq{l}", D) for l in range(2)]
        wk = [sb(f"wk{l}", D) for l in range(2)]
        wo = [sb(f"wo{l}", D) for l in range(2)]
        bv = sb("bv", D)
        kT = [sb(f"kT{l}", B * SC) for l in range(2)]
        vall = [sb(f"vall{l}", B * D) for l in range(2)]
        padrow = [sb(f"padrow{l}", B * SC, BF16, 1) for l in range(2)]
        maskc = sb("maskc", B)
        bfc = sb("bfc", D, F32, 1)
        wqkv, lwo = sb("wqkv", 3 * INNER), sb("lwo", LP * D)
        scl = sb("scl", 4 * LD)
        mw1, mw2 = sb("mw1", 2 * HID), sb("mw2", 3 * D)
        vec = sb("vec", 8)
        ones_row = sb("ones_row", P, F32, 1)

        progs = {e: [] for e in ("sync", "scalar", "vector", "gpsimd", "tensor")}
        phase = {}
        idle = []

        def sig(name, per, units=T, every=1, total=None):
            number, base = idle.pop(0) if idle else (sem(f"sem_{phase['name']}{name}"), 0)
            s = Sig(number, base, per, units, every, total)
            phase["sigs"].append(s)
            return s

        def prog(engine):
            return lambda f: progs[engine].append(f)

        def phase_begin(name):
            mem = ExitStack()
            phase.update(name=name + "_", sigs=[], mem=mem)

            def psb(label, cols, dt=F32, rows=P):
                return mem.enter_context(nc.sbuf_tensor(f"{name}_{label}", [rows, cols], dt))

            def many(label, n, cols, dt=F32):
                return [psb(f"{label}{i}", cols, dt) for i in range(n)]

            def pbank(label, n=1):
                return mem.enter_context(nc.psum_tensor(f"{name}_{label}", [P, 512 * n], F32))
            return psb, many, pbank

        def phase_end():
            done = list(phase["sigs"])
            idle.extend((s.sem, s.base + s.total) for s in done)
            phase["mem"].close()
            for e in progs:
                progs[e].append(lambda eng: [s.wait_all(eng) for s in done])

        tok = lambda t, n: t[:, bass.ds(n.at(D), D)]
        col = lambda v: v.rearrange("(p o) -> p o", o=1)

        def attention_weights(l):
            wl = [(wqkv[:, :], a["L0_ffn_wqkv"][l]),
                  (lwo[:, :].rearrange("p (c d) -> p c d", d=D), a["L0_ffn_wo"][l].rearrange("(c p) d -> p c d", p=P))]
            for i, name in enumerate(("L0_ffn_q_scale", "L0_ffn_k_scale")):
                v_ = a[name][l]
                for lo, src in ((LD * i, v_), (2 * LD + LD * i, v_[LD // 2:LD]), (2 * LD + LD * i + LD // 2, v_[0:LD // 2])):
                    wl.append((scl[:, lo:lo + src.shape[0]], src.partition_broadcast(P)))
            return wl

        def mlp_weights(l):
            bias = a["L0_ffn_b1"][l]
            wl = [(mw1[:, :], a["L0_ffn_w1"][l]), (vec[:, 0:1], col(a["L0_ffn_ln_g"][l])),
                  (vec[:, 1:2], col(a["L0_ffn_ln_b"][l]))]
            for c, k in enumerate(HCH):
                wl += [(mw2[0:k, D * c:D * c + D], a["L0_ffn_w2"][l][P * c:P * c + k, :]),
                       (vec[0:k, 2 + c:3 + c], col(bias[P * c:P * c + k])),
                       (vec[0:k, 5 + c:6 + c], col(bias[HID + P * c:HID + P * c + k]))]
            wl.append((mw2[HCH[2]:HCH[2] + 1, 2 * D:3 * D], a["L0_ffn_b2"][l].rearrange("(o d) -> o d", o=1)))
            return wl

        def prefetch(wl):
            if wl:
                s_pre = sig("pre", 0, total=16 * len(wl))

                @prog("sync")
                def _(sp):
                    for dst, src in wl:
                        sp.dma_start(dst, src).then_inc(s_pre.sem, 16)

        psb, many, pbank = phase_begin("c")
        c16f = psb("c16f", a["c16"].shape[1])
        ctx2T = psb("ctx2T", B * P)
        wv = psb("wv", 2 * D)
        maski, maskf = many("maski", 2, B * SC, I32), many("maskf", 2, B * SC)
        maskci = psb("maskci", B, I32)
        ps_k, ps_v = [pbank(f"ps_k{l}", 2) for l in range(2)], [pbank(f"ps_v{i}") for i in range(UNROLL)]
        seqs = lambda t: t[:, :].rearrange("p (b h k) -> p b h k", h=2, k=SC)
        names = [("Wq", "Wk", "Wv", "Wo"), ("Wq", "Wk", "Wv", "Wfc")]
        weight = lambda l, i: a[f"L{l}_xattn_{names[l][i]}T"]
        masks = [a[m].rearrange("b s -> (b s)") for m in ("mask_BxS2_if1", "mask_BxS2_ik0")]
        loads = {
            "sync": ([(seqs(ctx2T)[:, :, h_, :], a["ctxT"].rearrange("p (b k) -> p b k", k=SC)) for h_ in range(2)],
                     [(maski[0][:, :], masks[0].partition_broadcast(P)), (bv[:, :], a["L1_xattn_bv"].partition_broadcast(P))],
                     [(x[:, :].rearrange("p (t d) -> p t d", d=D), a["x"].rearrange("b (u p) d -> p (b u) d", p=P)),
                      (bq, col(a["L1_xattn_bq"]))]),
            "scalar": ([(wv[:, D * l:D * l + D], weight(l, 2)) for l in range(2)] + [(wk[l][:, :], weight(l, 1)) for l in range(2)],
                       [(maskci[SC * i:SC * i + SC, :], a["mask0T"]) for i in range(2)]
                       + [(maski[1][:, :], masks[1].partition_broadcast(P)), (bk, col(a["L1_xattn_bk"]))],
                       [(c16f[:, :], a["c16"]), (c32[:, :], a["c32"]),
                        (graw[:, 0:2], a["g_xattn"].partition_broadcast(P)), (graw[:, 2:4], a["g_ffn"].partition_broadcast(P)),
                        (bfc[:, :], a["L1_xattn_bfc"].rearrange("(o d) -> o d", o=1))]
                       + [(w[l][:, :], weight(l, i)) for l in range(2) for w, i in ((wq, 0), (wo, 3))]),
        }
        s_w, s_mask, s_load = (sig(name, 0, total=16 * sum(len(v[i]) for v in loads.values()))
                               for i, name in enumerate(("w", "mask", "load")))
        s_clear = sig("clear", 0, total=3)
        s_tanh, s_c16 = sig("tanh", 0, total=1), sig("c16", 0, total=1)
        s_k = sig("k", 0, total=2)
        s_ks = sig("ks", 0, total=2)
        s_md = sig("md", 0, total=8)
        s_vp = sig("vp", 1, B)
        s_ve = sig("ve", 2, B)

        def load(queue, name):
            for group, s_ in zip(loads[name], (s_w, s_mask, s_load)):
                if s_ is s_load:
                    s_mask.wait_all(queue)
                for dst, src in group:
                    queue.dma_start(dst, src).then_inc(s_.sem, 16)

        @prog("sync")
        def _(sp):
            load(sp, "sync")

        @prog("tensor")
        def _(pe):
            s_w.wait_all(pe)
            for n in range(B):
                s_ve.wait(pe, Unit(0, n - UNROLL))
                pe.matmul(ps_v[n % UNROLL][:, 0:2 * D], ctx2T[:, P * n:P * n + P], wv[:, :], start=True, stop=True)\
                    .then_inc(s_vp.sem, 1)
                if n == UNROLL - 1:
                    for l in range(2):
                        for i in range(2):
                            m = pe.matmul(ps_k[l][:, 512 * i:512 * i + 512].rearrange("p (b k) -> p b k", k=SC), wk[l][:, :],
                                          seqs(ctx2T)[:, B // 2 * i:B // 2 * i + B // 2, 0, :], start=True, stop=True)
                        m.then_inc(s_k.sem, 1)

        @prog("scalar")
        def _(act):
            load(act, "scalar")
            s_mask.wait_all(act)
            for l in range(2):
                s_k.wait_count(act, l + 1)
                act.activation(kT[l][:, :], ps_k[l][:, :], ACT.Identity, bias=bk if l else 0.0).then_inc(s_ks.sem, 1)
            s_load.wait_all(act)
            act.activation(tg, graw, ACT.Tanh).then_inc(s_tanh.sem, 1)

        @prog("vector")
        def _(v):
            s_mask.wait_all(v)
            done = [0]

            def do(i):
                i.then_inc(s_md.sem, 1)
                done[0] += 1
                s_md.wait_count(v, done[0])
            do(v.tensor_copy(maskc[:, :], maskci[:, :]))
            do(v.tensor_scalar(maskc[:, :], maskc[:, :], 0.0, None, ALU.not_equal))

            def values(n):
                s_vp.wait(v, n)
                v.tensor_tensor(tok(vall[0], n), ps_v[n.ring][:, 0:D], maskc[:, bass.ds(n.at(1), 1)].broadcast_to([P, D]),
                                ALU.mult).then_inc(s_ve.sem, 1)
                v.tensor_tensor(tok(vall[1], n), ps_v[n.ring][:, D:2 * D], bv[:, :], ALU.add).then_inc(s_ve.sem, 1)
            run_stages(v, [(0, values)], B)
            for l in range(2):
                do(v.tensor_copy(maskf[l][:, :], maski[l][:, :]))
                do(v.tensor_scalar(padrow[l][:, :], maskf[l][0:1, :], 0.0, -1e10 * XD ** 0.5 if l else PADDED,
                                   ALU.is_equal, ALU.mult))
            do(v.tensor_scalar(maskf[1][:, :], maskf[1][:, :], 0.0, None, ALU.not_equal))
            s_ks.wait_all(v)
            do(v.tensor_tensor(kT[1][:, :], kT[1][:, :], maskf[1][:, :], ALU.mult))

        @prog("gpsimd")
        def _(g):
            for t, v_ in ((ones_row[:, :], 1.0), (neg_half, -0.5), (one, 1.0)):
                g.memset(t, v_).then_inc(s_clear.sem, 1)
            s_load.wait_all(g)
            g.tensor_copy(c16[:, :], c16f[:, :]).then_inc(s_c16.sem, 1)
        phase_end()

        s_spare = {e: sem(f"spare_{e}") for e in ("vector", "gpsimd")}

        def alone(eng, name):
            eng.sem_inc(s_spare[name], 1)

        def layernorm(name, src, st, s_ready):
            s_st = sig(name + "_stats", 2)
            s_nm = sig(name + "_norm", 1)
            s_rs = sig(name + "_rstd", 2)

            def stats(v, n):
                t = st[n.u]
                if s_ready:
                    s_ready.wait(v, n)
                s_nm.wait(v, n.back(2))
                alone(v, "vector")
                v.bn_stats(t[:, 0:6], src(n)).then_inc(s_st.sem, 1)
                s_st.wait(v, n, 1)
                alone(v, "vector")
                v.bn_aggr(t[:, 6:8], t[:, 0:6]).then_inc(s_st.sem, 1)

            def rstd(g, n):
                t = st[n.u]
                s_st.wait(g, n)
                s_nm.wait(g, n.back(2))
                alone(g, "gpsimd")
                g.tensor_scalar(t[:, 8:9], t[:, 7:8], 1e-5, None, ALU.add).then_inc(s_rs.sem, 1)
                s_rs.wait(g, n, 1)
                g.tensor_tensor(t[:, 9:10], t[:, 8:9], neg_half, ALU.pow).then_inc(s_rs.sem, 1)

            def norm(v, n, dst, free=None):
                t = st[n.u]
                s_rs.wait(v, n)
                if free:
                    free.wait(v, n.back(2))
                v.tensor_scalar(dst, src(n), t[:, 6:7], t[:, 9:10], ALU.subtract, ALU.mult).then_inc(s_nm.sem, 1)
            return s_nm, stats, rstd, norm

        def cross_attention(l, later):
            kT_, vall_, padrow_ = kT[l], vall[l], padrow[l]
            psb, many, pbank = phase_begin(f"x{l}")
            prefetch(later)
            st, st2, stat = many("st", 2, 16), many("st2", 2, 16), many("stat", 2, 2 * XH)
            h, hT = many("h", 2, D), many("hT", 2, D)
            qT, qTr = many("qT", 2, D, F32R), many("qTr", 2, D, F32R)
            kTh, kTr = psb("kTh", B * SC, F32R), psb("kTr", B * SC)
            e_ = many("e", 2, XH * SC)
            eT = many("eT", 2, XH * SC)
            od = many("od", 2, 2 * P)
            on, onT = many("on", 2, D), many("onT", 2, D)
            kblk, kblkr = many("kblk", 2, XH * SC, F32R), many("kblkr", 2, XH * SC, F32R)
            vpair = many("vpair", 2, XP * 32)
            ps_s, ps_t = pbank("ps_s", 2), pbank("ps_t", 2)
            ps_x, ps_q, ps_o, ps_w = (pbank(f"ps{i}") for i in range(4))
            s_z = sig("z", 0, total=4 if l else 2)
            s_h, s_hc, s_q, s_qc = (sig(i, 1) for i in ("h", "hc", "q", "qc"))
            s_kb = sig("kb", 2, T, 2)
            s_kh, s_kr = sig("kh", 0, total=1), sig("kr", 0, total=1)
            s_qr = sig("qr", 1)
            s_vb = sig("vb", 2 if l else 3, T, 2)
            s_s, s_e, s_t, s_tc, s_o, s_oc, s_w, s_up = (sig(i, 1) for i in ("s", "e", "t", "tc", "o", "oc", "w", "up"))
            s_sm = sig("sm", 2)
            s_ot = sig("ot", 1)
            s_on = sig("on", 2)
            s_nt, s_nc = sig("nt", 1), sig("nc", 1)
            s_ln, ln_stats, ln_rstd, ln_norm = layernorm("ln", lambda n: tok(x, n), st, None)
            if not l:
                _, y_stats, y_rstd, y_norm = layernorm("ly", lambda n: tok(x, n), st2, s_up)

            @prog("tensor")
            def _(pe):
                def transpose_h(n):
                    s_ln.wait(pe, n)
                    s_hc.wait(pe, n.back(1))
                    pe.transpose(ps_x[:, 0:P], h[n.u][:, :], ident).then_inc(s_h.sem, 1)

                def project_q(n):
                    s_hc.wait(pe, n)
                    s_qc.wait(pe, n.back(1))
                    s_qr.wait(pe, n.back(1))
                    pe.matmul(ps_q[:, 0:P], wq[l][:, :], hT[n.u][:, :], start=True, stop=True).then_inc(s_q.sem, 1)

                def scores(n):
                    s_qc.wait(pe, n)
                    s_qr.wait(pe, n)
                    s_kb.wait(pe, n)
                    s_sm.wait(pe, n.back(1))
                    for i in range(2):
                        dst = ps_s[:, 512 * i:512 * i + 512]
                        pad = padrow_[0:1, bass.ds(n.half(SC), SC)].unsqueeze(1).broadcast_to([1, XH // 2, SC])
                        for q_, k_ in ((qT, kblk), (qT, kblkr), (qTr, kblk)):
                            pe.matmul(dst, q_[n.u][:, :], k_[n.bp][:, 512 * i:512 * i + 512],
                                      start=(q_ is qT and k_ is kblk), stop=False)
                        if not l and n.u == 0:
                            pe.matmul(dst, ident16[0:SC, :], causal.unsqueeze(1).broadcast_to([SC, XH // 2, SC]),
                                      start=False, stop=False)
                        m = pe.matmul(dst, ones16, pad, start=False, stop=True)
                    m.then_inc(s_s.sem, 1)

                def transpose_e(n):
                    s_e.wait(pe, n)
                    s_tc.wait(pe, n.back(1))
                    for i in range(XP):
                        m = pe.transpose(ps_t[:, P * i:P * i + P], e_[n.u][:, P * i:P * i + P], ident)
                    m.then_inc(s_t.sem, 1)

                def outputs(n):
                    s_tc.wait(pe, n)
                    s_vb.wait(pe, n)
                    s_on.wait(pe, n.back(1))
                    for pair in range(XP):
                        r, j = divmod(pair, 4)
                        m = pe.matmul(ps_o[32 * j:32 * j + 32, P * r:P * r + P],
                                      vpair[n.bp][:, 32 * pair:32 * pair + 32],
                                      eT[n.u][:, P * pair:P * pair + P], start=True, stop=True)
                    m.then_inc(s_o.sem, 1)

                def transpose_o(n):
                    s_oc.wait(pe, n)
                    for r in range(2):
                        m = pe.transpose(ps_o[:, 256 + P * r:256 + P * r + P], od[n.u][:, P * r:P * r + P], ident)
                    m.then_inc(s_ot.sem, 1)

                def transpose_on(n):
                    s_on.wait(pe, n)
                    s_up.wait(pe, n.back(1))
                    pe.transpose(ps_w[:, P:2 * P], on[n.u][:, :], ident).then_inc(s_nt.sem, 1)

                def project_o(n):
                    s_nc.wait(pe, n)
                    m = pe.matmul(ps_w[:, 0:D], onT[n.u][:, :], wo[l][:, :], start=True, stop=not l)
                    if l:
                        m = pe.matmul(ps_w[:, 0:D], ones_row[:, :], bfc[:, :], start=False, stop=True)
                    m.then_inc(s_w.sem, 1)
                run_stages(pe, [(9, project_o), (2, transpose_h), (3, project_q), (7, transpose_o), (4, scores),
                                (8, transpose_on), (5, transpose_e), (6, outputs)])

            @prog("scalar")
            def _(act):
                def copy_h(n):
                    s_h.wait(act, n)
                    s_q.wait(act, n.back(2))
                    act.activation(hT[n.u][:, :], ps_x[:, 0:P], ACT.Copy).then_inc(s_hc.sem, 1)

                def copy_q(n):
                    s_q.wait(act, n)
                    s_s.wait(act, n.back(2))
                    act.activation(qT[n.u][:, :], ps_q[:, 0:P], ACT.Identity, bias=bq if l else 0.0)\
                        .then_inc(s_qc.sem, 1)

                def exps(n):
                    s_sm.wait(act, n)
                    act.activation(e_[n.u][:, :], e_[n.u][:, :], ACT.Exp, scale=XD ** -0.5).then_inc(s_e.sem, 1)

                def copy_e(n):
                    s_t.wait(act, n)
                    s_o.wait(act, n.back(2))
                    act.activation(eT[n.u][:, :], ps_t[:, :], ACT.Copy).then_inc(s_tc.sem, 1)

                def copy_o(n):
                    s_o.wait(act, n)
                    s_ot.wait(act, n.back(2))
                    act.activation(od[n.u][:, :], ps_o[:, 0:2 * P], ACT.Copy).then_inc(s_oc.sem, 1)

                def copy_on(n):
                    s_nt.wait(act, n)
                    s_w.wait(act, n.back(2))
                    act.activation(onT[n.u][:, :], ps_w[:, P:2 * P], ACT.Copy).then_inc(s_nc.sem, 1)
                run_stages(act, [(5, exps), (2, copy_h), (3, copy_q), (8, copy_on), (5, copy_e), (6, copy_o)])

            @prog("vector")
            def _(v):
                v.tensor_copy(kTh[:, :], kT_[:, :]).then_inc(s_kh.sem, 1)
                s_kh.wait_all(v)
                v.tensor_tensor(kTr[:, :], kT_[:, :], kTh[:, :], ALU.subtract).then_inc(s_kr.sem, 1)

                def rest_q(n):
                    s_qc.wait(v, n)
                    s_s.wait(v, n.back(2))
                    if l:
                        i = v.scalar_tensor_tensor(out=qTr[n.u][:, :], in0=ps_q[:, 0:P], scalar=bq, in1=qT[n.u][:, :],
                                                   op0=ALU.add, op1=ALU.subtract)
                    else:
                        i = v.tensor_tensor(qTr[n.u][:, :], ps_q[:, 0:P], qT[n.u][:, :], ALU.subtract)
                    i.then_inc(s_qr.sem, 1)

                def softmax(n):
                    s_s.wait(v, n)
                    sc = ps_s[:, :].rearrange("p (h k) -> p h k", k=SC)
                    v.tensor_reduce(stat[n.u][:, 0:XH], sc, AX_X, ALU.max, negate=True).then_inc(s_sm.sem, 1)
                    s_sm.wait(v, n, 1)
                    s_t.wait(v, n.back(2))
                    v.tensor_tensor(e_[n.u][:, :].rearrange("p (h k) -> p h k", k=SC), sc,
                                    stat[n.u][:, 0:XH].unsqueeze(2).broadcast_to([P, XH, SC]), ALU.add)\
                        .then_inc(s_sm.sem, 1)

                def update(n):
                    s_w.wait(v, n)
                    v.scalar_tensor_tensor(out=tok(x, n), in0=ps_w[:, 0:D], scalar=tg[:, l:l + 1], in1=tok(x, n),
                                           op0=ALU.mult, op1=ALU.add).then_inc(s_up.sem, 1)

                def divide(n):
                    s_ot.wait(v, n)
                    s_nt.wait(v, n.back(2))
                    o4 = ps_o[:, 256:512].rearrange("p (r c) -> p r c", c=32)
                    inv = stat[n.u][:, XH:2 * XH].rearrange("p (r e) -> p r e", e=2)
                    v.reciprocal(inv, o4[:, :, 16:18]).then_inc(s_on.sem, 1)
                    s_on.wait(v, n, 1)
                    v.tensor_tensor(on[n.u][:, :].rearrange("p (r e d) -> p r e d", e=2, d=XD),
                                    o4[:, :, 0:16].rearrange("p r (e d) -> p r e d", e=2),
                                    inv.unsqueeze(3).broadcast_to([P, XP, 2, XD]), ALU.mult).then_inc(s_on.sem, 1)
                stages = [(9, update), (7, divide), (0, lambda n: ln_stats(v, n)),
                          (1, lambda n: ln_norm(v, n, h[n.u][:, :], s_h)), (3, rest_q), (4, softmax)]
                if not l:
                    stages = stages[:-1] + [(11, lambda n: y_norm(v, n, tok(y, n))), (10, lambda n: y_stats(v, n)), stages[-1]]
                run_stages(v, stages)

            @prog("gpsimd")
            def _(g):
                s_kh.wait_all(g)
                s_kr.wait_all(g)
                for t in vpair:
                    g.memset(t[:, :], 0.0).then_inc(s_z.sem, 1)
                s_z.wait_count(g, 2)
                sum_cols = lambda t: t[:, :].rearrange("p (r c) -> p r c", c=32)[:, :, 16:18]
                if l:
                    for t in vpair:
                        g.tensor_copy(sum_cols(t), halves.unsqueeze(1).broadcast_to([P, XP, 2])).then_inc(s_z.sem, 1)
                    s_z.wait_all(g)

                def key_blocks(n):
                    if n.u:
                        return
                    s_s.wait(g, n.back(3))
                    for blk, src in ((kblk, kTh), (kblkr, kTr)):
                        g.tensor_tensor(blk[n.bp][:, :].rearrange("p (h k) -> p h k", k=SC),
                                        src[:, bass.ds(n.half(SC), SC)].unsqueeze(1).broadcast_to([P, XH, SC]),
                                        own.unsqueeze(2).broadcast_to([P, XH, SC]), ALU.mult).then_inc(s_kb.sem, 1)

                def value_blocks(n):
                    if n.u:
                        return
                    s_o.wait(g, n.back(3))
                    s_kb.wait(g, n)
                    for i in range(2):
                        if i:
                            s_vb.wait(g, n, i)
                        src = vall_[SC * i:SC * i + SC, bass.ds(n.half(D), D)]\
                            .rearrange("p (r e d) -> p r e d", e=2, d=XD)[:, :, i, :]
                        dst = vpair[n.bp][SC * i:SC * i + SC, :].rearrange("p (r c) -> p r c", c=32)
                        g.tensor_copy(dst[:, :, XD * i:XD * i + XD], src).then_inc(s_vb.sem, 1)
                    s_vb.wait(g, n, 2)
                    if not l:
                        mc = maskc[:, bass.ds(n.half(1), 1)].unsqueeze(2).broadcast_to([P, XP, 2])
                        g.tensor_tensor(sum_cols(vpair[n.bp]), halves.unsqueeze(1).broadcast_to([P, XP, 2]), mc,
                                        ALU.mult).then_inc(s_vb.sem, 1)

                stages = [(0, lambda n: ln_rstd(g, n)), (2, key_blocks), (4, value_blocks)]
                if not l:
                    stages = [(10, lambda n: y_rstd(g, n))] + stages
                run_stages(g, stages)
            phase_end()

        def shift(sp, h, s_d, s_free, src):
            def stage(n):
                s_free.wait(sp, n.back(UNROLL))
                t, s = h[n.ring], s_d[n.ring].sem
                sp.dma_start(t[:, 0:64], src[:, bass.ds(n.at(D), 64)]).then_inc(s, 16)
                sp.dma_start(t[1:P, 64:D], src[0:P - 1, bass.ds(n.at(D, 64), 64)]).then_inc(s, 16)
                if n.u:
                    sp.dma_start(t[0:1, 64:D], src[P - 1:P, bass.ds(n.at(D, 64 - D), 64)]).then_inc(s, 16)
            return stage

        def local_attention(l):
            psb, many, pbank = phase_begin(f"a{l}")
            rtab = psb("rtab", 2 * nt)
            h = many("h", UNROLL, D)
            hT, hTr = many("hT", UNROLL, D, F32R), many("hTr", UNROLL, D, F32R)
            wqh, wqr = psb("wqh", 3 * INNER, F32R), psb("wqr", 3 * INNER, F32R)
            sq = many("sq", 1, 2 * INNER)
            rot, rot2 = many("rot", 2, 2 * INNER), many("rot2", 1, 2 * INNER)
            stat = many("stat", 2, 64)
            qbd = many("qbd", 2, LP * 2 * P)
            kTr = many("kTr", 2, LP * S)
            vt, vx = many("vt", UNROLL, INNER), many("vx", 2, INNER)
            e_, eT = many("e", 2, LP * 2 * P), many("eT", 2, LP * 2 * P)
            oT = many("oT", 2, INNER)
            ps_qk, ps_s, ps_t = pbank("ps_qk", 2), pbank("ps_s", 2), pbank("ps_t", 2)
            ps_a, ps_b = pbank("ps_a"), pbank("ps_b")
            s_tab = sig("tab", 0, total=2 * UPS)
            s_z = sig("z", 0, total=4)
            s_d = [sig(f"d{i}", 48 if i % 2 else 32, T, UNROLL) for i in range(UNROLL)]
            s_h, s_hc, s_vc, s_t, s_kc, s_s, s_en, s_et, s_o, s_oc, s_y, s_yc = (
                sig(i, 1) for i in ("h", "hc", "vc", "t", "kc", "s", "en", "et", "o", "oc", "y", "yc"))
            s_qk, s_v = sig("qk", 2), sig("v", 1)
            s_vx = [sig(f"vx{u}", 1, T, 2) for u in range(2)]
            s_sq = sig("sq", 2)
            s_r, s_ss = sig("r", 6), sig("ss", 1)
            s_n = sig("n", 4)
            s_hr = sig("hr", 1)
            s_wh, s_wr = sig("wh", 0, total=1), sig("wr", 0, total=1)
            s_nq = sig("nq", 1)
            s_qc = sig("qc", 2)
            s_mx = sig("mx", 2)
            s_e = sig("e", 2 * LP)
            s_ec = sig("ec", 1)

            @prog("sync")
            def _(sp):
                s_z.wait_count(sp, UNROLL // UPS)
                run_stages(sp, [(0, shift(sp, h, s_d, s_h, y))])

            @prog("tensor")
            def _(pe):
                s_wh.wait_all(pe)
                s_wr.wait_all(pe)

                def transpose_h(n):
                    s_d[n.ring].wait(pe, n)
                    s_hc.wait(pe, n.back(1))
                    s_hr.wait(pe, n.back(1))
                    s_yc.wait(pe, n.back(8))
                    pe.transpose(ps_a[:, 0:P], h[n.ring][:, :], ident).then_inc(s_h.sem, 1)

                def project_h(dst, n, lo):
                    for i, (lhs, w) in enumerate(((hT, wqh), (hT, wqr), (hTr, wqh))):
                        m = pe.matmul(dst, lhs[n.ring][:, :], w[:, lo:lo + 512], start=(i == 0), stop=(i == 2))
                    return m

                def qk(n):
                    s_hc.wait(pe, n)
                    s_hr.wait(pe, n)
                    s_r.wait(pe, n.back(1))
                    s_sq.wait(pe, n.back(1))
                    for i in range(2):
                        project_h(ps_qk[:, 512 * i:512 * i + 512], n, 512 * i).then_inc(s_qk.sem, 1)

                def values(n):
                    s_vc.wait(pe, n.back(1))
                    s_oc.wait(pe, n.back(3))
                    project_h(ps_b[:, :], n, 1024).then_inc(s_v.sem, 1)

                def transpose_qk(n):
                    s_n.wait(pe, n)
                    s_ec.wait(pe, n.back(2))
                    for i in range(2 * LP):
                        m = pe.transpose(ps_t[:, P * i:P * i + P], rot[n.u][:, P * i:P * i + P], ident)
                    m.then_inc(s_t.sem, 1)

                def scores(n):
                    s_qc.wait(pe, n)
                    s_kc.wait(pe, n)
                    s_e.wait(pe, n.back(1))
                    for i in range(2):
                        dst = ps_s[:, 512 * i:512 * i + 512]
                        pe.matmul(dst, ident16, lmask[:, n.u, :].unsqueeze(1).broadcast_to([P, 2, 2 * P]),
                                  start=True, stop=False)
                        for k in range(4):
                            pair, x_ = 2 * i + k // 2, k % 2
                            at = P * (2 * pair + x_)
                            ky = kTr[n.bp][:, S * pair:S * pair + S].rearrange("p (w k) -> p w k", k=WIN)
                            w = 2 * n.u + x_
                            own_, other = local_keys(w)
                            if other is None:
                                ky = ky[:, own_:own_ + 1, :].broadcast_to([P, 2, WIN])
                            elif other < own_:
                                ky = ky[:, other:own_ + 1, :][:, ::-1, :]
                            else:
                                ky = ky[:, own_:other + 1, :]
                            m = pe.matmul(ps_s[:, at:at + P].rearrange("p (w k) -> p w k", k=WIN),
                                          qbd[n.u][:, at:at + P], ky, start=False, stop=(k == 3))
                    m.then_inc(s_s.sem, 1)

                def transpose_e(n):
                    s_en.wait(pe, n)
                    s_qc.wait(pe, n.back(-1))
                    s_kc.wait(pe, n.back(-1))
                    for i in range(2 * LP):
                        m = pe.transpose(ps_t[:, P * i:P * i + P], e_[n.u][:, P * i:P * i + P], ident)
                    m.then_inc(s_et.sem, 1)

                def outputs(n):
                    s_ec.wait(pe, n)
                    if n.u:
                        s_vx[0].wait(pe, n)
                        s_vx[1].wait(pe, n)
                    s_oc.wait(pe, n.back(1))
                    s_vc.wait(pe, n.back(-2))
                    for pair in range(LP):
                        for x_ in range(2):
                            w = 2 * n.u + x_
                            vv = vx[n.bp] if w == 2 else vt[n.ring]
                            at = P * (2 * pair + x_)
                            for e in range(2):
                                m = pe.matmul(ps_b[LD * e:LD * e + LD, P * pair + WIN * x_:P * pair + WIN * x_ + WIN],
                                              vv[:, P * pair + LD * e:P * pair + LD * e + LD],
                                              eT[n.u][:, at + WIN * e:at + WIN * e + WIN], start=True, stop=True)
                    m.then_inc(s_o.sem, 1)

                def project(n):
                    s_oc.wait(pe, n)
                    s_yc.wait(pe, n.back(1))
                    s_hc.wait(pe, n.back(-7))
                    s_hr.wait(pe, n.back(-7))
                    for pair in range(LP):
                        m = pe.matmul(ps_a[:, 0:D], oT[n.u][:, P * pair:P * pair + P], lwo[:, D * pair:D * pair + D],
                                      start=(pair == 0), stop=(pair == LP - 1))
                    m.then_inc(s_y.sem, 1)
                run_stages(pe, [(5, scores), (1, transpose_h), (6, transpose_e), (7, outputs), (4, transpose_qk),
                                (2, qk), (8, project), (4, values)])

            @prog("scalar")
            def _(act):
                act.activation(wqh[:, :], wqkv[:, :], ACT.Copy).then_inc(s_wh.sem, 1)

                def copy_k(n):
                    s_t.wait(act, n)
                    s_s.wait(act, n.back(2))
                    act.activation(kTr[n.bp][:, :].rearrange("p (r t) -> p r t", t=S)[:, :, P * n.u:P * n.u + P],
                                   ps_t[:, 512:1024].rearrange("p (r t) -> p r t", t=P), ACT.Copy).then_inc(s_kc.sem, 1)

                def copy_e(n):
                    s_et.wait(act, n)
                    s_o.wait(act, n.back(2))
                    act.activation(eT[n.u][:, :], ps_t[:, :], ACT.Copy).then_inc(s_ec.sem, 1)

                def exps(n):
                    s_mx.wait(act, n, 1)
                    s_et.wait(act, n.back(2))
                    for i in range(2 * LP):
                        act.activation(e_[n.u][:, P * i:P * i + P], ps_s[:, P * i:P * i + P], ACT.Exp,
                                       bias=stat[n.u][:, i:i + 1], accum_out=stat[n.u][:, 8 + i:9 + i])\
                            .then_inc(s_e.sem, 1)

                def square(i):
                    def stage(n):
                        s_ss.wait(act, n.back(1))
                        s_qk.wait(act, n, i + 1)
                        at = slice(INNER * i, INNER * i + INNER)
                        act.activation(sq[0][:, at], ps_qk[:, at], ACT.Square).then_inc(s_sq.sem, 1)
                    return stage

                def copy_v(n):
                    s_v.wait(act, n)
                    s_o.wait(act, n.back(4))
                    if n.u:
                        act.activation(vx[n.bp][0:WIN, :], ps_b[0:WIN, :], ACT.Copy).then_inc(s_vx[1].sem, 1)
                    else:
                        s_vx[0].wait(act, n.back(4))
                    act.activation(vt[n.ring][:, :], ps_b[:, :], ACT.Copy).then_inc(s_vc.sem, 1)

                def copy_vx(n):
                    if not n.u:
                        s_vc.wait(act, n)
                        s_o.wait(act, n.back(3))
                        act.activation(vx[n.bp][WIN:P, :], vt[n.ring][WIN:P, :], ACT.Copy).then_inc(s_vx[0].sem, 1)

                def copy_h(n):
                    s_h.wait(act, n)
                    s_v.wait(act, n.back(UNROLL))
                    act.activation(hT[n.ring][:, :], ps_a[:, 0:P], ACT.Copy).then_inc(s_hc.sem, 1)
                run_stages(act, [(1, copy_h), (6, copy_e), (5, exps), (2, square(0)), (4, copy_k), (2, square(1)), (4, copy_v),
                                 (5, copy_vx)])

            @prog("vector")
            def _(v):
                for u in range(UPS):
                    for i, src in enumerate((cos_t, sin_t)):
                        w = 2 * LD
                        v.tensor_tensor(rtab[:, nt * i + w * u:nt * i + w * u + w], src[:, w * u:w * u + w],
                                        scl[:, w * i:w * i + w], ALU.mult).then_inc(s_tab.sem, 1)
                s_tab.wait_all(v)
                s_z.wait_all(v)
                s_wh.wait_all(v)
                v.tensor_tensor(wqr[:, :], wqkv[:, :], wqh[:, :], ALU.subtract).then_inc(s_wr.sem, 1)

                def rest_h(n):
                    s_hc.wait(v, n)
                    s_v.wait(v, n.back(UNROLL))
                    v.tensor_tensor(hTr[n.ring][:, :], ps_a[:, 0:P], hT[n.ring][:, :], ALU.subtract).then_inc(s_hr.sem, 1)

                def copy_q(n):
                    s_t.wait(v, n)
                    s_s.wait(v, n.back(2))
                    for e in range(2):
                        dst = qbd[n.u][LD * e:LD * e + LD, :].rearrange("p (r e q) -> p r e q", e=2, q=WIN)[:, :, e, :]
                        v.tensor_copy(dst, ps_t[LD * e:LD * e + LD, 0:512].rearrange("p (r q) -> p r q", q=WIN))\
                            .then_inc(s_qc.sem, 1)

                def maxima(n):
                    s_s.wait(v, n)
                    s_mx.wait(v, n.back(2))
                    s_en.wait(v, n.back(2))
                    v.tensor_reduce(stat[n.u][:, 0:8], ps_s[:, :].rearrange("p (r k) -> p r k", k=P), AX_X, ALU.max,
                                    negate=True).then_inc(s_mx.sem, 1)

                def sums(n):
                    s_e.wait(v, n)
                    v.reciprocal(stat[n.u][:, 16:24], stat[n.u][:, 8:16]).then_inc(s_mx.sem, 1)

                def add_q(n):
                    s_r.wait(v, n)
                    r = rot[n.u][:, 0:INNER]
                    v.tensor_tensor(r, r, rot2[0][:, 0:INNER], ALU.add).then_inc(s_nq.sem, 1)

                def copy_o(n):
                    s_o.wait(v, n)
                    s_y.wait(v, n.back(2))
                    v.tensor_copy(oT[n.u][:, :], ps_b[:, :]).then_inc(s_oc.sem, 1)

                def update(n):
                    s_y.wait(v, n)
                    v.tensor_tensor(tok(y2, n), ps_a[:, 0:D], tok(y, n), ALU.add).then_inc(s_yc.sem, 1)

                def rotate(n):
                    s_n.wait(v, n.back(1), 1)
                    s_nq.wait(v, n.back(1))
                    s_t.wait(v, n.back(2))
                    for i in range(2):
                        s_sq.wait(v, n, i + 1)
                        at = slice(INNER * i, INNER * i + INNER)
                        qk, out1, out2 = (t[:, at].rearrange("p (h d) -> p h d", d=LD)
                                          for t in (ps_qk, rot[n.u], rot2[0]))
                        lo = 2 * LD * n.u + LD * i
                        cos_, sin_ = rtab[:, lo:lo + LD], rtab[:, nt + lo:nt + lo + LD]
                        v.tensor_tensor(out1, qk, cos_.unsqueeze(1).broadcast_to([P, LH, LD]), ALU.mult)\
                            .then_inc(s_r.sem, 1)
                        for lo in (0, LD // 2):
                            hi = LD // 2 - lo
                            v.tensor_tensor(out2[:, :, lo:lo + LD // 2], qk[:, :, hi:hi + LD // 2],
                                            sin_[:, lo:lo + LD // 2].unsqueeze(1).broadcast_to([P, LH, LD // 2]),
                                            ALU.mult).then_inc(s_r.sem, 1)

                def squares(n):
                    s_n.wait(v, n.back(2))
                    s_sq.wait(v, n)
                    v.reduce_sum(stat[n.u][:, 32:48], sq[0][:, :].rearrange("p (h d) -> p h d", d=LD), axis=AX_X)\
                        .then_inc(s_ss.sem, 1)

                run_stages(v, [(3, squares), (5, maxima), (1, rest_h), (7, copy_o), (3, add_q), (4, copy_q), (5, sums), (2, rotate),
                               (8, update)])

            @prog("gpsimd")
            def _(g):
                for t in h[::UPS]:
                    g.memset(t[0:1, 64:D], 0.0).then_inc(s_z.sem, 1)
                for t in qbd:
                    g.memset(t[:, :], 0.0).then_inc(s_z.sem, 1)

                def normalise(n):
                    t = stat[n.u]
                    r = rot[n.u][:, INNER:]
                    s_r.wait(g, n)
                    g.tensor_tensor(r, r, rot2[0][:, INNER:], ALU.add).then_inc(s_n.sem, 1)
                    s_ss.wait(g, n)
                    alone(g, "gpsimd")
                    g.tensor_scalar(t[:, 32:48], t[:, 32:48], 1e-24, None, ALU.max).then_inc(s_n.sem, 1)
                    s_n.wait(g, n, 2)
                    g.tensor_tensor(t[:, 48:64], t[:, 32:48], neg_half.broadcast_to([P, 16]), ALU.pow)\
                        .then_inc(s_n.sem, 1)
                    s_n.wait(g, n, 3)
                    s_nq.wait(g, n)
                    r = rot[n.u][:, :].rearrange("p (h d) -> p h d", d=LD)
                    g.tensor_tensor(r, r, t[:, 48:64].unsqueeze(2).broadcast_to([P, 16, LD]), ALU.mult)\
                        .then_inc(s_n.sem, 1)

                def attention(n):
                    s_mx.wait(g, n)
                    e3 = e_[n.u][:, :].rearrange("p (r k) -> p r k", k=P)
                    g.tensor_tensor(e3, e3, stat[n.u][:, 16:24].unsqueeze(2).broadcast_to([P, 8, P]), ALU.mult)\
                        .then_inc(s_en.sem, 1)
                run_stages(g, [(3, normalise), (5, attention)])
            if l:
                prefetch(mlp_weights(l))
            phase_end()

        def mlp(l):
            psb, many, pbank = phase_begin(f"f{l}")
            h, hn, hT, st = many("h", UNROLL, D), many("hn", 2, D), many("hT", 2, D), many("st", 2, 16)
            gl, act_ = many("gl", 2, 3 * P), many("act", 2, 3 * P)
            yo = many("yo", 2, D)
            ps_x, ps_y = [pbank(f"ps_x{i}") for i in range(2)], [pbank(f"ps_y{i}") for i in range(2)]
            ps_a, ps_g = [pbank(f"ps_a{i}") for i in range(2)], [pbank(f"ps_g{i}") for i in range(2)]
            s_z = sig("z", 0, total=4)
            s_d = [sig(f"d{i}", 48 if i % 2 else 32, T, UNROLL) for i in range(UNROLL)]
            s_ln, ln_stats, ln_rstd, ln_norm = layernorm("ln", lambda n: h[n.ring][:, :], st, None)
            s_t, s_hc, s_g, s_a, s_y, s_yc = (sig(i, 1) for i in ("t", "hc", "g", "a", "y", "yc"))
            s_gl, s_ac = sig("gl", 3), sig("ac", 3)
            s_up = sig("up", l)

            @prog("sync")
            def _(sp):
                s_z.wait_count(sp, UNROLL // UPS)
                run_stages(sp, [(0, shift(sp, h, s_d, s_ln, y2))])

            @prog("tensor")
            def _(pe):
                def transpose_h(n):
                    s_ln.wait(pe, n)
                    s_hc.wait(pe, n.back(2))
                    pe.transpose(ps_x[n.u][:, 0:P], hn[n.u][:, :], ident).then_inc(s_t.sem, 1)

                def up(n):
                    s_hc.wait(pe, n)
                    for dst, lo, s_, free in ((ps_g, HID, s_g, s_gl), (ps_a, 0, s_a, s_ac)):
                        free.wait(pe, n.back(2))
                        for c, k in enumerate(HCH):
                            m = pe.matmul(dst[n.u][0:k, P * c:P * c + P], mw1[:, lo + P * c:lo + P * c + k],
                                          hT[n.u][:, :], start=True, stop=True)
                        m.then_inc(s_.sem, 1)

                def down(n):
                    s_ac.wait(pe, n)
                    s_yc.wait(pe, n.back(2))
                    for c, k in enumerate(HCH):
                        k += c == 2
                        m = pe.matmul(ps_y[n.u][:, 0:D], act_[n.u][0:k, P * c:P * c + P], mw2[0:k, D * c:D * c + D],
                                      start=(c == 0), stop=(c == 2))
                    m.then_inc(s_y.sem, 1)
                run_stages(pe, [(4, transpose_h), (7, down), (5, up)])

            @prog("scalar")
            def _(act):
                def copy_h(n):
                    s_t.wait(act, n)
                    s_g.wait(act, n.back(2))
                    s_a.wait(act, n.back(2))
                    act.activation(hT[n.u][:, :], ps_x[n.u][:, 0:P], ACT.Identity, bias=vec[:, 1:2], scale=vec[:, 0:1])\
                        .then_inc(s_hc.sem, 1)

                def gelu(n):
                    s_g.wait(act, n)
                    s_ac.wait(act, n.back(2))
                    for c, k in enumerate(HCH):
                        act.activation(gl[n.u][0:k, P * c:P * c + P], ps_g[n.u][0:k, P * c:P * c + P], ACT.Gelu,
                                       bias=vec[0:k, 5 + c:6 + c]).then_inc(s_gl.sem, 1)
                run_stages(act, [(4, copy_h), (5, gelu)])

            @prog("vector")
            def _(v):
                s_z.wait_all(v)

                def stats(n):
                    s_d[n.ring].wait(v, n)
                    ln_stats(v, n)

                def gate(n):
                    s_gl.wait(v, n)
                    s_a.wait(v, n)
                    s_y.wait(v, n.back(2))
                    for c, k in enumerate(HCH):
                        at = slice(P * c, P * c + P)
                        v.scalar_tensor_tensor(out=act_[n.u][0:k, at], in0=ps_a[n.u][0:k, at], scalar=vec[0:k, 2 + c:3 + c],
                                               in1=gl[n.u][0:k, at], op0=ALU.add, op1=ALU.mult).then_inc(s_ac.sem, 1)

                def update(n):
                    s_y.wait(v, n)
                    if l:
                        s_up.wait(v, n.back(2))
                    dst = tok(y, n) if not l else yo[n.u][:, :]
                    v.tensor_tensor(dst, ps_y[n.u][:, 0:D], tok(y2, n), ALU.add).then_inc(s_yc.sem, 1)

                def update_x(n):
                    if l:
                        s_yc.wait(v, n)
                        v.scalar_tensor_tensor(out=tok(x, n), in0=yo[n.u][:, :], scalar=tg[:, 2:3], in1=tok(x, n),
                                               op0=ALU.mult, op1=ALU.add).then_inc(s_up.sem, 1)
                run_stages(v, [(6, gate), (3, lambda n: ln_norm(v, n, hn[n.u][:, :], s_t)), (9, update_x), (8, update), (2, stats)])

            @prog("gpsimd")
            def _(g):
                for t in h[::UPS]:
                    g.memset(t[0:1, 64:D], 0.0).then_inc(s_z.sem, 1)
                for t in act_:
                    g.memset(t[64:P, 2 * P:3 * P], 1.0).then_inc(s_z.sem, 1)
                run_stages(g, [(2, lambda n: ln_rstd(g, n))])
            if not l:
                prefetch(attention_weights(1))
            phase_end()

        def experts():
            psb, many, pbank = phase_begin("m")
            h, hT, st = many("h", 2, D), many("hT", 2, D), many("st", 2, 16)
            rt = many("rt", 2, 64)
            ri = many("ri", 2, E, U32)
            up_ = many("up", 2, CH * P)
            yw = many("yw", 2, E * D)
            ys = many("ys", 2, D)
            ps_h = [pbank(f"ps_h{i}") for i in range(CH // 4)]
            ps_y = pbank("ps_y", 2)
            ps_x, ps_r = pbank("ps_x"), pbank("ps_r")
            s_ln, ln_stats, ln_rstd, ln_norm = layernorm("ln", lambda n: tok(x, n), st, None)
            s_t, s_hc, s_r, s_p, s_y, s_up = (sig(i, 1) for i in ("t", "hc", "r", "p", "y", "up"))
            s_h, s_re, s_sq = (sig(i, CH // 4) for i in ("h", "re", "sq"))
            s_top = sig("top", 6)
            s_comb = sig("comb", 4)
            s_yw = sig("yw", 2)
            s_out = sig("out", 16)

            @prog("sync")
            def _(sp):
                def store(n):
                    s_up.wait(sp, n)
                    dst = out.rearrange("b s d -> (b s) d")[bass.ds(n.at(P), P), :]
                    sp.dma_start(dst, tok(x, n)).then_inc(s_out.sem, 16)
                run_stages(sp, [(7, store)])

            @prog("tensor")
            def _(pe):
                def transpose_h(n):
                    s_ln.wait(pe, n)
                    s_hc.wait(pe, n.back(1))
                    pe.transpose(ps_x[:, 0:P], h[n.u][:, :], ident).then_inc(s_t.sem, 1)

                def route(n):
                    s_hc.wait(pe, n)
                    s_p.wait(pe, n.back(1))
                    pe.matmul(ps_r[:, 0:E], hT[n.u][:, :], rw[:, :], start=True, stop=True).then_inc(s_r.sem, 1)

                def up(n):
                    for b in range(CH // 4):
                        s_re.wait(pe, n.back(1), b + 1)
                        for i in range(4):
                            c = 4 * b + i
                            m = pe.matmul(ps_h[b][:, P * i:P * i + P], w1[:, P * c:P * c + P], hT[n.u][:, :],
                                          start=True, stop=True)
                        m.then_inc(s_h.sem, 1)

                def down(n):
                    s_sq.wait(pe, n)
                    s_yw.wait(pe, n.back(1), 1)
                    c = 0
                    for e, w in enumerate(EW):
                        for i in range(w // P):
                            m = pe.matmul(ps_y[:, D * e:D * e + D], up_[n.u][:, P * c:P * c + P], w2[:, D * c:D * c + D],
                                          start=(i == 0), stop=(i == w // P - 1))
                            c += 1
                    m.then_inc(s_y.sem, 1)
                run_stages(pe, [(2, transpose_h), (3, route), (3, up), (4, down)])

            @prog("scalar")
            def _(act):
                def copy_h(n):
                    s_t.wait(act, n)
                    s_r.wait(act, n.back(2))
                    s_h.wait(act, n.back(2))
                    act.activation(hT[n.u][:, :], ps_x[:, 0:P], ACT.Copy).then_inc(s_hc.sem, 1)

                def probabilities(n):
                    s_r.wait(act, n)
                    s_top.wait(act, n.back(2))
                    act.activation(rt[n.u][:, 0:E], ps_r[:, 0:E], ACT.Sigmoid).then_inc(s_p.sem, 1)

                def relu(n):
                    for b in range(CH // 4):
                        s_h.wait(act, n, b + 1)
                        s_y.wait(act, n.back(2))
                        act.activation(up_[n.u][:, 512 * b:512 * b + 512], ps_h[b][:, :], ACT.Relu).then_inc(s_re.sem, 1)

                def square(n):
                    for b in range(CH // 4):
                        s_re.wait(act, n, b + 1)
                        r = up_[n.u][:, 512 * b:512 * b + 512]
                        act.activation(r, r, ACT.Square).then_inc(s_sq.sem, 1)
                run_stages(act, [(2, copy_h), (3, probabilities), (3, relu), (3, square)])

            @prog("vector")
            def _(v):
                def top2(first, last):
                    def stage(n):
                        t, ti = rt[n.u], ri[n.u]
                        steps = [
                            lambda: v.max(t[:, 8:16], t[:, 0:E]),
                            lambda: v.max_index(ti[:, :], t[:, 8:16], t[:, 0:E]),
                            lambda: v.tensor_copy(t[:, 16:18], ti[:, 0:2]),
                            lambda: v.tensor_tensor(t[:, 18:19], t[:, 8:9], t[:, 9:10], ALU.add),
                            lambda: v.tensor_scalar(t[:, 18:19], t[:, 18:19], 1e-20, None, ALU.add),
                            lambda: v.reciprocal(t[:, 19:20], t[:, 18:19]),
                        ]
                        for i in range(first, last):
                            if i:
                                s_top.wait(v, n, i)
                            else:
                                s_p.wait(v, n)
                                s_yw.wait(v, n.back(2), 1)
                            alone(v, "vector")
                            steps[i]().then_inc(s_top.sem, 1)
                    return stage

                def weigh(n):
                    s_comb.wait(v, n)
                    s_y.wait(v, n)
                    v.tensor_tensor(yw[n.u][:, :].rearrange("p (e d) -> p e d", d=D),
                                    ps_y[:, :].rearrange("p (e d) -> p e d", d=D),
                                    rt[n.u][:, 40:48].unsqueeze(2).broadcast_to([P, E, D]), ALU.mult)\
                        .then_inc(s_yw.sem, 1)

                def add_up(n):
                    s_yw.wait(v, n, 1)
                    v.reduce_sum(ys[n.u][:, :], yw[n.u][:, :].rearrange("p (e d) -> p d e", d=D), axis=AX_X)\
                        .then_inc(s_yw.sem, 1)

                def update(n):
                    s_yw.wait(v, n)
                    v.scalar_tensor_tensor(out=tok(x, n), in0=ys[n.u][:, :], scalar=tg[:, 3:4], in1=tok(x, n),
                                           op0=ALU.mult, op1=ALU.add).then_inc(s_up.sem, 1)
                run_stages(v, [(5, weigh), (3, top2(0, 1)), (0, lambda n: ln_stats(v, n)), (3, top2(1, 2)), (5, add_up),
                               (3, top2(2, 3)), (1, lambda n: ln_norm(v, n, h[n.u][:, :], s_t)), (3, top2(3, 4)),
                               (5, update), (3, top2(4, 6))])

            @prog("gpsimd")
            def _(g):
                def weights(n):
                    t = rt[n.u]
                    steps = [
                        lambda: g.tensor_scalar(t[:, 20:22], t[:, 8:10], t[:, 19:20], None, ALU.mult),
                        lambda: g.tensor_scalar(t[:, 24:32], iota, t[:, 16:17], t[:, 20:21], ALU.is_equal, ALU.mult),
                        lambda: g.tensor_scalar(t[:, 32:40], iota, t[:, 17:18], t[:, 21:22], ALU.is_equal, ALU.mult),
                        lambda: g.tensor_tensor(t[:, 40:48], t[:, 24:32], t[:, 32:40], ALU.add),
                    ]
                    s_top.wait(g, n)
                    for i, op in enumerate(steps):
                        if i:
                            s_comb.wait(g, n, i)
                        alone(g, "gpsimd")
                        op().then_inc(s_comb.sem, 1)
                run_stages(g, [(0, lambda n: ln_rstd(g, n)), (4, weights)])
            phase_end()

        cross_attention(0, attention_weights(0) + mlp_weights(0))
        for l in range(2):
            local_attention(l)
            mlp(l)
        w1, w2, rw = sb("w1", CH * P), sb("w2", CH * D), sb("rw", E)
        cross_attention(1, [(w1[:, :], a["L1_ffn_w1"]), (rw[:, :], a["router_wT"]),
                            (w2[:, :].rearrange("p (c d) -> p c d", d=D), a["L1_ffn_w2"].rearrange("(c p) d -> p c d", p=P))])
        experts()

        block = ctx.enter_context(nc.Block())
        starts = {"sync": block.sync, "scalar": block.scalar, "vector": block.vector, "gpsimd": block.gpsimd,
                  "tensor": block.tensor}
        for name, steps in progs.items():
            @starts[name]
            def _(eng, steps=steps):
                for f in steps:
                    f(eng)


_AS_IS = ["x", "mask_BxS2_if1", "mask_BxS2_ik0", "g_xattn", "g_ffn", "L0_ffn_wqkv", "L0_ffn_q_scale", "L0_ffn_k_scale",
          "L0_ffn_wo", "L0_ffn_ln_g", "L0_ffn_ln_b", "L0_ffn_w1", "L0_ffn_b1", "L0_ffn_w2", "L0_ffn_b2", "L1_xattn_bq",
          "L1_xattn_bk", "L1_xattn_bv", "L1_xattn_bfc", "L1_ffn_w1", "L1_ffn_w2"]
_TRANSPOSED = {"L0_xattn_WqT": "L0_xattn_Wq", "L0_xattn_WkT": "L0_xattn_Wk", "L0_xattn_WvT": "L0_xattn_Wv",
               "L0_xattn_WoT": "L0_xattn_Wo", "L1_xattn_WqT": "L1_xattn_Wq", "L1_xattn_WkT": "L1_xattn_Wk",
               "L1_xattn_WvT": "L1_xattn_Wv", "L1_xattn_WfcT": "L1_xattn_Wfc", "router_wT": "L1_ffn_router_w"}


def kernel(**inputs):
    import concourse.bacc as _bacc
    from concourse.bass_utils import run_bass_kernel_spmd as _run

    nc = _bacc.Bacc("TRN2", target_bir_lowering=False, num_devices=1)
    arrays = {n: np.ascontiguousarray(inputs[n]) for n in _AS_IS}
    arrays.update({n: np.ascontiguousarray(np.asarray(inputs[m]).T) for n, m in _TRANSPOSED.items()})
    arrays["ctxT"] = np.ascontiguousarray(np.asarray(inputs["ctx_1024"]).reshape(B * SC, D).T)
    arrays["mask0T"] = np.ascontiguousarray(np.asarray(inputs["mask_BxS2_if1"]).T)
    arrays["c32"], arrays["c16"] = constants()
    sent, args = {}, {}
    for name, v in arrays.items():
        key = f"in_{name}_dram"
        sent[key] = v
        args[name] = nc.dram_tensor(key, v.shape, mybir.dt.from_np(v.dtype), kind="ExternalInput").ap()
    out = nc.dram_tensor("out_0_dram", (B, S, D), F32, kind="ExternalOutput").ap()
    build(nc, args, out)
    r = _run(nc, [sent], core_ids=[0])
    return r.results[0]["out_0_dram"]
```
